# Optimizing a Trainium2 kernel written in Bass

```python
import numpy as np
import jax
import jax.numpy as jnp

def _softmax(x, axis=-1):
    return jax.nn.softmax(x, axis=axis)

def _gelu(x):
    return jax.nn.gelu(x, approximate=True)

def _silu(x):
    return jax.nn.silu(x)

def _sigmoid(x):
    return jax.nn.sigmoid(x)

def _layernorm(x, axis=-1, eps=1e-05):
    m = jnp.mean(x, axis=axis, keepdims=True)
    v = jnp.var(x, axis=axis, keepdims=True)
    return (x - m) / jnp.sqrt(v + eps)

def _scatter_add(tgt, idx, src, axis=0):
    return tgt.at[idx].add(src)

def _segment_sum(src, seg, n):
    return jax.ops.segment_sum(src, seg, n)
kernel_name = 'mk_gnn_preln_d4_gnn_r32_470e0b'

def setup_inputs(seed: int=0):
    np.random.seed(seed)
    _w = jnp.asarray

    def _rec_inputs():
        import jax
        import jax.numpy as jnp
        _gk = jax.random.key(seed)
        x = -0.000202 + 1 * jax.random.normal(jax.random.fold_in(_gk, 1), (3125, 128), jnp.float32)
        _s = jax.random.randint(jax.random.fold_in(_gk, 2), (25000,), 0, 3125, jnp.int32)
        _d = jax.random.randint(jax.random.fold_in(_gk, 3), (25000,), 0, 3125, jnp.int32)
        _loop = jnp.arange(3125, dtype=jnp.int32)
        src = jnp.concatenate([_s, _d, _loop])
        dst = jnp.concatenate([_d, _s, _loop])
        _o = jnp.argsort(dst, stable=True)
        src = src[_o]
        dst = dst[_o]
        edge_attr_2 = -0.000414295 + 0.999828 * jax.random.normal(jax.random.fold_in(_gk, 12), (53125, 2), jnp.float32)
        edge_weight = jax.random.uniform(jax.random.fold_in(_gk, 14), (53125,), jnp.float32, 0.0, 0.999998)
        return (x, src, dst, edge_attr_2, edge_weight)
    x, src, dst, edge_attr_2, edge_weight = _rec_inputs()

    def _L0_gnn_setup():
        import jax, jax.numpy as jnp
        import numpy as np
        N_NODES = 50000
        N_EDGES = 25000
        IN_DIM = 128
        OUT_DIM = 128
        EDGE_DIM = 2
        LN_EPS = 1e-05
        key = jax.random.key(seed)
        ks = jax.random.split(key, 8)
        s = lambda fan_in: 1.0 / np.sqrt(fan_in)
        x = jax.random.normal(ks[0], (N_NODES, IN_DIM), dtype=jnp.float32)
        edge_attr = jax.random.normal(ks[1], (N_EDGES, EDGE_DIM), dtype=jnp.float32)
        mW1 = jax.random.normal(ks[2], (2 * IN_DIM + EDGE_DIM, OUT_DIM), dtype=jnp.float32) * s(2 * IN_DIM + EDGE_DIM)
        mb1 = jnp.zeros((OUT_DIM,), jnp.float32)
        mW2 = jax.random.normal(ks[3], (OUT_DIM, OUT_DIM), dtype=jnp.float32) * s(OUT_DIM)
        mb2 = jnp.zeros((OUT_DIM,), jnp.float32)
        uW1 = jax.random.normal(ks[4], (IN_DIM + OUT_DIM, OUT_DIM), dtype=jnp.float32) * s(IN_DIM + OUT_DIM)
        ub1 = jnp.zeros((OUT_DIM,), jnp.float32)
        uW2 = jax.random.normal(ks[5], (OUT_DIM, OUT_DIM), dtype=jnp.float32) * s(OUT_DIM)
        ub2 = jnp.zeros((OUT_DIM,), jnp.float32)
        gamma = jnp.ones((OUT_DIM,), jnp.float32)
        beta = jnp.zeros((OUT_DIM,), jnp.float32)
        edge_index = jax.random.randint(ks[6], (2, N_EDGES), 0, N_NODES, dtype=jnp.int64 if jax.config.jax_enable_x64 else jnp.int32)
        return {'x': x, 'edge_attr': edge_attr, 'mW1': mW1, 'mb1': mb1, 'mW2': mW2, 'mb2': mb2, 'uW1': uW1, 'ub1': ub1, 'uW2': uW2, 'ub2': ub2, 'gamma': gamma, 'beta': beta, 'edge_index': edge_index}
    _L0_gnn_all = _L0_gnn_setup()
    _L0_gnn_in = {k: v for k, v in _L0_gnn_all.items() if k in ('mW1', 'mb1', 'mW2', 'mb2', 'uW1', 'ub1', 'uW2', 'ub2', 'gamma', 'beta')}
    del _L0_gnn_all

    def _L1_gnn_setup():
        import jax, jax.numpy as jnp
        import numpy as np
        N_NODES = 50000
        N_EDGES = 25000
        D_IN = 128
        D_OUT = 128
        key = jax.random.key(seed)
        k1, k2, k3, k4, k5 = jax.random.split(key, 5)
        shape_features = jax.random.normal(k1, (N_NODES, D_IN), dtype=jnp.float32)
        edge_src = jax.random.randint(k2, (N_EDGES,), 0, N_NODES, dtype=jnp.int64)
        edge_dst = jax.random.randint(k3, (N_EDGES,), 0, N_NODES, dtype=jnp.int64)
        limit = 0.1 * np.sqrt(6.0 / (D_IN + D_OUT))
        W1 = jax.random.uniform(k4, (D_IN, D_OUT), dtype=jnp.float32, minval=-limit, maxval=limit)
        W2 = jax.random.uniform(k5, (D_IN, D_OUT), dtype=jnp.float32, minval=-limit, maxval=limit)
        b1 = jnp.zeros((D_OUT,), dtype=jnp.float32)
        b2 = jnp.zeros((D_OUT,), dtype=jnp.float32)
        return {'shape_features': shape_features, 'edge_src': edge_src, 'edge_dst': edge_dst, 'W1': W1, 'b1': b1, 'W2': W2, 'b2': b2}
    _L1_gnn_all = _L1_gnn_setup()
    _L1_gnn_in = {k: v for k, v in _L1_gnn_all.items() if k in ('W1', 'b1', 'W2', 'b2')}
    del _L1_gnn_all

    def _L2_gnn_setup():
        import jax, jax.numpy as jnp
        import numpy as np
        N = 3125
        E = 18750
        D_IN = 128
        D_OUT = 128
        key = jax.random.key(seed)
        k1, k2, k3, k4 = jax.random.split(key, 4)
        x = jax.random.normal(k1, (N, D_IN), dtype=jnp.float32)
        edge_index = jax.random.randint(k2, (2, E), 0, N, dtype=jnp.int64)
        edge_weight = jax.random.uniform(k3, (E,), dtype=jnp.float32)
        W = jax.random.normal(k4, (D_IN, D_OUT), dtype=jnp.float32) / np.sqrt(D_IN)
        bias = jnp.zeros((D_OUT,), dtype=jnp.float32)
        return {'x': x, 'edge_index': edge_index, 'edge_weight': edge_weight, 'W': W, 'bias': bias}
    _L2_gnn_all = _L2_gnn_setup()
    _L2_gnn_in = {k: v for k, v in _L2_gnn_all.items() if k in ('W', 'bias')}
    del _L2_gnn_all

    def _L3_gnn_setup():
        import jax, jax.numpy as jnp
        import numpy as np
        N_NODES = 50000
        D_FEAT = 128
        N_EDGES = 18750
        ALPHA = 0.1

        def _appnp_k1(x, edge_index):
            n = x.shape[0]
            loops = jnp.arange(n, dtype=edge_index.dtype)
            src = jnp.concatenate([edge_index[0], loops])
            dst = jnp.concatenate([edge_index[1], loops])
            ones = jnp.ones(src.shape[0], dtype=x.dtype)
            deg = jax.ops.segment_sum(ones, dst, num_segments=n)
            dinv = jnp.where(deg > 0, jax.lax.rsqrt(deg), 0.0)
            norm = dinv[src] * dinv[dst]
            agg = jax.ops.segment_sum(x[src] * norm[:, None], dst, num_segments=n)
            return (1.0 - ALPHA) * agg + ALPHA * x
        key = jax.random.key(seed)
        k1, k2 = jax.random.split(key)
        x = jax.random.normal(k1, (N_NODES, D_FEAT), dtype=jnp.float32)
        edge_index = jax.random.randint(k2, (2, N_EDGES), 0, N_NODES, dtype=jnp.int64)
        return {'x': x, 'edge_index': edge_index}
    _L3_gnn_all = _L3_gnn_setup()
    _L3_gnn_in = {k: v for k, v in _L3_gnn_all.items() if k in ()}
    del _L3_gnn_all
    return {'x': x, 'src': src, 'dst': dst, 'edge_attr_2': edge_attr_2, 'edge_weight': edge_weight, 'L0_gnn_mW1': _L0_gnn_in['mW1'], 'L0_gnn_mb1': _L0_gnn_in['mb1'], 'L0_gnn_mW2': _L0_gnn_in['mW2'], 'L0_gnn_mb2': _L0_gnn_in['mb2'], 'L0_gnn_uW1': _L0_gnn_in['uW1'], 'L0_gnn_ub1': _L0_gnn_in['ub1'], 'L0_gnn_uW2': _L0_gnn_in['uW2'], 'L0_gnn_ub2': _L0_gnn_in['ub2'], 'L0_gnn_gamma': _L0_gnn_in['gamma'], 'L0_gnn_beta': _L0_gnn_in['beta'], 'L1_gnn_W1': _L1_gnn_in['W1'], 'L1_gnn_b1': _L1_gnn_in['b1'], 'L1_gnn_W2': _L1_gnn_in['W2'], 'L1_gnn_b2': _L1_gnn_in['b2'], 'L2_gnn_W': _L2_gnn_in['W'], 'L2_gnn_bias': _L2_gnn_in['bias']}

def reference(x, src, dst, edge_attr_2, edge_weight, L0_gnn_mW1, L0_gnn_mb1, L0_gnn_mW2, L0_gnn_mb2, L0_gnn_uW1, L0_gnn_ub1, L0_gnn_uW2, L0_gnn_ub2, L0_gnn_gamma, L0_gnn_beta, L1_gnn_W1, L1_gnn_b1, L1_gnn_W2, L1_gnn_b2, L2_gnn_W, L2_gnn_bias):
    import jax
    import jax.numpy as jnp

    def _L0_gnn_ref(x, edge_attr, mW1, mb1, mW2, mb2, uW1, ub1, uW2, ub2, gamma, beta, edge_index):
        import jax, jax.numpy as jnp
        import numpy as np
        N_NODES = 50000
        N_EDGES = 25000
        IN_DIM = 128
        OUT_DIM = 128
        EDGE_DIM = 2
        LN_EPS = 1e-05
        num_nodes = x.shape[0]
        src, dst = (edge_index[0], edge_index[1])
        msg_in = jnp.concatenate([x[src], x[dst], edge_attr], axis=-1)
        msgs = jnp.maximum(msg_in @ mW1 + mb1, 0.0) @ mW2 + mb2
        agg = jax.ops.segment_sum(msgs, dst, num_segments=num_nodes)
        cnt = jax.ops.segment_sum(jnp.ones((dst.shape[0],), x.dtype), dst, num_segments=num_nodes)
        agg = agg / jnp.clip(cnt, 1.0)[:, None]
        upd_in = jnp.concatenate([x, agg], axis=-1)
        upd = jnp.maximum(upd_in @ uW1 + ub1, 0.0) @ uW2 + ub2
        upd = upd + x
        mu = jnp.mean(upd, axis=-1, keepdims=True)
        var = jnp.mean(jnp.square(upd - mu), axis=-1, keepdims=True)
        return (upd - mu) * jax.lax.rsqrt(var + LN_EPS) * gamma + beta

    def _L1_gnn_ref(shape_features, edge_src, edge_dst, W1, b1, W2, b2):
        import jax, jax.numpy as jnp
        import numpy as np
        N_NODES = 50000
        N_EDGES = 25000
        D_IN = 128
        D_OUT = 128
        gathered = shape_features[edge_src]
        aggr = jax.ops.segment_sum(gathered, edge_dst, num_segments=shape_features.shape[0])
        out = shape_features @ W1 + b1 + (aggr @ W2 + b2)
        return out

    def _L2_gnn_ref(x, edge_index, edge_weight, W, bias):
        import jax, jax.numpy as jnp
        import numpy as np
        N = 3125
        E = 18750
        D_IN = 128
        D_OUT = 128
        n = x.shape[0]
        loop = jnp.arange(n, dtype=edge_index.dtype)
        row = jnp.concatenate([edge_index[0], loop])
        col = jnp.concatenate([edge_index[1], loop])
        ew = jnp.concatenate([edge_weight, jnp.ones((n,), dtype=x.dtype)])
        deg = jax.ops.segment_sum(ew, col, num_segments=n)
        dinv = jnp.where(deg > 0, jax.lax.rsqrt(deg), 0.0)
        norm = dinv[row] * ew * dinv[col]
        xw = x @ W
        msgs = norm[:, None] * xw[row]
        out = jax.ops.segment_sum(msgs, col, num_segments=n)
        return out + bias

    def _L3_gnn_ref(x, edge_index):
        import jax, jax.numpy as jnp
        import numpy as np
        N_NODES = 50000
        D_FEAT = 128
        N_EDGES = 18750
        ALPHA = 0.1

        def _appnp_k1(x, edge_index):
            n = x.shape[0]
            loops = jnp.arange(n, dtype=edge_index.dtype)
            src = jnp.concatenate([edge_index[0], loops])
            dst = jnp.concatenate([edge_index[1], loops])
            ones = jnp.ones(src.shape[0], dtype=x.dtype)
            deg = jax.ops.segment_sum(ones, dst, num_segments=n)
            dinv = jnp.where(deg > 0, jax.lax.rsqrt(deg), 0.0)
            norm = dinv[src] * dinv[dst]
            agg = jax.ops.segment_sum(x[src] * norm[:, None], dst, num_segments=n)
            return (1.0 - ALPHA) * agg + ALPHA * x
        h = _appnp_k1(x, edge_index)
        return x + jax.nn.relu(h)
    edge_index = jnp.stack([src, dst])
    h = jnp.maximum(_layernorm(x, axis=-1), 0.0)
    x = x + _L0_gnn_ref(h, edge_attr_2, L0_gnn_mW1, L0_gnn_mb1, L0_gnn_mW2, L0_gnn_mb2, L0_gnn_uW1, L0_gnn_ub1, L0_gnn_uW2, L0_gnn_ub2, L0_gnn_gamma, L0_gnn_beta, edge_index)
    h = jnp.maximum(_layernorm(x, axis=-1), 0.0)
    x = x + _L1_gnn_ref(h, src, dst, L1_gnn_W1, L1_gnn_b1, L1_gnn_W2, L1_gnn_b2)
    h = jnp.maximum(_layernorm(x, axis=-1), 0.0)
    x = x + _L2_gnn_ref(h, edge_index, edge_weight, L2_gnn_W, L2_gnn_bias)
    h = jnp.maximum(_layernorm(x, axis=-1), 0.0)
    x = x + _L3_gnn_ref(h, edge_index)
    return x

_drawn_inputs = setup_inputs


def setup_inputs(seed=0):
    import zlib

    import numpy as np

    out = dict(_drawn_inputs(seed))
    spreads = {'L0_gnn_mb1': (0.0, 0.425),
     'L0_gnn_mb2': (0.0, 0.1),
     'L0_gnn_ub1': (0.0, 0.1),
     'L0_gnn_ub2': (0.0, 0.1),
     'L0_gnn_gamma': (1.0, 0.2),
     'L0_gnn_beta': (0.0, 0.1),
     'L1_gnn_b1': (0.0, 0.1),
     'L1_gnn_b2': (0.0, 0.1),
     'L2_gnn_bias': (0.0, 0.1)}
    factors = {'edge_attr_2': 8.0}
    for name, (base, spread) in spreads.items():
        noise = np.random.default_rng([zlib.crc32(name.encode()), seed]).standard_normal(out[name].shape)
        drawn = base * np.exp(spread * noise) if base else spread * noise
        out[name] = jnp.asarray(drawn.astype(out[name].dtype))
    for name, factor in factors.items():
        out[name] = (out[name] * factor).astype(out[name].dtype)
    return out
```

```python
import concourse.bass as bass
from concourse import mybir
from contextlib import ExitStack



def gnn_kernel(nc, x_in, src_in, dst_in, ea_in, ew_in, mW1, mb1, mW2, mb2, uW1, ub1, uW2, ub2,
               gamma, beta, W1, b1, W2, b2, W3, b3, out):
    fp32, bf16 = mybir.dt.float32, mybir.dt.bfloat16
    i32, u32 = mybir.dt.int32, mybir.dt.uint32
    ALU = mybir.AluOpType
    ACT = mybir.ActivationFunctionType
    AX = mybir.AxisListType

    N, D = x_in.shape
    E = src_in.shape[0]
    EPS = 1e-5
    TINY = 2.0 ** -116
    NT = -(-N // 128)
    NP = NT * 128
    NR = N - (NT - 1) * 128
    QE = 512
    NQ = -(-E // QE)
    ITER = 4
    NI = NQ // ITER
    assert NI * ITER == NQ
    QR = E - (NQ - 1) * QE
    QA = NQ // 32 * 32
    WB = 64
    NB = -(-N // WB)
    PAD_DST = NB * WB - 1
    assert N <= PAD_DST < NP
    MAXP = (NB - 1) // 2 + 1
    PARTS = 3
    NC = -(-NT // 4)
    TILES = [list(range(4 * j, min(4 * j + 4, NT))) for j in range(NC)]
    HALVES = [list(range(2 * m, min(2 * m + 2, NT))) for m in range(-(-NT // 2))]
    ACC_BANKS = -(-NB * WB // 512)
    DEG = 512 * (ACC_BANKS - 1) + 128
    assert NB * WB <= DEG and DEG + 4 * NB <= 512 * ACC_BANKS and ACC_BANKS < 8
    PRE = 7 * 512

    P_tab = nc.dram_tensor("p_parts", [NP, PARTS * D], bf16).ap()
    Q_tab = nc.dram_tensor("q_parts", [NP, PARTS * D], bf16).ap()
    H1_tab = nc.dram_tensor("h1_parts", [NP, PARTS * D], bf16).ap()
    G2_tab = nc.dram_tensor("g2_rows", [NP, D], fp32).ap()
    G3_tab = nc.dram_tensor("g3_parts", [NP, PARTS * D], bf16).ap()
    dst_row = nc.dram_tensor("dst_row", [NQ, QE], fp32).ap()
    ea_rows = nc.dram_tensor("ea_rows", [18, NQ * QE], bf16).ap()
    blk_tab = nc.dram_tensor("blk_tab", [NQ, 2], i32).ap()
    wc_tab = nc.dram_tensor("wc_parts", [2, PARTS, D], bf16).ap()

    ctx = ExitStack()
    with ctx:
        def sb(name, shape, dt=fp32):
            return ctx.enter_context(nc.sbuf_tensor(name, shape, dt))

        def sem(name):
            return ctx.enter_context(nc.semaphore(name))

        x = sb("x", [128, NT, D])
        h = sb("h", [128, NT, D])
        hT = sb("hT", [128, NP])
        ST = sb("ST", [128, NP])
        aggT = sb("aggT", [128, NP])
        g3 = aggT[:, :].rearrange("p (t d) -> p t d", d=D)
        r_bc = sb("r_bc", [128, NP], bf16)
        bn = sb("bn", [128, NT, 6])
        mv = sb("mv", [128, NT, 2])
        sd = sb("sd", [128, NT])
        rs = sb("rs", [128, NT])
        nb = sb("nb", [128, NT])
        rs2 = sb("rs2", [128, NT])
        nb2 = sb("nb2", [128, NT])
        pq = sb("pq", [128, 2, 2, 2, D])
        parts = sb("parts", [128, 2, 4, 2, PARTS, D], bf16)
        rest = sb("rest", [128, 2, 4 * D])
        degs = sb("degs", [128, 1 + NB, 4])
        deg2 = sb("deg2", [128, 2, 2 * NT + 1])
        cnt = sb("cnt", [128, 2, NT])
        dv = sb("dv", [128, 8, NT])
        INV_CNT, HAS, DINV2, DINV3, D09, SELF3, T0_, T1_ = range(8)
        ident = sb("ident", [128, 128])
        shift = sb("shift", [128, 256])
        identb = sb("identb", [128, 128], bf16)
        iota = sb("iota", [128, 128])
        iota_w = sb("iota_w", [128, 128])
        pio = sb("pio", [128, 1])
        pio_w = sb("pio_w", [128, 1])
        eps = sb("eps", [128, 1])
        zerob = sb("zerob", [128, 512], bf16)
        wab = sb("wab", [128, 2, D])
        w_m2 = sb("w_m2", [128, D])
        w_u1 = sb("w_u1", [128, 2, D])
        w_u2 = sb("w_u2", [128, D])
        w_11 = sb("w_11", [128, D])
        w_12 = sb("w_12", [128, D])
        w_3 = sb("w_3", [128, D])
        wcf = sb("wcf", [2, D])
        wcp = sb("wcp", [2, PARTS, D], bf16)
        wcr = sb("wcr", [2, D])
        wc18 = sb("wc18", [18, D], bf16)
        cols = sb("cols", [128, 2])
        bc = sb("bc", [128, 8, D])
        B_P, B_Q, B_U2, B_GA, B_BE, B_L1, B_L1B, B_L2 = range(8)
        idx = sb("idx", [128, NQ, 4], u32)
        idx_q = sb("idx_q", [128, ITER, 4], u32)
        dstT = sb("dstT", [128, NQ, 4])
        wT = sb("wT", [128, NQ, 4])
        wq = sb("wq", [128, NQ, 4, 4], bf16)
        wr = sb("wr", [128, 2, NQ, 4])
        blk = sb("blk", [128, 2])
        blk_i = sb("blk_i", [128, 2], i32)
        blk_s = sb("blk_s", [128, 2], i32)
        base64 = sb("base64", [128, 1])
        row_i = sb("row_i", [1, NQ, 2], i32)
        row_f = sb("row_f", [1, NQ, 2])
        far = sb("far", [1, NQ])
        far1 = sb("far1", [1, 1])
        far_i = sb("far_i", [1, 1], i32)
        far_s = sb("far_s", [1, 1], i32)
        passes_i = sb("passes_i", [1, 1], i32)
        tab_f = sb("tab_f", [1, NQ])
        tab_i = sb("tab_i", [1, NQ], i32)
        Qw = sb("Qw", [128, NB, PARTS * D], bf16)
        G = sb("G", [128, ITER, 4, PARTS * D], bf16)
        row_bc = sb("row_bc", [128, ITER, QE])
        ea18 = sb("ea18", [18, ITER, QE], bf16)
        sT = sb("sT", [128, ITER, QE], bf16)
        oh = sb("oh", [128, ITER, 4, 128], bf16)
        R = sb("R", [128, 2, 4, D])
        R_left = sb("R_left", [128, 2, 4, D])
        RP = sb("RP", [128, 2, PARTS, 4, D], bf16)
        dst_l = hT[0:NQ, 0:QE].bitcast(i32)
        src_l = hT[0:NQ, QE:2 * QE].bitcast(i32)
        w_l = hT[0:NQ, 2 * QE:3 * QE]
        dst_f = ST[0:NQ, 0:QE]
        src_f = ST[0:NQ, QE:2 * QE]
        ea_l = ST[0:NQ, 2 * QE:4 * QE]
        dst_r = ST[0:NQ, 4 * QE:5 * QE]
        ea_r = aggT[0:NQ, 0:2 * QE].rearrange("p (i e) -> p i e", i=2)
        ea_m = aggT[0:NQ, 2 * QE:5 * QE].bitcast(bf16).rearrange("p (i a e) -> p i a e", i=2, a=PARTS)

        ps = ctx.enter_context(nc.psum_tensor("ps", [128, 8 * 512], fp32))

        def bank(j, n=512):
            return ps[:, 512 * j:512 * j + n]

        s_con = sem("constants_made")
        s_pad = sem("padding_made")
        s_dst = sem("dst_loaded")
        s_src = sem("src_loaded")
        s_ea = sem("ea_loaded")
        s_x = sem("x_loaded")
        s_wt = sem("weights_loaded")
        s_wc = sem("wc_stored")
        s_wc18 = sem("wc18_loaded")
        s_blk = sem("blocks_stored")
        s_row = sem("blocks_loaded")
        s_dr = sem("dst_row_stored")
        s_eas = sem("ea_rows_stored")
        s_pass = sem("passes_known")
        s_prep = sem("edge_prep")
        s_prepT = sem("edge_transposes")
        s_prepE = sem("edge_transposes_read")
        s_wcp = sem("wc_parts")
        s_eap = sem("ea_parts")
        s_dve = sem("dve_chain")
        s_act = sem("act_chain")
        s_pool = sem("pool_chain")
        LN = range(5)
        s_var = [sem(f"ln{n}_variance") for n in LN]
        s_root = [sem(f"ln{n}_root") for n in LN]
        s_norm = [sem(f"ln{n}_scale") for n in LN]
        s_rows = [sem(f"ln{n}_rows") for n in LN]
        STAGES = ["T0", "PQ", "DG", "B", "R", "A", "U", "V", "T1", "O1", "T2", "O2", "O3"]
        mm = {n: sem(f"{n}_done") for n in STAGES}
        ev = {n: sem(f"{n}_read") for n in STAGES}
        s_hi = sem("parts_hi")
        s_re = sem("parts_rest")
        s_mi = sem("parts_mid")
        s_lo = sem("parts_lo")
        s_st = [sem(f"parts_stored_{k}") for k in range(2)]
        s_g2 = sem("g2_stored")
        s_qw = sem("q_windows_loaded")
        s_zero = sem("acc_zeroed")
        s_acc = sem("acc_read")
        s_fin = sem("out_rows")
        s_out = sem("out_stored")
        s_degs = sem("degrees_known")
        s_bias = sem("x_with_bias")
        s_tab = sem("pass_tables")
        s_oh = sem("onehot_ready")
        s_seg = sem("quad_summed")
        s_ix = sem("indices_ready")
        s_turn = sem("quads_to_gather")
        s_gat = [sem(f"gathered_{k}") for k in range(ITER)]
        s_rl = [sem(f"edge_rows_loaded_{k}") for k in range(ITER)]
        s_sT = sem("window_rows_ready")
        s_pre = sem("messages_in_psum")
        s_R = sem("rows_to_split")
        s_rhi = sem("row_hi")
        s_rre = sem("row_rest")
        s_rmi = sem("row_mid")
        s_rlo = sem("row_lo")
        block = ctx.enter_context(nc.Block())

        L0, L1, L2, L3 = range(4)

        def step_count(s, w, i, P):
            return (P * s + w) * NI + i

        def pipeline(*stages):
            for step in range(NC + len(stages) - 1):
                for lag, stage in enumerate(stages):
                    if 0 <= step - lag < NC:
                        stage(step - lag)

        NH = len(HALVES)
        SPLIT0 = {"PQ": 0, "H1": NH, "G3": NH + NC}

        def stored(n):
            before = [m for m in range(n + 1) if m % 2 == n % 2]
            return s_st[n % 2], sum(32 if m < NH else 16 for m in before)

        @block.sync
        def _(sp):
            sp.dma_start(dst_l[0:QA, :], dst_in[0:QA * QE].rearrange("(p e) -> p e", e=QE)).then_inc(s_dst, 16)
            sp.dma_start(x[:, 0:NT - 1, :], x_in[0:128 * (NT - 1), :].rearrange("(t p) d -> p t d", p=128))\
                .then_inc(s_x, 16)
            sp.wait_ge(s_pad, 5)
            sp.dma_start(x[0:NR, NT - 1, :], x_in[128 * (NT - 1):N, :]).then_inc(s_x, 16)
            for tile, array, width, arrived in ((dst_l, dst_in, QE, s_dst), (src_l, src_in, QE, s_src),
                                                (w_l, ew_in, QE, s_src),
                                                (ea_l, ea_in.rearrange("e i -> (e i)"), 2 * QE, s_ea)):
                if array is not dst_in:
                    sp.dma_start(tile[0:QA, :], array[0:QA * width].rearrange("(p e) -> p e", e=width))\
                        .then_inc(arrived, 16)
                sp.dma_start(tile[QA:NQ - 1, :],
                             array[QA * width:(NQ - 1) * width].rearrange("(p e) -> p e", e=width))\
                    .then_inc(arrived, 16)
                rest_of = QR * (width // QE)
                sp.dma_start(tile[NQ - 1:NQ, 0:rest_of],
                             array[(NQ - 1) * width:(NQ - 1) * width + rest_of].rearrange("(a e) -> a e", a=1))\
                    .then_inc(arrived, 16)
            sp.wait_ge(s_prep, 1)
            sp.dma_start(blk_tab, blk_s[0:NQ, :]).then_inc(s_blk, 16)
            sp.wait_ge(s_blk, 16)
            sp.dma_start(row_i[:, :, :], blk_tab.rearrange("q (a b) -> a q b", a=1)).then_inc(s_row, 16)
            sp.wait_ge(s_prep, 2)
            sp.dma_start(dst_row, dst_r).then_inc(s_dr, 16)
            sp.wait_ge(s_eap, 5)
            for b in range(PARTS):
                sp.dma_start(ea_rows[6 * b:6 * b + 6, :].rearrange("r (p e) -> p r e", e=QE),
                             ea_m.rearrange("p i a e -> p (i a) e")).then_inc(s_eas, 16)
            sp.wait_ge(s_wcp, 5)
            sp.dma_start(wc_tab, wcp[:, :, :]).then_inc(s_wc, 16)
            sp.wait_ge(s_wc, 16)
            for b in range(PARTS):
                for i in range(2):
                    sp.dma_start(wc18[6 * b + 3 * i:6 * b + 3 * i + 3, :],
                                 wc_tab[i, b:b + 1, :].to_broadcast([3, D])).then_inc(s_wc18, 16)
            for m, tiles in enumerate(HALVES):
                sp.wait_ge(s_lo, m + 1)
                t0, n = tiles[0], len(tiles)
                for which, table in enumerate((P_tab, Q_tab)):
                    sp.dma_start(table[128 * t0:128 * (t0 + n), :].rearrange("(t p) c -> p t c", p=128),
                                 parts[:, m % 2, 0:n, which, :, :].rearrange("p t a d -> p t (a d)"))\
                        .then_inc(s_st[m % 2], 16)
            for m in (NH - 2, NH - 1):
                which, value = stored(m)
                sp.wait_ge(which, value)
            for half in range(2):
                sp.dma_start(Qw[WB * half:WB * half + WB, :, :],
                             Q_tab[WB * half:WB * (half + NB), :].rearrange("(b p) c -> p b c", p=WB))\
                    .then_inc(s_qw, 16)
            sp.wait_ge(s_pass, 1)
            P = sp.value_load(passes_i[0:1, 0:1], min_val=1, max_val=MAXP)
            sp.wait_ge(s_dr, 16)
            sp.wait_ge(s_eas, 16 * PARTS)
            with sp.Fori(0, P) as w:
                with sp.Fori(0, NI) as i:
                    for k in range(ITER):
                        sp.wait_ge(s_pre, (w * NI + i) * ITER + k + 1)
                        q = i * ITER + k
                        sp.dma_start(row_bc[:, k, :], dst_row[bass.ds(q, 1), :].to_broadcast([128, QE]))\
                            .then_inc(s_rl[k], 16)
                        sp.dma_start(ea18[:, k, :], ea_rows[:, bass.ds(q * QE, QE)]).then_inc(s_rl[k], 16)
            for name, table in (("H1", H1_tab), ("G2", G2_tab), ("G3", G3_tab)):
                for j, tiles in enumerate(TILES):
                    t0, n = tiles[0], len(tiles)
                    rows = slice(128 * t0, 128 * (t0 + n))
                    if name == "G2":
                        sp.wait_ge(s_rows[3], j + 1)
                        sp.dma_start(table[rows, :].rearrange("(t p) c -> p t c", p=128), h[:, t0:t0 + n, :])\
                            .then_inc(s_g2, 16)
                    else:
                        m = SPLIT0[name] + j
                        sp.wait_ge(s_lo, m + 1)
                        sp.dma_start(table[rows, :].rearrange("(t p) c -> p t c", p=128),
                                     parts[:, m % 2, 0:n, 0, :, :].rearrange("p t a d -> p t (a d)"))\
                            .then_inc(s_st[m % 2], 16)
            for j, tiles in enumerate(TILES):
                sp.wait_ge(s_fin, j + 1)
                t0, full = tiles[0], [t for t in tiles if 128 * (t + 1) <= N]
                if full:
                    sp.dma_start(out[128 * t0:128 * (t0 + len(full)), :].rearrange("(t p) d -> p t d", p=128),
                                 h[:, t0:t0 + len(full), :]).then_inc(s_out, 16)
                if len(full) < len(tiles):
                    sp.dma_start(out[128 * (NT - 1):N, :], h[0:NR, NT - 1, :]).then_inc(s_out, 16)
            sp.wait_ge(s_out, 16 * NC)

        @block.gpsimd
        def _(pool):
            links = [0]

            def link(ins):
                links[0] += 1
                ins.then_inc(s_pool, 1)
                pool.wait_ge(s_pool, links[0])

            pool.memset(zerob[:, :], 0.0).then_inc(s_con, 1)
            pool.memset(eps[:, :], EPS).then_inc(s_con, 1)
            pool.iota(iota[:, :], pattern=[[1, 128]], base=0, channel_multiplier=0,
                      allow_small_or_imprecise_dtypes=True).then_inc(s_con, 1)
            pool.iota(pio[:, :], pattern=[[0, 1]], base=0, channel_multiplier=1,
                      allow_small_or_imprecise_dtypes=True).then_inc(s_con, 1)
            link(pool.memset(shift[:, :], 0.0))
            link(pool.affine_select(out=shift[:, :], in_=shift[:, :], compare_op=ALU.not_equal, fill=1.0, base=WB,
                                    pattern=[[-1, 256]], channel_multiplier=1))
            pool.tensor_copy(ident[:, :], shift[:, WB:WB + 128]).then_inc(s_con, 1)
            pool.tensor_copy(identb[:, :], shift[:, WB:WB + 128]).then_inc(s_con, 1)
            pool.memset(bc[:, B_P, :], 0.0).then_inc(s_con, 1)
            pool.memset(degs[:, 0, :], 0.0).then_inc(s_con, 1)
            pool.memset(wq[:, :, :, 0], 1.0).then_inc(s_con, 1)

            pool.wait_ge(s_ea, 48)
            ea_v = ea_l.rearrange("p (e i) -> p i e", i=2)
            pool.tensor_copy(ea_m[:, :, 0, :], ea_v).then_inc(s_eap, 1)
            pool.wait_ge(s_eap, 1)
            pool.tensor_tensor(ea_r, ea_v, ea_m[:, :, 0, :], ALU.subtract).then_inc(s_eap, 1)
            pool.wait_ge(s_eap, 2)
            pool.tensor_copy(ea_m[:, :, 1, :], ea_r).then_inc(s_eap, 1)
            pool.wait_ge(s_eap, 3)
            pool.tensor_tensor(ea_r, ea_r, ea_m[:, :, 1, :], ALU.subtract).then_inc(s_eap, 1)
            pool.wait_ge(s_eap, 4)
            pool.tensor_copy(ea_m[:, :, 2, :], ea_r).then_inc(s_eap, 1)

            def split_rest(m, source, width, form):
                pool.wait_ge(s_hi, m + 1)
                pool.tensor_tensor(rest[:, m % 2, 0:width].rearrange(form, d=D, **({"w": 2} if "w" in form else {})),
                                   source, part(m, 0), ALU.subtract).then_inc(s_re, 1)

            def part(m, a):
                if m < NH:
                    return parts[:, m % 2, 0:len(HALVES[m]), :, a, :]
                return parts[:, m % 2, 0:len(TILES[(m - NH) % NC]), 0, a, :]

            def split_lo(m, width, form):
                pool.wait_ge(s_mi, m + 1)
                pool.tensor_tensor(part(m, 2),
                                   rest[:, m % 2, 0:width].rearrange(form, d=D, **({"w": 2} if "w" in form else {})),
                                   part(m, 1), ALU.subtract).then_inc(s_lo, 1)

            for m, tiles in enumerate(HALVES):
                n = len(tiles)
                split_rest(m, pq[:, m % 2, 0:n, :, :], 2 * D * n, "p (t w d) -> p t w d")
                split_lo(m, 2 * D * n, "p (t w d) -> p t w d")

            pool.wait_ge(s_pass, 1)
            P = pool.value_load(passes_i[0:1, 0:1], min_val=1, max_val=MAXP)
            pool.wait_ge(s_prepE, 3)

            def sweep(s, table, rows):
                with pool.Fori(0, P) as w:
                    with pool.Fori(0, NI) as i:
                        quads = step_count(s, w, i, P) * ITER
                        for k in range(ITER):
                            pool.wait_ge(s_seg, quads + k + 1)
                            pool.tensor_copy(idx_q[:, k, :],
                                             idx[:, bass.ds(i * ITER + k, 1), :].rearrange("p a c -> p (a c)"))\
                                .then_inc(s_ix, 1)
                            pool.wait_ge(s_ix, quads + k + 1)
                            pool.sem_inc(s_turn, 1)
                            for c in range(4):
                                pool.indirect_dma_start(
                                    rows(k, c), None, table,
                                    bass.IndirectOffsetOnAxis(ap=idx_q[:, k, c:c + 1], axis=0))\
                                    .then_inc(s_gat[k], 16)

            def rows3(k, c):
                return G[:, k, c, :]

            def rows_f(k, c):
                return G[:, k, c, 0:2 * D].bitcast(fp32)

            for m in (NH - 2, NH - 1):
                which, value = stored(m)
                pool.wait_ge(which, value)
            sweep(L0, P_tab, rows3)
            for j, tiles in enumerate(TILES):
                t0, n = tiles[0], len(tiles)
                split_rest(SPLIT0["H1"] + j, h[:, t0:t0 + n, :], D * n, "p (t d) -> p t d")
                split_lo(SPLIT0["H1"] + j, D * n, "p (t d) -> p t d")
            for m in (SPLIT0["H1"] + NC - 2, SPLIT0["H1"] + NC - 1):
                which, value = stored(m)
                pool.wait_ge(which, value)
            sweep(L1, H1_tab, rows3)
            pool.wait_ge(s_g2, 16 * NC)
            sweep(L2, G2_tab, rows_f)
            for j, tiles in enumerate(TILES):
                t0, n = tiles[0], len(tiles)
                split_rest(SPLIT0["G3"] + j, g3[:, t0:t0 + n, :], D * n, "p (t d) -> p t d")
                split_lo(SPLIT0["G3"] + j, D * n, "p (t d) -> p t d")
            for m in (SPLIT0["G3"] + NC - 2, SPLIT0["G3"] + NC - 1):
                which, value = stored(m)
                pool.wait_ge(which, value)
            sweep(L3, G3_tab, rows3)

        @block.scalar
        def _(act):
            links = [0]

            def link(ins):
                links[0] += 1
                ins.then_inc(s_act, 1)
                act.wait_ge(s_act, links[0])

            loads = [(wab[:, 0, :], mW1[0:D, :]), (wab[:, 1, :], mW1[D:2 * D, :]), (wcf[:, :], mW1[2 * D:2 * D + 2, :]),
                     (w_m2[:, :], mW2), (w_u1[:, 0, :], uW1[0:D, :]), (w_u1[:, 1, :], uW1[D:2 * D, :]),
                     (w_u2[:, :], uW2), (w_11[:, :], W1), (w_12[:, :], W2), (w_3[:, :], W3),
                     (cols[:, 0:1], mb2.rearrange("(p a) -> p a", a=1)),
                     (cols[:, 1:2], ub1.rearrange("(p a) -> p a", a=1))]
            for slot, v in ((B_Q, mb1), (B_U2, ub2), (B_GA, gamma), (B_BE, beta), (B_L1, b1), (B_L1B, b2), (B_L2, b3)):
                loads.append((bc[:, slot, :], v.rearrange("(a d) -> a d", a=1).to_broadcast([128, D])))
            assert len(loads) == 19
            for to, of in loads:
                act.dma_start(to, of).then_inc(s_wt, 16)

            act.wait_ge(s_con, 9)

            def root(n):
                def stage(j):
                    act.wait_ge(s_var[n], j + 1)
                    ts = slice(TILES[j][0], TILES[j][-1] + 1)
                    act.activation(sd[:, ts], mv[:, ts, 1], ACT.Sqrt, bias=eps[:, 0:1]).then_inc(s_root[n], 1)
                return stage

            def rows(n, to, func, source, scaled=None):
                def stage(j):
                    act.wait_ge(s_norm[n], j + 1)
                    for t in TILES[j]:
                        last = act.activation(to[:, t, :], source[:, t, :], func, scale=rs[:, t:t + 1],
                                              bias=nb[:, t:t + 1])
                        if scaled is not None:
                            last = act.activation(scaled[:, t, :], source[:, t, :], func, scale=rs2[:, t:t + 1],
                                                  bias=nb2[:, t:t + 1])
                    last.then_inc(s_rows[n], 1)
                return stage

            def part(m, a):
                if m < NH:
                    return parts[:, m % 2, 0:len(HALVES[m]), :, a, :]
                return parts[:, m % 2, 0:len(TILES[(m - NH) % NC]), 0, a, :]

            def split_hi(m, source):
                if m >= 2:
                    which, value = stored(m - 2)
                    act.wait_ge(which, value)
                act.activation(part(m, 0), source, ACT.Copy).then_inc(s_hi, 1)

            def split_mid(m, width, form):
                act.wait_ge(s_re, m + 1)
                act.activation(part(m, 1),
                               rest[:, m % 2, 0:width].rearrange(form, d=D, **({"w": 2} if "w" in form else {})),
                               ACT.Copy).then_inc(s_mi, 1)

            def split_rows(name, source, n):
                def stage(j):
                    t0, c = TILES[j][0], len(TILES[j])
                    act.wait_ge(s_rows[n], j + 1)
                    split_hi(SPLIT0[name] + j, source[:, t0:t0 + c, :])
                    split_mid(SPLIT0[name] + j, D * c, "p (t d) -> p t d")
                return stage

            act.wait_ge(s_x, 32)
            pipeline(root(0), rows(0, h, ACT.Relu, x))
            act.wait_ge(s_wt, 16 * 19)
            act.activation(wcp[:, 0, :], wcf[:, :], ACT.Copy).then_inc(s_wcp, 1)
            act.wait_ge(s_wcp, 2)
            act.activation(wcp[:, 1, :], wcr[:, :], ACT.Copy).then_inc(s_wcp, 1)
            act.wait_ge(s_wcp, 4)
            act.activation(wcp[:, 2, :], wcr[:, :], ACT.Copy).then_inc(s_wcp, 1)
            act.wait_ge(s_prepT, 3)
            for j in range(NC):
                act.wait_ge(mm["T0"], j + 1)
                c = 128 * len(TILES[j])
                act.activation(hT[:, 512 * j:512 * j + c], bank(j, c), ACT.Copy).then_inc(ev["T0"], 1)
            for m, tiles in enumerate(HALVES):
                act.wait_ge(ev["PQ"], m + 1)
                n = len(tiles)
                split_hi(m, pq[:, m % 2, 0:n, :, :])
                split_mid(m, 2 * D * n, "p (t w d) -> p t w d")

            act.wait_ge(s_pass, 1)
            P = act.value_load(passes_i[0:1, 0:1], min_val=1, max_val=MAXP)

            def split_hi_mid(s):
                with act.Fori(0, P) as w:
                    with act.Fori(0, NI) as i:
                        u0 = step_count(s // 2, w, i, P) * ITER
                        n0 = step_count(s, w, i, P) * ITER

                        def first(k):
                            if s == L0:
                                act.wait_ge(s_pre, u0 + k + 1 + ITER)
                                act.wait_ge(s_rre, u0 + k + 1)
                                act.activation(R[:, k % 2, :, :],
                                               bank(7).rearrange("p (c d) -> p c d", d=D), ACT.Relu).then_inc(s_R, 1)
                            act.wait_ge(s_R, u0 + k + 2)
                            act.wait_ge(s_seg, n0 + k + ITER - 1)
                            act.activation(RP[:, k % 2, 0, :, :], R[:, k % 2, :, :], ACT.Copy).then_inc(s_rhi, 1)

                        def mid(k):
                            act.wait_ge(s_rre, u0 + k + 3)
                            act.activation(RP[:, k % 2, 1, :, :], R_left[:, k % 2, :, :], ACT.Copy)\
                                .then_inc(s_rmi, 1)

                        for k in range(ITER):
                            first(k)
                            mid(k)

            split_hi_mid(L0)

            def read_acc(s):
                act.wait_ge(s_seg, P * ((s + 1) * NQ) + ITER)
                for j in range(NC):
                    c = 128 * len(TILES[j])
                    if s == L0 and j == NC - 1:
                        act.wait_ge(ev["DG"], 1)
                    act.activation(ST[:, 512 * j:512 * j + c], bank(j, c), ACT.Copy).then_inc(s_acc, 1)

            read_acc(L0)
            act.wait_ge(s_degs, 1)
            act.activation(dv[:, T0_, :], dv[:, T0_, :], ACT.Sqrt).then_inc(s_degs, 1)
            act.activation(dv[:, T1_, :], dv[:, T1_, :], ACT.Sqrt).then_inc(s_degs, 1)
            for j in range(NC):
                act.wait_ge(mm["R"], j + 1)
                c = 128 * len(TILES[j])
                act.activation(r_bc[:, 512 * j:512 * j + c], bank(j, c), ACT.Copy).then_inc(ev["R"], 1)
            for j in range(NC):
                act.wait_ge(mm["U"], j + 1)
                c = 128 * len(TILES[j])
                act.activation(ST[:, 512 * j:512 * j + c], bank(j, c), ACT.Relu, bias=cols[:, 1:2])\
                    .then_inc(ev["U"], 1)
            pipeline(root(1), rows(1, h, ACT.Identity, h), lambda j: None, root(2), rows(2, h, ACT.Relu, x),
                     split_rows("H1", h, 2))
            read_acc(L1)
            pipeline(root(3), rows(3, h, ACT.Relu, x))

            split_hi_mid(L2)
            read_acc(L2)
            pipeline(root(4), rows(4, h, ACT.Relu, x, scaled=g3), split_rows("G3", g3, 4))
            own = hT[:, :].rearrange("p (t d) -> p t d", d=D)
            for t in range(NT):
                last = act.activation(own[:, t, :], h[:, t, :], ACT.Copy, scale=dv[:, SELF3, t:t + 1])
            last.then_inc(s_bias, 1)
            read_acc(L3)

        @block.vector
        def _(dve):
            links = [0]

            def link(ins):
                links[0] += 1
                ins.then_inc(s_dve, 1)
                dve.wait_ge(s_dve, links[0])

            dve.memset(dst_l[QA:NQ, :], PAD_DST).then_inc(s_pad, 1)
            dve.memset(src_l[QA:NQ, :], 0).then_inc(s_pad, 1)
            dve.memset(w_l[QA:NQ, :], 0.0).then_inc(s_pad, 1)
            dve.memset(ea_l[QA:NQ, :], 0.0).then_inc(s_pad, 1)
            dve.memset(x[:, NT - 1, :], 0.0).then_inc(s_pad, 1)
            dve.wait_ge(s_dst, 48)
            link(dve.tensor_copy(dst_f, dst_l))
            dve.tensor_reduce(blk[0:NQ, 0:1], dst_f, AX.X, ALU.min)
            link(dve.tensor_reduce(blk[0:NQ, 1:2], dst_f, AX.X, ALU.max))
            link(dve.tensor_copy(blk_i[0:NQ, :], blk[0:NQ, :]))
            link(dve.tensor_single_scalar(blk_s[0:NQ, :], blk_i[0:NQ, :], 6, ALU.arith_shift_right))
            dve.tensor_scalar(base64[0:NQ, :], blk_s[0:NQ, 0:1], float(WB), None, ALU.mult).then_inc(s_prep, 1)
            dve.wait_ge(s_prep, 1)
            dve.tensor_scalar(dst_r, dst_f, base64[0:NQ, 0:1], None, ALU.subtract).then_inc(s_prep, 1)
            dve.wait_ge(s_src, 96)
            dve.tensor_copy(src_f, src_l).then_inc(s_prep, 1)

            def variance(n, source):
                def stage(j):
                    for t in TILES[j]:
                        last = dve.bn_stats(bn[:, t, :], source[:, t, :])
                    link(last)
                    for t in TILES[j]:
                        last = dve.bn_aggr(mv[:, t, :], bn[:, t, :])
                    last.then_inc(s_var[n], 1)
                return stage

            def norm(n, by=None, by2=None):
                def stage(j):
                    ts = slice(TILES[j][0], TILES[j][-1] + 1)
                    dve.wait_ge(s_root[n], j + 1)
                    link(dve.reciprocal(rs[:, ts], sd[:, ts]))
                    if by is not None:
                        link(dve.tensor_tensor(rs[:, ts], rs[:, ts], dv[:, by, ts], ALU.mult))
                    last = dve.scalar_tensor_tensor(nb[:, ts], mv[:, ts, 0], -1.0, rs[:, ts], ALU.mult, ALU.mult)
                    if by2 is not None:
                        link(last)
                        dve.tensor_tensor(rs2[:, ts], rs[:, ts], dv[:, by2, ts], ALU.mult)
                        last = dve.tensor_tensor(nb2[:, ts], nb[:, ts], dv[:, by2, ts], ALU.mult)
                    last.then_inc(s_norm[n], 1)
                return stage

            dve.wait_ge(s_x, 32)
            pipeline(variance(0, x), norm(0))

            dve.wait_ge(s_row, 16)
            link(dve.tensor_copy(row_f[:, :, :], row_i[:, :, :]))
            link(dve.tensor_tensor(far[:, :], row_f[:, :, 1], row_f[:, :, 0], ALU.subtract))
            link(dve.tensor_reduce(far1[:, :], far[:, :], AX.X, ALU.max))
            link(dve.tensor_copy(far_i[:, :], far1[:, :]))
            link(dve.tensor_single_scalar(far_s[:, :], far_i[:, :], 1, ALU.arith_shift_right))
            dve.tensor_scalar(passes_i[:, :], far_s[:, :], 1.0, None, ALU.add).then_inc(s_pass, 1)

            dve.wait_ge(s_wcp, 1)
            dve.tensor_tensor(wcr[:, :], wcf[:, :], wcp[:, 0, :], ALU.subtract).then_inc(s_wcp, 1)
            dve.wait_ge(s_wcp, 3)
            dve.tensor_tensor(wcr[:, :], wcr[:, :], wcp[:, 1, :], ALU.subtract).then_inc(s_wcp, 1)

            for n, (to, j) in enumerate(((dstT, 1), (idx, 0), (wT, 2))):
                dve.wait_ge(s_prepT, n + 1)
                dve.tensor_copy(to[:, :, :].rearrange("p q c -> p c q"),
                                bank(j, 4 * NQ).rearrange("p (c q) -> p c q", c=4)).then_inc(s_prepE, 1)
            dve.wait_ge(s_prepE, 3)
            dve.wait_ge(s_con, 9)
            link(dve.tensor_copy(wq[:, :, :, 1], wT[:, :, :]))
            link(dve.tensor_tensor(wr[:, 0, :, :], wT[:, :, :], wq[:, :, :, 1], ALU.subtract))
            link(dve.tensor_copy(wq[:, :, :, 2], wr[:, 0, :, :]))
            link(dve.tensor_tensor(wr[:, 1, :, :], wr[:, 0, :, :], wq[:, :, :, 2], ALU.subtract))
            link(dve.tensor_copy(wq[:, :, :, 3], wr[:, 1, :, :]))

            dve.wait_ge(s_wt, 16 * 19)
            for m, tiles in enumerate(HALVES):
                n = len(tiles)
                dve.wait_ge(mm["PQ"], m + 1)
                if m >= 2:
                    dve.wait_ge(s_re, m - 1)
                dve.tensor_tensor(pq[:, m % 2, 0:n, :, :],
                                  bank(m % 8, 256 * n).rearrange("p (t w d) -> p t w d", w=2, d=D),
                                  bc[:, B_P:B_Q + 1, :].rearrange("p (a w) d -> p a w d", a=1)
                                  .to_broadcast([128, n, 2, D]), ALU.add).then_inc(ev["PQ"], 1)

            P = dve.value_load(passes_i[0:1, 0:1], min_val=1, max_val=MAXP)

            def start_tables():
                dve.tensor_scalar(tab_f[:, :], row_f[:, :, 0], -2.0, None, ALU.add)
                dve.tensor_scalar(pio_w[:, :], pio[:, :], -128.0, None, ALU.add)
                link(dve.tensor_scalar(iota_w[:, :], iota[:, :], -128.0, None, ALU.add))

            def move_tables(s, w):
                dve.wait_ge(s_seg, (P * s + w) * NQ + ITER)
                dve.tensor_scalar(tab_f[:, :], tab_f[:, :], 2.0, float(NB - 1), ALU.add, ALU.min)\
                    .then_inc(s_tab, 1)
                dve.tensor_scalar(pio_w[:, :], pio_w[:, :], 128.0, None, ALU.add).then_inc(s_tab, 1)
                dve.tensor_scalar(iota_w[:, :], iota_w[:, :], 128.0, None, ALU.add).then_inc(s_tab, 1)
                dve.wait_ge(s_tab, (P * s + w) * 4 + 3)
                dve.tensor_copy(tab_i[:, :], tab_f[:, :]).then_inc(s_tab, 1)

            def onehot(s, w, i, k):
                dve.wait_ge(s_seg, step_count(s, w, i, P) * ITER + k + 1)
                dve.tensor_tensor(oh[:, k, :, :],
                                  iota_w[:, :].rearrange("p (a n) -> p a n", a=1).to_broadcast([128, 4, 128]),
                                  dstT[:, bass.ds(i * ITER + k, 1), :].rearrange("p a (c b) -> p (a c) b", b=1)
                                  .to_broadcast([128, 4, 128]), ALU.is_equal).then_inc(s_oh, 1)

            def row_rest(u, k):
                dve.wait_ge(s_rhi, u + 1)
                dve.tensor_tensor(R_left[:, k % 2, :, :], R[:, k % 2, :, :], RP[:, k % 2, 0, :, :], ALU.subtract)\
                    .then_inc(s_rre, 1)

            def row_lo(u, k):
                dve.wait_ge(s_rmi, u + 1)
                dve.tensor_tensor(RP[:, k % 2, 2, :, :], R_left[:, k % 2, :, :], RP[:, k % 2, 1, :, :],
                                  ALU.subtract).then_inc(s_rlo, 1)

            start_tables()
            with dve.Fori(0, P) as w:
                move_tables(L0, w)
                with dve.Fori(0, NI) as i:
                    steps = w * NI + i

                    def build(k):
                        onehot(L0, w, i, k)
                        dve.wait_ge(s_rl[k], (steps + 1) * 32)
                        dve.tensor_scalar(sT[:, k, :], row_bc[:, k, :], pio_w[:, 0:1], None, ALU.is_equal)\
                            .then_inc(s_sT, 1)

                    build(0)
                    build(1)
                    for k in range(ITER):
                        row_rest(steps * ITER + k, k)
                        if k + 2 < ITER:
                            build(k + 2)
                        row_lo(steps * ITER + k, k)

            dve.wait_ge(s_seg, P * NQ + ITER)
            link(dve.tensor_copy(degs[:, 1:1 + NB, :],
                                 ps[:, DEG:DEG + 4 * NB].rearrange("p (b f) -> p b f", f=4)))
            dve.tensor_copy(deg2[:, 0, 0:NB + 1], degs[:, :, 0])
            link(dve.tensor_tensor(deg2[:, 1, 0:NB + 1], degs[:, :, 2], degs[:, :, 3], ALU.add))
            link(dve.tensor_tensor(deg2[:, 1, 0:NB + 1], deg2[:, 1, 0:NB + 1], degs[:, :, 1], ALU.add))
            dve.memset(deg2[:, :, NB + 1:2 * NT + 1], 0.0).then_inc(ev["DG"], 1)
            dve.wait_ge(mm["DG"], 1)
            link(dve.tensor_copy(cnt[:, :, :], ps[:, PRE:PRE + 2 * NT].rearrange("p (f t) -> p f t", f=2)))
            link(dve.tensor_scalar(dv[:, INV_CNT, :], cnt[:, 0, :], 1.0, None, ALU.max))
            dve.reciprocal(dv[:, INV_CNT, :], dv[:, INV_CNT, :])
            dve.tensor_scalar(dv[:, HAS, :], cnt[:, 0, :], 1.0, None, ALU.min).then_inc(ev["DG"], 1)
            dve.tensor_scalar(dv[:, T1_, :], cnt[:, 0, :], 1.0, None, ALU.add)
            link(dve.tensor_scalar(dv[:, SELF3, :], cnt[:, 1, :], 1.0, None, ALU.add))
            dve.tensor_scalar(dv[:, DINV2, :], dv[:, SELF3, :], 0.0, None, ALU.is_gt)
            dve.tensor_scalar(dv[:, T0_, :], dv[:, SELF3, :], TINY, None, ALU.max).then_inc(s_degs, 1)
            dve.wait_ge(s_degs, 3)
            dve.reciprocal(dv[:, T0_, :], dv[:, T0_, :])
            link(dve.reciprocal(dv[:, DINV3, :], dv[:, T1_, :]))
            dve.tensor_tensor(dv[:, DINV2, :], dv[:, DINV2, :], dv[:, T0_, :], ALU.mult)
            link(dve.tensor_scalar(dv[:, D09, :], dv[:, DINV3, :], 0.9, None, ALU.mult))
            link(dve.tensor_tensor(dv[:, SELF3, :], dv[:, D09, :], dv[:, DINV3, :], ALU.mult))
            link(dve.tensor_scalar(dv[:, SELF3, :], dv[:, SELF3, :], 0.1, None, ALU.add))
            for j in range(NC):
                dve.wait_ge(s_acc, j + 1)
                dve.wait_ge(mm["B"], j + 1)
                c = 128 * len(TILES[j])
                dve.tensor_tensor(ST[:, 512 * j:512 * j + c], ST[:, 512 * j:512 * j + c], bank(j, c), ALU.mult)\
                    .then_inc(ev["B"], 1)
            for j in range(NC):
                dve.wait_ge(mm["A"], j + 1)
                c = 128 * len(TILES[j])
                dve.scalar_tensor_tensor(aggT[:, 512 * j:512 * j + c], r_bc[:, 512 * j:512 * j + c], cols[:, 0:1],
                                         bank(j, c), ALU.mult, ALU.add).then_inc(ev["A"], 1)

            def tiles_of(a, j):
                return a[:, TILES[j][0]:TILES[j][-1] + 1, :]

            def bias_of(slot, n):
                return bc[:, slot:slot + 1, :].to_broadcast([128, n, D])

            def bank_of(j):
                return bank(j, 128 * len(TILES[j])).rearrange("p (t d) -> p t d", d=D)

            def update(j):
                dve.wait_ge(mm["V"], j + 1)
                dve.tensor_tensor(tiles_of(h, j), bank_of(j), tiles_of(h, j), ALU.add).then_inc(ev["V"], 1)
                dve.wait_ge(ev["V"], j + 1)
                link(dve.tensor_tensor(tiles_of(h, j), tiles_of(h, j), bias_of(B_U2, len(TILES[j])), ALU.add))

            def residual(j):
                n = len(TILES[j])
                dve.wait_ge(s_rows[1], j + 1)
                link(dve.tensor_tensor(tiles_of(h, j), tiles_of(h, j), bias_of(B_GA, n), ALU.mult))
                link(dve.tensor_tensor(tiles_of(x, j), tiles_of(x, j), bias_of(B_BE, n), ALU.add))
                link(dve.tensor_tensor(tiles_of(x, j), tiles_of(x, j), tiles_of(h, j), ALU.add))

            def both(*stages):
                def stage(j):
                    for s in stages:
                        s(j)
                return stage

            pipeline(both(update, variance(1, h)), norm(1), both(residual, variance(2, x)), norm(2))
            for j in range(NC):
                dve.wait_ge(mm["T1"], j + 1)
                c = 128 * len(TILES[j])
                dve.tensor_copy(hT[:, 512 * j:512 * j + c], bank(j, c)).then_inc(ev["T1"], 1)

            def plain_sweep(s):
                start_tables()
                with dve.Fori(0, P) as w:
                    move_tables(s, w)
                    with dve.Fori(0, NI) as i:
                        for k in range(ITER):
                            onehot(s, w, i, k)

            def add_bias(*slots):
                for slot in slots:
                    link(dve.tensor_tensor(x[:, :, :], x[:, :, :], bias_of(slot, NT), ALU.add))

            add_bias(B_L1, B_L1B)
            plain_sweep(L1)

            def out1(j):
                dve.wait_ge(mm["O1"], j + 1)
                dve.tensor_tensor(tiles_of(x, j), tiles_of(x, j), bank_of(j), ALU.add).then_inc(ev["O1"], 1)
                dve.wait_ge(ev["O1"], j + 1)

            pipeline(both(out1, variance(3, x)), norm(3, by=DINV2))
            for j in range(NC):
                dve.wait_ge(mm["T2"], j + 1)
                c = 128 * len(TILES[j])
                dve.tensor_copy(hT[:, 512 * j:512 * j + c], bank(j, c)).then_inc(ev["T2"], 1)
            add_bias(B_L2)

            start_tables()
            with dve.Fori(0, P) as w:
                move_tables(L2, w)
                with dve.Fori(0, NI) as i:
                    steps = step_count(L2, w, i, P)
                    split0 = step_count(L1, w, i, P) * ITER

                    def weigh(k):
                        dve.wait_ge(s_gat[k], (steps + 1) * 64)
                        dve.wait_ge(s_rre, split0 + k + 1)
                        dve.tensor_tensor(R[:, k % 2, :, :], G[:, k, :, 0:2 * D].bitcast(fp32),
                                          wT[:, bass.ds(i * ITER + k, 1), :].rearrange("p a (c b) -> p (a c) b", b=1)
                                          .to_broadcast([128, 4, D]), ALU.mult).then_inc(s_R, 1)

                    onehot(L2, w, i, 0)
                    weigh(0)
                    for k in range(ITER):
                        row_rest(split0 + k, k)
                        if k + 1 < ITER:
                            onehot(L2, w, i, k + 1)
                            weigh(k + 1)
                        row_lo(split0 + k, k)

            def out2(j):
                dve.wait_ge(mm["O2"], j + 1)
                for n, t in enumerate(TILES[j]):
                    last = dve.scalar_tensor_tensor(x[:, t, :], bank(j)[:, 128 * n:128 * n + 128],
                                                    dv[:, DINV2, t:t + 1], x[:, t, :], ALU.mult, ALU.add)
                last.then_inc(ev["O2"], 1)
                dve.wait_ge(ev["O2"], j + 1)

            pipeline(both(out2, variance(4, x)), norm(4, by2=DINV3))
            dve.wait_ge(s_rows[4], NC)
            link(dve.tensor_tensor(x[:, :, :], x[:, :, :], h[:, :, :], ALU.add))
            plain_sweep(L3)
            own = hT[:, :].rearrange("p (t d) -> p t d", d=D)
            dve.wait_ge(s_bias, 1)
            for j in range(NC):
                dve.wait_ge(mm["O3"], j + 1)
                for n, t in enumerate(TILES[j]):
                    last = dve.scalar_tensor_tensor(own[:, t, :], bank(j)[:, 128 * n:128 * n + 128],
                                                    dv[:, D09, t:t + 1], own[:, t, :], ALU.mult, ALU.add)
                link(last)
                dve.scalar_tensor_tensor(tiles_of(h, j), tiles_of(own, j), 0.0, tiles_of(x, j), ALU.max, ALU.add)\
                    .then_inc(s_fin, 1)

        @block.tensor
        def _(pe):
            pe.wait_ge(s_con, 9)
            for n, (array, j, ready, value) in enumerate(((dst_r, 1, s_prep, 2), (src_f, 0, s_prep, 3),
                                                          (w_l, 2, s_src, 96))):
                pe.wait_ge(ready, value)
                for c in range(4):
                    last = pe.transpose(ps[:, 512 * j + NQ * c:512 * j + NQ * (c + 1)],
                                        array[:, 128 * c:128 * c + 128], ident[0:NQ, 0:NQ])
                last.then_inc(s_prepT, 1)

            def transposes(stage, source, ready):
                for j, tiles in enumerate(TILES):
                    ready(j)
                    for n, t in enumerate(tiles):
                        last = pe.transpose(ps[:, 512 * j + 128 * n:512 * j + 128 * n + 128], source[:, t, :],
                                            ident[:, :])
                    last.then_inc(mm[stage], 1)

            def h0_ready(j):
                pe.wait_ge(s_rows[0], j + 1)
                if j == 0:
                    pe.wait_ge(s_prepE, 3)
            transposes("T0", h, h0_ready)

            pe.wait_ge(s_wt, 16 * 19)
            pe.wait_ge(ev["T0"], NC)
            for m, tiles in enumerate(HALVES):
                if m >= 8:
                    pe.wait_ge(ev["PQ"], m - 7)
                for n, t in enumerate(tiles):
                    b = 512 * (m % 8) + 256 * n
                    last = pe.matmul(ps[:, b:b + 256], hT[:, 128 * t:128 * t + 128],
                                     wab[:, :, :].rearrange("p w d -> p (w d)"), start=True, stop=True)
                last.then_inc(mm["PQ"], 1)

            pe.wait_ge(s_pass, 1)
            P = pe.value_load(passes_i[0:1, 0:1], min_val=1, max_val=MAXP)

            def zero_acc():
                for b in range(ACC_BANKS):
                    last = pe.matmul(bank(b), zerob[:, 0:128], zerob[:, :], start=True, stop=True)
                last.then_inc(s_zero, 1)

            def add_to(col, width, lhsT, rhs):
                return pe.matmul(ps[:, bass.ds(col, width)], lhsT, rhs, start=False, stop=True,
                                 skip_group_check=True)

            def sum_chunk(b, rows, k, c):
                for half in range(2):
                    for a in range(PARTS):
                        last = add_to(b * WB + WB * half, WB, rows(a), oh[:, k, c, WB * half:WB * half + WB])
                return last

            pe.wait_ge(ev["PQ"], NH)
            zero_acc()
            pe.sem_inc(s_seg, ITER)
            pe.sem_inc(s_pre, ITER)
            pe.sem_inc(s_R, 1)
            pe.sem_inc(s_rre, 2)
            pe.wait_ge(s_qw, 32)
            pe.wait_ge(s_wc18, 16 * 2 * PARTS)

            with pe.Fori(0, P) as w:
                with pe.Fori(0, NI) as i:
                    pe.wait_ge(s_tab, w * 4 + 4)
                    steps = w * NI + i
                    quads = steps * ITER
                    base = {}

                    def pre(k):
                        base[k] = pe.value_load(tab_i[0:1, bass.ds(i * ITER + k, 1)], min_val=0, max_val=NB - 1)
                        pe.wait_ge(s_sT, quads + k + 1)
                        pe.wait_ge(s_rl[k], (steps + 1) * 32)
                        pe.wait_ge(s_gat[k], (steps + 1) * 64)
                        pe.wait_ge(s_R, quads + k + 1)
                        for c in range(4):
                            to = ps[:, PRE + 128 * c:PRE + 128 * c + 128]
                            edges = slice(128 * c, 128 * c + 128)
                            pe.matmul(to, ea18[:, k, edges], wc18[:, :], start=True, stop=False)
                            for a in range(PARTS):
                                pe.matmul(to, identb[:, :], G[:, k, c, D * a:D * a + D], start=False, stop=False)
                            for a in range(PARTS):
                                last = pe.matmul(to, sT[:, k, edges],
                                                 Qw[:, bass.ds(base[k], 1), D * a:D * a + D]
                                                 .rearrange("p a d -> p (a d)"),
                                                 start=False, stop=a == PARTS - 1)
                        last.then_inc(s_pre, 1)

                    def seg(k):
                        pe.wait_ge(s_oh, quads + k + 1)
                        pe.wait_ge(s_rlo, quads + k + 1)
                        for c in range(4):
                            add_to(base[k] * 4 + DEG, 4, oh[:, k, c, :],
                                   wq[:, bass.ds(i * ITER + k, 1), c, :].rearrange("p a f -> p (a f)"))
                            last = sum_chunk(base[k], lambda a: RP[:, k % 2, a, c, :], k, c)
                        last.then_inc(s_seg, 1)

                    pre(0)
                    for k in range(ITER):
                        if k + 1 < ITER:
                            pre(k + 1)
                        seg(k)

            pe.wait_ge(ev["DG"], 1)
            for f in range(2):
                to = ps[:, PRE + NT * f:PRE + NT * f + NT]
                pe.matmul(to, shift[:, WB:WB + 128], deg2[:, f, 1:2 * NT:2], start=True, stop=False)
                pe.matmul(to, shift[:, 128:256], deg2[:, f, 0:2 * NT - 1:2], start=False, stop=False)
                last = pe.matmul(to, shift[:, 0:128], deg2[:, f, 2:2 * NT + 1:2], start=False, stop=True)
            last.then_inc(mm["DG"], 1)
            pe.wait_ge(ev["DG"], 2)
            for stage, slot in (("B", INV_CNT), ("R", HAS)):
                for j, tiles in enumerate(TILES):
                    if stage == "B":
                        pe.wait_ge(s_acc, j + 1)
                    else:
                        pe.wait_ge(ev["B"], j + 1)
                    for n, t in enumerate(tiles):
                        last = pe.matmul(ps[:, 512 * j + 128 * n:512 * j + 128 * n + 128],
                                         dv[:, slot, t:t + 1].to_broadcast([128, 128]), ident[:, :],
                                         start=True, stop=True)
                    last.then_inc(mm[stage], 1)
            for j, tiles in enumerate(TILES):
                pe.wait_ge(ev["R"], j + 1)
                c = 128 * len(tiles)
                pe.matmul(bank(j, c), w_m2[:, :], ST[:, 512 * j:512 * j + c], start=True, stop=True)\
                    .then_inc(mm["A"], 1)
            for j, tiles in enumerate(TILES):
                pe.wait_ge(ev["A"], j + 1)
                c = 128 * len(tiles)
                pe.matmul(bank(j, c), w_u1[:, 0, :], hT[:, 512 * j:512 * j + c], start=True, stop=False)
                pe.matmul(bank(j, c), w_u1[:, 1, :], aggT[:, 512 * j:512 * j + c], start=False, stop=True)\
                    .then_inc(mm["U"], 1)

            def by_node(stage, ready, *products):
                for j, tiles in enumerate(TILES):
                    ready(j)
                    for n, t in enumerate(tiles):
                        for k, (lhsT, weights) in enumerate(products):
                            last = pe.matmul(ps[:, 512 * j + 128 * n:512 * j + 128 * n + 128],
                                             lhsT[:, 128 * t:128 * t + 128], weights[:, :],
                                             start=k == 0, stop=k == len(products) - 1)
                    last.then_inc(mm[stage], 1)

            by_node("V", lambda j: pe.wait_ge(ev["U"], j + 1), (ST, w_u2))
            def h1_ready(j):
                pe.wait_ge(s_rows[2], j + 1)
            transposes("T1", h, h1_ready)
            pe.wait_ge(ev["T1"], NC)

            def plain_sweep(s):
                zero_acc()
                with pe.Fori(0, P) as w:
                    with pe.Fori(0, NI) as i:
                        pe.wait_ge(s_tab, (P * s + w) * 4 + 4)
                        steps = step_count(s, w, i, P)
                        for k in range(ITER):
                            b = pe.value_load(tab_i[0:1, bass.ds(i * ITER + k, 1)], min_val=0, max_val=NB - 1)
                            pe.wait_ge(s_oh, steps * ITER + k + 1)
                            pe.wait_ge(s_gat[k], (steps + 1) * 64)
                            for c in range(4):
                                last = sum_chunk(b, lambda a: G[:, k, c, D * a:D * a + D], k, c)
                            last.then_inc(s_seg, 1)

            plain_sweep(L1)
            by_node("O1", lambda j: pe.wait_ge(s_acc, NC + j + 1), (hT, w_11), (ST, w_12))
            def g2_ready(j):
                pe.wait_ge(s_rows[3], j + 1)
                pe.wait_ge(ev["O1"], j + 1)
            transposes("T2", h, g2_ready)
            pe.wait_ge(ev["T2"], NC)

            zero_acc()
            with pe.Fori(0, P) as w:
                with pe.Fori(0, NI) as i:
                    pe.wait_ge(s_tab, (P * L2 + w) * 4 + 4)
                    steps = step_count(L2, w, i, P)
                    split0 = step_count(L1, w, i, P) * ITER
                    for k in range(ITER):
                        b = pe.value_load(tab_i[0:1, bass.ds(i * ITER + k, 1)], min_val=0, max_val=NB - 1)
                        pe.wait_ge(s_oh, steps * ITER + k + 1)
                        pe.wait_ge(s_rlo, split0 + k + 1)
                        for c in range(4):
                            last = sum_chunk(b, lambda a: RP[:, k % 2, a, c, :], k, c)
                        last.then_inc(s_seg, 1)
            by_node("O2", lambda j: pe.wait_ge(s_acc, 2 * NC + j + 1), (ST, w_3), (hT, w_3))
            pe.wait_ge(ev["O2"], NC)
            plain_sweep(L3)
            transposes("O3", ST[:, :].rearrange("p (t d) -> p t d", d=D),
                       lambda j: pe.wait_ge(s_acc, 3 * NC + j + 1))


_INS = ['x', 'src', 'dst', 'edge_attr_2', 'edge_weight', 'L0_gnn_mW1', 'L0_gnn_mb1', 'L0_gnn_mW2', 'L0_gnn_mb2',
        'L0_gnn_uW1', 'L0_gnn_ub1', 'L0_gnn_uW2', 'L0_gnn_ub2', 'L0_gnn_gamma', 'L0_gnn_beta', 'L1_gnn_W1',
        'L1_gnn_b1', 'L1_gnn_W2', 'L1_gnn_b2', 'L2_gnn_W', 'L2_gnn_bias']
_OUT = (3125, 128)


def kernel(**inputs):
    import numpy as _np
    import concourse.bacc as _bacc
    from concourse import mybir as _mybir
    from concourse.bass_utils import run_bass_kernel_spmd as _run

    nc = _bacc.Bacc("TRN2", target_bir_lowering=False, num_devices=1)
    arrays, args = {}, []
    for name in _INS:
        a = _np.ascontiguousarray(inputs[name])
        arrays[f"in_{name}"] = a
        args.append(nc.dram_tensor(f"in_{name}", a.shape, _mybir.dt.from_np(a.dtype), kind="ExternalInput").ap())
    args.append(nc.dram_tensor("out_0", _OUT, _mybir.dt.float32, kind="ExternalOutput").ap())
    gnn_kernel(nc, *args)
    r = _run(nc, [arrays], core_ids=[0])
    return r.results[0]["out_0"]
```

```python
import concourse.bass as bass
from concourse import mybir
from contextlib import ExitStack



def gnn_kernel(nc, x_in, src_in, dst_in, ea_in, ew_in, mW1, mb1, mW2, mb2, uW1, ub1, uW2, ub2,
               gamma, beta, W1, b1, W2, b2, W3, b3, out):
    fp32, bf16 = mybir.dt.float32, mybir.dt.bfloat16
    i32, u32 = mybir.dt.int32, mybir.dt.uint32
    ALU = mybir.AluOpType
    ACT = mybir.ActivationFunctionType
    AX = mybir.AxisListType

    N, D = x_in.shape
    E = src_in.shape[0]
    EPS = 1e-5
    TINY = 2.0 ** -116
    NT = -(-N // 128)
    NP = NT * 128
    NR = N - (NT - 1) * 128
    QE = 512
    NQ = -(-E // QE)
    ITER = 4
    NI = NQ // ITER
    assert NI * ITER == NQ
    QR = E - (NQ - 1) * QE
    QA = NQ // 32 * 32
    WB = 64
    NB = -(-N // WB)
    PAD_DST = NB * WB - 1
    assert N <= PAD_DST < NP
    MAXP = (NB - 1) // 2 + 1
    PARTS = 3
    NC = -(-NT // 4)
    TILES = [list(range(4 * j, min(4 * j + 4, NT))) for j in range(NC)]
    HALVES = [list(range(2 * m, min(2 * m + 2, NT))) for m in range(-(-NT // 2))]
    ACC_BANKS = -(-NB * WB // 512)
    DEG = 512 * (ACC_BANKS - 1) + 128
    assert NB * WB <= DEG and DEG + 4 * NB <= 512 * ACC_BANKS and ACC_BANKS < 8
    PRE = 7 * 512
    CB = 16
    CT = 4
    NCB = 2 * NQ
    assert NCB * CB >= NP and NT * CB <= 512 and NCB * CT % 2 == 0 and NT < 32
    CW = NT * CB
    CQ = 512 // (2 * CB)

    P_tab = nc.dram_tensor("p_parts", [NP, PARTS * D], bf16).ap()
    Q_tab = nc.dram_tensor("q_parts", [NP, PARTS * D], bf16).ap()
    H1_tab = nc.dram_tensor("h1_parts", [NP, PARTS * D], bf16).ap()
    G2_tab = nc.dram_tensor("g2_rows", [NP, D], fp32).ap()
    G3_tab = nc.dram_tensor("g3_parts", [NP, PARTS * D], bf16).ap()
    dst_row = nc.dram_tensor("dst_row", [NQ, QE], fp32).ap()
    ea_rows = nc.dram_tensor("ea_rows", [18, NQ * QE], bf16).ap()
    blk_tab = nc.dram_tensor("blk_tab", [NQ, 2], i32).ap()
    cnt_tab = nc.dram_tensor("count_blocks", [NQ, 128, 2 * CW], bf16).ap()
    first_tab = nc.dram_tensor("first_store", [2, 128], bf16).ap()
    wc_tab = nc.dram_tensor("wc_parts", [2, PARTS, D], bf16).ap()

    ctx = ExitStack()
    with ctx:
        def sb(name, shape, dt=fp32):
            return ctx.enter_context(nc.sbuf_tensor(name, shape, dt))

        def sem(name):
            return ctx.enter_context(nc.semaphore(name))

        x = sb("x", [128, NT, D])
        h = sb("h", [128, NT, D])
        hT = sb("hT", [128, NP])
        ST = sb("ST", [128, NP])
        aggT = sb("aggT", [128, NP])
        g3 = aggT[:, :].rearrange("p (t d) -> p t d", d=D)
        r_bc = sb("r_bc", [128, NP], bf16)
        bn = sb("bn", [128, NT, 6])
        mv = sb("mv", [128, NT, 2])
        sd = sb("sd", [128, NT])
        rs = sb("rs", [128, NT])
        nb = sb("nb", [128, NT])
        rs2 = sb("rs2", [128, NT])
        nb2 = sb("nb2", [128, NT])
        pq = sb("pq", [128, 2, 2, 2, D])
        Hp = sb("Hp", [128, NT, PARTS, D], bf16)
        parts = Hp[:, 0:8, :, :].rearrange("p (b t w) a d -> p b t w a d", b=2, t=2)
        rest = sb("rest", [128, 2, 4 * D])
        degs = sb("degs", [128, 1 + NB, 4])
        deg2 = sb("deg2", [128, 2, 2 * NT + 1])
        cnt = sb("cnt", [128, 2, NT])
        dv = sb("dv", [128, 8, NT])
        INV_CNT, HAS, DINV2, DINV3, D09, SELF3, T0_, T1_ = range(8)
        ident = sb("ident", [128, 128])
        shift = sb("shift", [128, 256])
        identb = sb("identb", [128, 128], bf16)
        iota = sb("iota", [128, 128])
        iota_w = sb("iota_w", [128, 128])
        pio = sb("pio", [128, 1])
        pio_w = sb("pio_w", [128, 1])
        eps = sb("eps", [128, 1])
        zerob = sb("zerob", [128, 512], bf16)
        wab = sb("wab", [128, 2, D])
        w_m2 = sb("w_m2", [128, D])
        w_u1 = sb("w_u1", [128, 2, D])
        w_u2 = sb("w_u2", [128, D])
        w_11 = sb("w_11", [128, D])
        w_12 = sb("w_12", [128, D])
        w_3 = sb("w_3", [128, D])
        wcf = sb("wcf", [2, D])
        wcp = sb("wcp", [2, PARTS, D], bf16)
        wcr = sb("wcr", [2, D])
        wc18 = sb("wc18", [18, D], bf16)
        cols = sb("cols", [128, 2])
        bc = sb("bc", [128, 8, D])
        B_P, B_Q, B_U2, B_GA, B_BE, B_L1, B_L1B, B_L2 = range(8)
        onesb = sb("onesb", [128, 128], bf16)
        ones = sb("ones", [128, 1])
        iota_i = sb("iota_i", [128, NT, CB])
        iota_m = sb("iota_m", [128, CW], mybir.dt.float16)
        iota_b = sb("iota_b", [128, NCB])
        iota_c = sb("iota_c", [128, CT])
        idx = sb("idx", [128, NQ, 4], u32)
        idx_q = sb("idx_q", [128, ITER, 4], u32)
        dstT = sb("dstT", [128, NQ, 4])
        wT = sb("wT", [128, NQ, 4])
        wq = sb("wq", [128, NQ, 4, 4], bf16)
        blk = sb("blk", [128, 2])
        blk_i = sb("blk_i", [128, 2], i32)
        blk_s = sb("blk_s", [128, 2], i32)
        base64 = sb("base64", [128, 1])
        row_i = sb("row_i", [1, NQ, 2], i32)
        row_f = sb("row_f", [1, NQ, 2])
        far = sb("far", [1, NQ])
        far1 = sb("far1", [1, 1])
        far_i = sb("far_i", [1, 1], i32)
        far_s = sb("far_s", [1, 1], i32)
        passes_i = sb("passes_i", [1, 1], i32)
        tab_f = sb("tab_f", [1, NQ])
        tab_i = sb("tab_i", [1, NQ], i32)
        room = sb("room", [128, 2 * CQ * 2 * CW], bf16)
        sel = room[:, 0:8 * NCB * CT].bitcast(fp32).rearrange("p (j c) -> p j c", j=4)
        Qw = room[:, 0:NB * PARTS * D].rearrange("p (b c) -> p b c", b=NB)
        AT = NB * PARTS * D
        mov = room[:, AT:AT + 2 * CT * CW].rearrange("p (s j c) -> p s j c", s=2, j=CT)
        AT += 2 * CT * CW
        sta = room[:, AT:AT + 2 * CT * 128].rearrange("p (s j c) -> p s j c", s=2, j=CT)
        assert AT + 2 * CT * 128 <= 2 * CQ * 2 * CW
        counts = room[:, :].rearrange("p (s c) -> p s c", s=2)
        cmax = sb("cmax", [128, 4])
        later = sb("later", [128, 4, NCB], bf16)
        slots = sb("slots", [128, NCB, CT])
        K4 = sb("K4", [128, NCB, CT])
        lo4 = sb("lo4", [128, NCB, CT])
        whole = sb("whole", [128, 2])
        whole1 = sb("whole1", [1, 4])
        many = sb("many", [128, NT])
        flag_i = sb("flag_i", [1, 1], i32)
        cnt_out = sb("cnt_out", [128, 2, 2, CW], bf16)
        ea18 = sb("ea18", [18, ITER, QE], bf16)
        sT = sb("sT", [128, ITER, QE], bf16)
        aggT_b = aggT[:, :].bitcast(bf16)
        G = aggT_b[:, 0:ITER * 4 * PARTS * D].rearrange("p (k c d) -> p k c d", k=ITER, c=4)
        ST_b = ST[:, :].bitcast(bf16)
        oh = ST_b[:, 0:ITER * QE].rearrange("p (k c n) -> p k c n", k=ITER, c=4)
        RP = ST_b[:, ITER * QE:ITER * QE + 2 * PARTS * 4 * D].rearrange("p (k a c d) -> p k a c d", k=2, a=PARTS, c=4)
        Hp_f = Hp[:, :, :, :].rearrange("p t a d -> p (t a d)").bitcast(fp32)
        R = Hp_f[:, 0:8 * D].rearrange("p (k c d) -> p k c d", k=2, c=4)
        R_left = Hp_f[:, 8 * D:16 * D].rearrange("p (k c d) -> p k c d", k=2, c=4)
        row_bc = Hp_f[:, 16 * D:16 * D + ITER * QE].rearrange("p (k e) -> p k e", k=ITER)
        wr = r_bc[:, 2 * QE:2 * QE + 4 * NQ * 4].bitcast(fp32).rearrange("p (s q c) -> p s q c", s=2, q=NQ)
        inb = r_bc[:, 0:2 * NCB * CT].bitcast(fp32).rearrange("p (b j) -> p b j", b=NCB)
        dst_l = hT[0:NQ, 0:QE].bitcast(i32)
        src_l = hT[0:NQ, QE:2 * QE].bitcast(i32)
        w_l = hT[0:NQ, 2 * QE:3 * QE]
        hi_i = hT[0:NQ, 3 * QE:4 * QE].bitcast(i32)
        hi_f = hT[0:NQ, 4 * QE:5 * QE]
        key_f = ST[0:NQ, 5 * QE:6 * QE]
        lo_f = r_bc[0:NQ, 0:2 * QE].bitcast(fp32)
        dst_f = ST[0:NQ, 0:QE]
        src_f = ST[0:NQ, QE:2 * QE]
        ea_l = ST[0:NQ, 2 * QE:4 * QE]
        dst_r = ST[0:NQ, 4 * QE:5 * QE]
        ea_r = aggT[0:NQ, 0:2 * QE].rearrange("p (i e) -> p i e", i=2)
        ea_m = aggT[0:NQ, 2 * QE:5 * QE].bitcast(bf16).rearrange("p (i a e) -> p i a e", i=2, a=PARTS)

        ps = ctx.enter_context(nc.psum_tensor("ps", [128, 8 * 512], fp32))

        def bank(j, n=512):
            return ps[:, 512 * j:512 * j + n]

        s_con = sem("constants_made")
        s_pad = sem("padding_made")
        s_dst = sem("dst_loaded")
        s_src = sem("src_loaded")
        s_ea = sem("ea_loaded")
        s_x = sem("x_loaded")
        s_wt = sem("weights_loaded")
        s_wc = sem("wc_stored")
        s_wc18 = sem("wc18_loaded")
        s_blk = sem("blocks_stored")
        s_row = sem("blocks_loaded")
        s_dr = sem("dst_row_stored")
        s_eas = sem("ea_rows_stored")
        s_pass = sem("passes_known")
        s_prep = sem("edge_prep")
        s_prepT = sem("edge_transposes")
        s_prepE = sem("edge_transposes_read")
        s_wcp = sem("wc_parts")
        s_eap = sem("ea_parts")
        s_dve = sem("dve_chain")
        s_act = sem("act_chain")
        s_pool = sem("pool_chain")
        LN = range(5)
        s_var = [sem(f"ln{n}_variance") for n in LN]
        s_root = [sem(f"ln{n}_root") for n in LN]
        s_norm = [sem(f"ln{n}_scale") for n in LN]
        s_rows = [sem(f"ln{n}_rows") for n in LN]
        STAGES = ["T0", "PQ", "DG", "B", "R", "A", "U", "V", "T1", "O1", "T2", "O2", "O3"]
        mm = {n: sem(f"{n}_done") for n in STAGES}
        ev = {n: sem(f"{n}_read") for n in STAGES}
        s_hi = sem("parts_hi")
        s_re = sem("parts_rest")
        s_mi = sem("parts_mid")
        s_lo = sem("parts_lo")
        s_st = [sem(f"parts_stored_{k}") for k in range(2)]
        s_g2 = sem("g2_stored")
        s_qw = sem("q_windows_loaded")
        s_zero = sem("acc_zeroed")
        s_acc = sem("acc_read")
        s_fin = sem("out_rows")
        s_out = sem("out_stored")
        s_degs = sem("degrees_known")
        s_bias = sem("x_with_bias")
        SW = range(4)
        s_tab = [sem(f"pass_tables_{s}") for s in SW]
        s_oh = [sem(f"onehot_ready_{s}") for s in SW]
        s_seg = [sem(f"quad_summed_{s}") for s in SW]
        s_ix = [sem(f"indices_ready_{s}") for s in SW]
        s_turn = sem("quads_to_gather")
        s_gat = [[sem(f"gathered_{s}_{k}") for k in range(ITER)] for s in SW]
        s_c0 = sem("first_chunks")
        s_slot = sem("slots_ready")
        s_K4 = sem("block_keys_in_psum")
        s_key = sem("block_keys")
        s_cop = sem("count_operands")
        s_cmm = sem("counts_in_psum")
        s_cev = sem("counts_read")
        s_cst = [sem(f"counts_stored_{k}") for k in range(2)]
        s_flag = sem("flag_known")
        s_cld = [sem(f"counts_loaded_{k}") for k in range(2)]
        s_den = {1: sem("dense_1"), 3: sem("dense_3")}
        s_fb = {1: sem("h1_stored"), 3: sem("g3_stored")}
        s_rl = [sem(f"edge_rows_loaded_{k}") for k in range(ITER)]
        s_sT = sem("window_rows_ready")
        s_pre = sem("messages_in_psum")
        s_R = sem("rows_to_split")
        s_rhi = sem("row_hi")
        s_rre = sem("row_rest")
        s_rmi = sem("row_mid")
        s_rlo = sem("row_lo")
        block = ctx.enter_context(nc.Block())

        L0, L1, L2, L3 = range(4)

        def split_count(s, w, i, P):
            return (P * (s // 2) + w) * (NI * ITER) + i * ITER

        def pipeline(*stages):
            for step in range(NC + len(stages) - 1):
                for lag, stage in enumerate(stages):
                    if 0 <= step - lag < NC:
                        stage(step - lag)

        NH = len(HALVES)
        SPLIT0 = {"PQ": 0, "H1": NH, "G3": NH + NC}

        def part(m, a):
            if m < NH:
                return parts[:, m % 2, 0:len(HALVES[m]), :, a, :]
            tiles = TILES[(m - NH) % NC]
            return Hp[:, tiles[0]:tiles[-1] + 1, a, :]

        def stored(m):
            return s_st[m % 2], 32 * (m // 2 + 1)

        def left(m, width):
            if m < NH:
                return rest[:, m % 2, 0:width].rearrange("p (t w d) -> p t w d", w=2, d=D)
            return rest[:, m % 2, 0:width].rearrange("p (t d) -> p t d", d=D)

        @block.sync
        def _(sp):
            sp.dma_start(dst_l[0:QA, :], dst_in[0:QA * QE].rearrange("(p e) -> p e", e=QE)).then_inc(s_dst, 16)
            sp.dma_start(x[:, 0:NT - 1, :], x_in[0:128 * (NT - 1), :].rearrange("(t p) d -> p t d", p=128))\
                .then_inc(s_x, 16)
            sp.wait_ge(s_pad, 5)
            sp.dma_start(x[0:NR, NT - 1, :], x_in[128 * (NT - 1):N, :]).then_inc(s_x, 16)
            for tile, array, width, arrived in ((dst_l, dst_in, QE, s_dst), (src_l, src_in, QE, s_src),
                                                (w_l, ew_in, QE, s_src),
                                                (ea_l, ea_in.rearrange("e i -> (e i)"), 2 * QE, s_ea)):
                if array is not dst_in:
                    sp.dma_start(tile[0:QA, :], array[0:QA * width].rearrange("(p e) -> p e", e=width))\
                        .then_inc(arrived, 16)
                sp.dma_start(tile[QA:NQ - 1, :],
                             array[QA * width:(NQ - 1) * width].rearrange("(p e) -> p e", e=width))\
                    .then_inc(arrived, 16)
                rest_of = QR * (width // QE)
                sp.dma_start(tile[NQ - 1:NQ, 0:rest_of],
                             array[(NQ - 1) * width:(NQ - 1) * width + rest_of].rearrange("(a e) -> a e", a=1))\
                    .then_inc(arrived, 16)
            sp.wait_ge(s_prep, 1)
            sp.dma_start(blk_tab, blk_s[0:NQ, :]).then_inc(s_blk, 16)
            sp.wait_ge(s_blk, 16)
            sp.dma_start(row_i[:, :, :], blk_tab.rearrange("q (a b) -> a q b", a=1)).then_inc(s_row, 16)
            sp.wait_ge(s_prep, 2)
            sp.dma_start(dst_row, dst_r).then_inc(s_dr, 16)
            sp.wait_ge(s_eap, 5)
            for b in range(PARTS):
                sp.dma_start(ea_rows[6 * b:6 * b + 6, :].rearrange("r (p e) -> p r e", e=QE),
                             ea_m.rearrange("p i a e -> p (i a) e")).then_inc(s_eas, 16)
            sp.wait_ge(s_wcp, 5)
            sp.dma_start(wc_tab, wcp[:, :, :]).then_inc(s_wc, 16)
            sp.wait_ge(s_wc, 16)
            for b in range(PARTS):
                for i in range(2):
                    sp.dma_start(wc18[6 * b + 3 * i:6 * b + 3 * i + 3, :],
                                 wc_tab[i, b:b + 1, :].to_broadcast([3, D])).then_inc(s_wc18, 16)
            for m, tiles in enumerate(HALVES):
                sp.wait_ge(s_lo, m + 1)
                t0, n = tiles[0], len(tiles)
                for which, table in enumerate((P_tab, Q_tab)):
                    sp.dma_start(table[128 * t0:128 * (t0 + n), :].rearrange("(t p) c -> p t c", p=128),
                                 parts[:, m % 2, 0:n, which, :, :].rearrange("p t a d -> p t (a d)"))\
                        .then_inc(s_st[m % 2], 16)
            for m in (NH - 2, NH - 1):
                which, value = stored(m)
                sp.wait_ge(which, value)
            sp.wait_ge(s_key, 1)
            for half in range(2):
                sp.dma_start(Qw[WB * half:WB * half + WB, :, :],
                             Q_tab[WB * half:WB * (half + NB), :].rearrange("(b p) c -> p b c", p=WB))\
                    .then_inc(s_qw, 16)
            sp.wait_ge(s_pass, 1)
            P = sp.value_load(passes_i[0:1, 0:1], min_val=1, max_val=MAXP)
            sp.wait_ge(s_dr, 16)
            sp.wait_ge(s_eas, 16 * PARTS)
            sp.wait_ge(s_con, 14)
            for k in range(2):
                sp.dma_start(first_tab[k:k + 1, :], zerob[0:1, 0:128]).then_inc(s_cst[k], 16)
            with sp.Fori(0, P) as w:
                with sp.Fori(0, NI) as i:
                    for k in range(ITER):
                        sp.wait_ge(s_pre, (w * NI + i) * ITER + k + 1)
                        q = i * ITER + k
                        sp.dma_start(row_bc[:, k, :], dst_row[bass.ds(q, 1), :].to_broadcast([128, QE]))\
                            .then_inc(s_rl[k], 16)
                        sp.dma_start(ea18[:, k, :], ea_rows[:, bass.ds(q * QE, QE)]).then_inc(s_rl[k], 16)
            sp.wait_ge(s_flag, 1)
            flag = sp.value_load(flag_i[0:1, 0:1], min_val=0, max_val=1)

            def load_counts(s):
                for j, tiles in enumerate(TILES):
                    n = 4 * len(tiles)
                    c = j + NC * (s // 2)
                    if j >= 2:
                        sp.wait_ge(s_den[s], j - 1)
                    elif s == L3:
                        sp.wait_ge(s_den[L1], NC)
                    sp.dma_start(counts[:, c % 2, 0:n * 2 * CW].rearrange("p (q c) -> p q c", q=n),
                                 cnt_tab[CQ * j:CQ * j + n, :, :].rearrange("q p c -> p q c"))\
                        .then_inc(s_cld[c % 2], 16)

            def store_rows(s, name, table):
                sp.wait_ge(s_lo, SPLIT0[name] + NC)
                sp.dma_start(table.rearrange("(t p) c -> p t c", p=128),
                             Hp[:, :, :, :].rearrange("p t a d -> p t (a d)")).then_inc(s_fb[s], 16)

            with sp.If(flag > 0):
                for k in range(2):
                    sp.wait_ge(s_cst[k], P * (16 * NQ // 2) + 16)
                load_counts(L1)
            with sp.Else():
                store_rows(L1, "H1", H1_tab)
            for j, tiles in enumerate(TILES):
                t0, n = tiles[0], len(tiles)
                sp.wait_ge(s_rows[3], j + 1)
                sp.dma_start(G2_tab[128 * t0:128 * (t0 + n), :].rearrange("(t p) c -> p t c", p=128),
                             h[:, t0:t0 + n, :]).then_inc(s_g2, 16)
            with sp.If(flag > 0):
                load_counts(L3)
            with sp.Else():
                store_rows(L3, "G3", G3_tab)
            for j, tiles in enumerate(TILES):
                sp.wait_ge(s_fin, j + 1)
                t0, full = tiles[0], [t for t in tiles if 128 * (t + 1) <= N]
                if full:
                    sp.dma_start(out[128 * t0:128 * (t0 + len(full)), :].rearrange("(t p) d -> p t d", p=128),
                                 h[:, t0:t0 + len(full), :]).then_inc(s_out, 16)
                if len(full) < len(tiles):
                    sp.dma_start(out[128 * (NT - 1):N, :], h[0:NR, NT - 1, :]).then_inc(s_out, 16)
            sp.wait_ge(s_out, 16 * NC)

        @block.gpsimd
        def _(pool):
            links = [0]

            def link(ins):
                links[0] += 1
                ins.then_inc(s_pool, 1)
                pool.wait_ge(s_pool, links[0])

            pool.memset(zerob[:, :], 0.0).then_inc(s_con, 1)
            pool.memset(eps[:, :], EPS).then_inc(s_con, 1)
            pool.iota(iota[:, :], pattern=[[1, 128]], base=0, channel_multiplier=0,
                      allow_small_or_imprecise_dtypes=True).then_inc(s_con, 1)
            pool.iota(pio[:, :], pattern=[[0, 1]], base=0, channel_multiplier=1,
                      allow_small_or_imprecise_dtypes=True).then_inc(s_con, 1)
            link(pool.memset(shift[:, :], 0.0))
            link(pool.affine_select(out=shift[:, :], in_=shift[:, :], compare_op=ALU.not_equal, fill=1.0, base=WB,
                                    pattern=[[-1, 256]], channel_multiplier=1))
            pool.tensor_copy(ident[:, :], shift[:, WB:WB + 128]).then_inc(s_con, 1)
            pool.tensor_copy(identb[:, :], shift[:, WB:WB + 128]).then_inc(s_con, 1)
            pool.memset(bc[:, B_P, :], 0.0).then_inc(s_con, 1)
            pool.memset(degs[:, 0, :], 0.0).then_inc(s_con, 1)
            pool.memset(wq[:, :, :, 0], 1.0).then_inc(s_con, 1)
            pool.memset(onesb[:, :], 1.0).then_inc(s_con, 1)
            pool.memset(ones[:, :], 1.0).then_inc(s_con, 1)
            pool.iota(iota_i[:, :, :], pattern=[[1, NT], [32, CB]], base=0, channel_multiplier=0,
                      allow_small_or_imprecise_dtypes=True).then_inc(s_con, 1)
            pool.iota(iota_b[:, :], pattern=[[CB, NCB]], base=0, channel_multiplier=0,
                      allow_small_or_imprecise_dtypes=True).then_inc(s_con, 1)
            pool.iota(iota_c[:, :], pattern=[[1, CT]], base=0, channel_multiplier=0,
                      allow_small_or_imprecise_dtypes=True).then_inc(s_con, 1)

            pool.wait_ge(s_ea, 48)
            ea_v = ea_l.rearrange("p (e i) -> p i e", i=2)
            pool.tensor_copy(ea_m[:, :, 0, :], ea_v).then_inc(s_eap, 1)
            pool.wait_ge(s_eap, 1)
            pool.tensor_tensor(ea_r, ea_v, ea_m[:, :, 0, :], ALU.subtract).then_inc(s_eap, 1)
            pool.wait_ge(s_eap, 2)
            pool.tensor_copy(ea_m[:, :, 1, :], ea_r).then_inc(s_eap, 1)
            pool.wait_ge(s_eap, 3)
            pool.tensor_tensor(ea_r, ea_r, ea_m[:, :, 1, :], ALU.subtract).then_inc(s_eap, 1)
            pool.wait_ge(s_eap, 4)
            pool.tensor_copy(ea_m[:, :, 2, :], ea_r).then_inc(s_eap, 1)

            def split_rest(m, source, width):
                pool.wait_ge(s_hi, m + 1)
                pool.tensor_tensor(left(m, width), source, part(m, 0), ALU.subtract).then_inc(s_re, 1)

            def split_lo(m, width):
                pool.wait_ge(s_mi, m + 1)
                pool.tensor_tensor(part(m, 2), left(m, width), part(m, 1), ALU.subtract).then_inc(s_lo, 1)

            for m, tiles in enumerate(HALVES):
                n = len(tiles)
                split_rest(m, pq[:, m % 2, 0:n, :, :], 2 * D * n)
                split_lo(m, 2 * D * n)

            pool.wait_ge(s_pass, 1)
            P = pool.value_load(passes_i[0:1, 0:1], min_val=1, max_val=MAXP)
            pool.wait_ge(s_prepE, 3)

            def sweep(s, table, rows):
                with pool.Fori(0, P) as w:
                    with pool.Fori(0, NI) as i:
                        quads = (w * NI + i) * ITER
                        for k in range(ITER):
                            pool.wait_ge(s_seg[s], quads + k + 1)
                            pool.tensor_copy(idx_q[:, k, :],
                                             idx[:, bass.ds(i * ITER + k, 1), :].rearrange("p a c -> p (a c)"))\
                                .then_inc(s_ix[s], 1)
                            pool.wait_ge(s_ix[s], quads + k + 1)
                            pool.sem_inc(s_turn, 1)
                            for c in range(4):
                                pool.indirect_dma_start(
                                    rows(k, c), None, table,
                                    bass.IndirectOffsetOnAxis(ap=idx_q[:, k, c:c + 1], axis=0))\
                                    .then_inc(s_gat[s][k], 16)

            def rows3(k, c):
                return G[:, k, c, :]

            def rows_f(k, c):
                return G[:, k, c, 0:2 * D].bitcast(fp32)

            for m in (NH - 2, NH - 1):
                which, value = stored(m)
                pool.wait_ge(which, value)
            sweep(L0, P_tab, rows3)
            pool.wait_ge(s_flag, 1)
            flag = pool.value_load(flag_i[0:1, 0:1], min_val=0, max_val=1)

            def split(name, source):
                for j, tiles in enumerate(TILES):
                    t0, n = tiles[0], len(tiles)
                    split_rest(SPLIT0[name] + j, source[:, t0:t0 + n, :], D * n)
                    split_lo(SPLIT0[name] + j, D * n)

            split("H1", h)
            with pool.If(flag > 0):
                pool.sem_inc(s_turn, 1)
            with pool.Else():
                pool.wait_ge(s_fb[L1], 16)
                sweep(L1, H1_tab, rows3)
            pool.wait_ge(s_g2, 16 * NC)
            sweep(L2, G2_tab, rows_f)
            split("G3", g3)
            with pool.If(flag > 0):
                pool.sem_inc(s_turn, 1)
            with pool.Else():
                pool.wait_ge(s_fb[L3], 16)
                sweep(L3, G3_tab, rows3)

        @block.scalar
        def _(act):
            links = [0]

            def link(ins):
                links[0] += 1
                ins.then_inc(s_act, 1)
                act.wait_ge(s_act, links[0])

            loads = [(wab[:, 0, :], mW1[0:D, :]), (wab[:, 1, :], mW1[D:2 * D, :]), (wcf[:, :], mW1[2 * D:2 * D + 2, :]),
                     (w_m2[:, :], mW2), (w_u1[:, 0, :], uW1[0:D, :]), (w_u1[:, 1, :], uW1[D:2 * D, :]),
                     (w_u2[:, :], uW2), (w_11[:, :], W1), (w_12[:, :], W2), (w_3[:, :], W3),
                     (cols[:, 0:1], mb2.rearrange("(p a) -> p a", a=1)),
                     (cols[:, 1:2], ub1.rearrange("(p a) -> p a", a=1))]
            for slot, v in ((B_Q, mb1), (B_U2, ub2), (B_GA, gamma), (B_BE, beta), (B_L1, b1), (B_L1B, b2), (B_L2, b3)):
                loads.append((bc[:, slot, :], v.rearrange("(a d) -> a d", a=1).to_broadcast([128, D])))
            assert len(loads) == 19
            for to, of in loads:
                act.dma_start(to, of).then_inc(s_wt, 16)

            act.wait_ge(s_con, 14)

            def root(n):
                def stage(j):
                    act.wait_ge(s_var[n], j + 1)
                    ts = slice(TILES[j][0], TILES[j][-1] + 1)
                    act.activation(sd[:, ts], mv[:, ts, 1], ACT.Sqrt, bias=eps[:, 0:1]).then_inc(s_root[n], 1)
                return stage

            def rows(n, to, func, source, scaled=None):
                def stage(j):
                    act.wait_ge(s_norm[n], j + 1)
                    for t in TILES[j]:
                        last = act.activation(to[:, t, :], source[:, t, :], func, scale=rs[:, t:t + 1],
                                              bias=nb[:, t:t + 1])
                        if scaled is not None:
                            last = act.activation(scaled[:, t, :], source[:, t, :], func, scale=rs2[:, t:t + 1],
                                                  bias=nb2[:, t:t + 1])
                    last.then_inc(s_rows[n], 1)
                return stage

            def split_hi(m, source):
                if 2 <= m < NH:
                    which, value = stored(m - 2)
                    act.wait_ge(which, value)
                act.activation(part(m, 0), source, ACT.Copy).then_inc(s_hi, 1)

            def split_mid(m, width):
                act.wait_ge(s_re, m + 1)
                act.activation(part(m, 1), left(m, width), ACT.Copy).then_inc(s_mi, 1)

            def split_rows(name, source, n):
                def stage(j):
                    t0, c = TILES[j][0], len(TILES[j])
                    act.wait_ge(s_rows[n], j + 1)
                    split_hi(SPLIT0[name] + j, source[:, t0:t0 + c, :])
                    split_mid(SPLIT0[name] + j, D * c)
                return stage

            act.wait_ge(s_x, 32)
            pipeline(root(0), rows(0, h, ACT.Relu, x))
            act.wait_ge(s_wt, 16 * 19)
            act.activation(wcp[:, 0, :], wcf[:, :], ACT.Copy).then_inc(s_wcp, 1)
            act.wait_ge(s_wcp, 2)
            act.activation(wcp[:, 1, :], wcr[:, :], ACT.Copy).then_inc(s_wcp, 1)
            act.wait_ge(s_wcp, 4)
            act.activation(wcp[:, 2, :], wcr[:, :], ACT.Copy).then_inc(s_wcp, 1)
            act.wait_ge(s_prepT, 3)
            for j in range(NC):
                act.wait_ge(mm["T0"], j + 1)
                c = 128 * len(TILES[j])
                act.activation(hT[:, 512 * j:512 * j + c], bank(j, c), ACT.Copy).then_inc(ev["T0"], 1)
            for m, tiles in enumerate(HALVES):
                act.wait_ge(ev["PQ"], m + 1)
                n = len(tiles)
                split_hi(m, pq[:, m % 2, 0:n, :, :])
                split_mid(m, 2 * D * n)

            act.wait_ge(s_pass, 1)
            P = act.value_load(passes_i[0:1, 0:1], min_val=1, max_val=MAXP)

            def split_hi_mid(s):
                with act.Fori(0, P) as w:
                    with act.Fori(0, NI) as i:
                        u0 = split_count(s, w, i, P)
                        n0 = (w * NI + i) * ITER

                        def hi(k):
                            if s == L0:
                                act.wait_ge(s_pre, u0 + k + 1 + ITER)
                                act.wait_ge(s_rre, u0 + k + 1)
                                act.activation(R[:, k % 2, :, :],
                                               bank(7).rearrange("p (c d) -> p c d", d=D), ACT.Relu).then_inc(s_R, 1)
                            act.wait_ge(s_R, u0 + k + 2)
                            act.wait_ge(s_seg[s], n0 + k + ITER - 1)
                            act.activation(RP[:, k % 2, 0, :, :], R[:, k % 2, :, :], ACT.Copy).then_inc(s_rhi, 1)

                        def mid(k):
                            act.wait_ge(s_rre, u0 + k + 3)
                            act.activation(RP[:, k % 2, 1, :, :], R_left[:, k % 2, :, :], ACT.Copy)\
                                .then_inc(s_rmi, 1)

                        def read_counts(k, r):
                            n = (n0 + k) * 2 + r
                            act.wait_ge(s_cmm, n + 3)
                            if r == 0:
                                act.wait_ge(s_cst[k % 2], (w * NI + i) * 32 + 16 * (k // 2) + 16)
                            act.activation(cnt_out[:, k % 2, r, :], bank(7, CW), ACT.Copy).then_inc(s_cev, 1)

                        def store_counts(k):
                            act.wait_ge(s_cev, (n0 + k) * 2 + 3)
                            act.dma_start(cnt_tab[bass.ds(i * ITER + k, 1), :, :].rearrange("q p c -> p (q c)"),
                                          cnt_out[:, k % 2, :, :].rearrange("p r c -> p (r c)"))\
                                .then_inc(s_cst[k % 2], 16)

                        if s == L2:
                            for k in range(ITER):
                                hi(k)
                                mid(k)
                        else:
                            hi(0)
                            mid(0)
                            for k in range(ITER):
                                if k + 1 < ITER:
                                    hi(k + 1)
                                read_counts(k, 0)
                                if k + 1 < ITER:
                                    mid(k + 1)
                                read_counts(k, 1)
                                store_counts(k)

            split_hi_mid(L0)

            def read_acc(s, dense=False):
                def stage(j):
                    if dense:
                        act.wait_ge(s_den[s], j + 1)
                    elif j == 0:
                        act.wait_ge(s_seg[s], P * NQ + ITER)
                    c = 128 * len(TILES[j])
                    if s == L0 and j == NC - 1:
                        act.wait_ge(ev["DG"], 1)
                    act.activation(ST[:, 512 * j:512 * j + c], bank(j, c), ACT.Copy).then_inc(s_acc, 1)
                return stage

            pipeline(read_acc(L0))
            act.wait_ge(s_degs, 1)
            act.activation(dv[:, T0_, :], dv[:, T0_, :], ACT.Sqrt).then_inc(s_degs, 1)
            act.activation(dv[:, T1_, :], dv[:, T1_, :], ACT.Sqrt).then_inc(s_degs, 1)
            for j in range(NC):
                act.wait_ge(mm["R"], j + 1)
                c = 128 * len(TILES[j])
                act.activation(r_bc[:, 512 * j:512 * j + c], bank(j, c), ACT.Copy).then_inc(ev["R"], 1)
            for j in range(NC):
                act.wait_ge(mm["U"], j + 1)
                c = 128 * len(TILES[j])
                act.activation(ST[:, 512 * j:512 * j + c], bank(j, c), ACT.Relu, bias=cols[:, 1:2])\
                    .then_inc(ev["U"], 1)
            pipeline(root(1), rows(1, h, ACT.Identity, h), lambda j: None, root(2), rows(2, h, ACT.Relu, x),
                     split_rows("H1", h, 2))
            act.wait_ge(s_flag, 1)
            flag = act.value_load(flag_i[0:1, 0:1], min_val=0, max_val=1)

            def idle(j):
                pass

            with act.If(flag > 0):
                pipeline(read_acc(L1, dense=True), idle, root(3), rows(3, h, ACT.Relu, x))
            with act.Else():
                pipeline(read_acc(L1))
                pipeline(root(3), rows(3, h, ACT.Relu, x))

            split_hi_mid(L2)
            pipeline(read_acc(L2))
            pipeline(root(4), rows(4, h, ACT.Relu, x, scaled=g3), split_rows("G3", g3, 4))
            own = hT[:, :].rearrange("p (t d) -> p t d", d=D)
            for t in range(NT):
                last = act.activation(own[:, t, :], h[:, t, :], ACT.Copy, scale=dv[:, SELF3, t:t + 1])
            last.then_inc(s_bias, 1)
            with act.If(flag > 0):
                pipeline(read_acc(L3, dense=True))
            with act.Else():
                pipeline(read_acc(L3))

        @block.vector
        def _(dve):
            links = [0]

            def link(ins):
                links[0] += 1
                ins.then_inc(s_dve, 1)
                dve.wait_ge(s_dve, links[0])

            dve.memset(dst_l[QA:NQ, :], PAD_DST).then_inc(s_pad, 1)
            dve.memset(src_l[QA:NQ, :], 0).then_inc(s_pad, 1)
            dve.memset(w_l[QA:NQ, :], 0.0).then_inc(s_pad, 1)
            dve.memset(ea_l[QA:NQ, :], 0.0).then_inc(s_pad, 1)
            dve.memset(x[:, NT - 1, :], 0.0).then_inc(s_pad, 1)
            dve.wait_ge(s_dst, 48)
            link(dve.tensor_copy(dst_f, dst_l))
            dve.tensor_reduce(blk[0:NQ, 0:1], dst_f, AX.X, ALU.min)
            link(dve.tensor_reduce(blk[0:NQ, 1:2], dst_f, AX.X, ALU.max))
            link(dve.tensor_copy(blk_i[0:NQ, :], blk[0:NQ, :]))
            link(dve.tensor_single_scalar(blk_s[0:NQ, :], blk_i[0:NQ, :], 6, ALU.arith_shift_right))
            dve.tensor_scalar(base64[0:NQ, :], blk_s[0:NQ, 0:1], float(WB), None, ALU.mult).then_inc(s_prep, 1)
            dve.wait_ge(s_prep, 1)
            dve.tensor_scalar(dst_r, dst_f, base64[0:NQ, 0:1], None, ALU.subtract).then_inc(s_prep, 1)
            dve.wait_ge(s_src, 96)
            dve.tensor_copy(src_f, src_l).then_inc(s_prep, 1)
            link(dve.tensor_single_scalar(hi_i, src_l, 7, ALU.arith_shift_right))
            dve.tensor_reduce(cmax[0:NQ, :], dst_f.rearrange("p (c e) -> p c e", c=4), AX.X, ALU.max)
            link(dve.tensor_copy(hi_f, hi_i))
            dve.scalar_tensor_tensor(key_f, dst_f, 32.0, hi_f, ALU.mult, ALU.add)
            dve.wait_ge(s_prep, 3)
            dve.scalar_tensor_tensor(lo_f, hi_f, -128.0, src_f, ALU.mult, ALU.add).then_inc(s_prep, 1)
            dve.wait_ge(s_con, 14)
            for c in range(4):
                last = dve.tensor_scalar(later[0:NQ, c, :], iota_b[0:NQ, :], cmax[0:NQ, c:c + 1], None, ALU.is_gt)
            last.then_inc(s_prep, 1)
            dve.tensor_copy(iota_m[:, :], iota_i[:, :, :].rearrange("p h w -> p (h w)")).then_inc(s_prep, 1)

            def variance(n, source):
                def stage(j):
                    for t in TILES[j]:
                        last = dve.bn_stats(bn[:, t, :], source[:, t, :])
                    link(last)
                    for t in TILES[j]:
                        last = dve.bn_aggr(mv[:, t, :], bn[:, t, :])
                    last.then_inc(s_var[n], 1)
                return stage

            def norm(n, by=None, by2=None):
                def stage(j):
                    ts = slice(TILES[j][0], TILES[j][-1] + 1)
                    dve.wait_ge(s_root[n], j + 1)
                    link(dve.reciprocal(rs[:, ts], sd[:, ts]))
                    if by is not None:
                        link(dve.tensor_tensor(rs[:, ts], rs[:, ts], dv[:, by, ts], ALU.mult))
                    last = dve.scalar_tensor_tensor(nb[:, ts], mv[:, ts, 0], -1.0, rs[:, ts], ALU.mult, ALU.mult)
                    if by2 is not None:
                        link(last)
                        dve.tensor_tensor(rs2[:, ts], rs[:, ts], dv[:, by2, ts], ALU.mult)
                        last = dve.tensor_tensor(nb2[:, ts], nb[:, ts], dv[:, by2, ts], ALU.mult)
                    last.then_inc(s_norm[n], 1)
                return stage

            dve.wait_ge(s_x, 32)
            pipeline(variance(0, x), norm(0))

            dve.wait_ge(s_row, 16)
            link(dve.tensor_copy(row_f[:, :, :], row_i[:, :, :]))
            link(dve.tensor_tensor(far[:, :], row_f[:, :, 1], row_f[:, :, 0], ALU.subtract))
            link(dve.tensor_reduce(far1[:, :], far[:, :], AX.X, ALU.max))
            link(dve.tensor_copy(far_i[:, :], far1[:, :]))
            link(dve.tensor_single_scalar(far_s[:, :], far_i[:, :], 1, ALU.arith_shift_right))
            dve.tensor_scalar(passes_i[:, :], far_s[:, :], 1.0, None, ALU.add).then_inc(s_pass, 1)

            dve.wait_ge(s_c0, 1)
            link(dve.tensor_tensor(slots[:, :, :],
                                   bank(3, NCB).rearrange("p (b j) -> p b j", j=1).to_broadcast([128, NCB, CT]),
                                   iota_c[:, :].rearrange("p (a j) -> p a j", a=1).to_broadcast([128, NCB, CT]),
                                   ALU.add))
            link(dve.tensor_scalar(base64[:, :], pio[:, :], 4.0, None, ALU.mult))
            for c in range(4):
                last = dve.tensor_scalar(sel[0:NQ, c, :], slots[0:NQ, :, :].rearrange("p b j -> p (b j)"),
                                         -float(c), base64[0:NQ, 0:1], ALU.add, ALU.is_equal)
            last.then_inc(s_slot, 1)

            dve.wait_ge(s_wcp, 1)
            dve.tensor_tensor(wcr[:, :], wcf[:, :], wcp[:, 0, :], ALU.subtract).then_inc(s_wcp, 1)
            dve.wait_ge(s_wcp, 3)
            dve.tensor_tensor(wcr[:, :], wcr[:, :], wcp[:, 1, :], ALU.subtract).then_inc(s_wcp, 1)

            for n, (to, j) in enumerate(((dstT, 1), (idx, 0), (wT, 2))):
                dve.wait_ge(s_prepT, n + 1)
                dve.tensor_copy(to[:, :, :].rearrange("p q c -> p c q"),
                                bank(j, 4 * NQ).rearrange("p (c q) -> p c q", c=4)).then_inc(s_prepE, 1)
            dve.wait_ge(s_prepE, 3)
            dve.wait_ge(s_con, 14)
            link(dve.tensor_copy(wq[:, :, :, 1], wT[:, :, :]))
            link(dve.tensor_tensor(wr[:, 0, :, :], wT[:, :, :], wq[:, :, :, 1], ALU.subtract))
            link(dve.tensor_copy(wq[:, :, :, 2], wr[:, 0, :, :]))
            link(dve.tensor_tensor(wr[:, 1, :, :], wr[:, 0, :, :], wq[:, :, :, 2], ALU.subtract))
            link(dve.tensor_copy(wq[:, :, :, 3], wr[:, 1, :, :]))

            dve.wait_ge(s_wt, 16 * 19)
            for m, tiles in enumerate(HALVES):
                n = len(tiles)
                dve.wait_ge(mm["PQ"], m + 1)
                if m >= 2:
                    dve.wait_ge(s_re, m - 1)
                dve.tensor_tensor(pq[:, m % 2, 0:n, :, :],
                                  bank(m % 8, 256 * n).rearrange("p (t w d) -> p t w d", w=2, d=D),
                                  bc[:, B_P:B_Q + 1, :].rearrange("p (a w) d -> p a w d", a=1)
                                  .to_broadcast([128, n, 2, D]), ALU.add).then_inc(ev["PQ"], 1)

            dve.wait_ge(s_K4, 1)
            link(dve.tensor_scalar(slots[:, :, 0], iota_b[:, :], 32.0, None, ALU.mult))
            for n in range(2):
                half = slice(n * (NCB // 2), (n + 1) * (NCB // 2))
                dve.tensor_tensor(K4[:, half, :],
                                  bank(n, NCB * CT // 2).rearrange("p (b j) -> p b j", j=CT),
                                  slots[:, half, 0:1].to_broadcast([128, NCB // 2, CT]), ALU.subtract)
                last = dve.tensor_copy(lo4[:, half, :],
                                       bank(2 + n, NCB * CT // 2).rearrange("p (b j) -> p b j", j=CT))
            last.then_inc(s_key, 1)
            dve.wait_ge(s_key, 1)
            link(dve.tensor_scalar(inb[:, :, :], K4[:, :, :], 32.0 * CB, None, ALU.is_lt))
            link(dve.scalar_tensor_tensor(inb[:, :, :], K4[:, :, :], 0.0, inb[:, :, :], ALU.is_ge, ALU.mult))
            link(dve.tensor_reduce(whole[:, 0:1], inb[:, :, :], AX.XY, ALU.add))

            P = dve.value_load(passes_i[0:1, 0:1], min_val=1, max_val=MAXP)

            def start_tables(s):
                dve.tensor_scalar(tab_f[:, :], row_f[:, :, 0], -2.0, None, ALU.add)
                dve.tensor_scalar(pio_w[:, :], pio[:, :], -128.0, None, ALU.add)
                dve.tensor_scalar(iota_w[:, :], iota[:, :], -128.0, None, ALU.add).then_inc(s_tab[s], 1)
                dve.wait_ge(s_tab[s], 1)

            def move_tables(s, w):
                dve.wait_ge(s_seg[s], w * NQ + ITER)
                dve.tensor_scalar(tab_f[:, :], tab_f[:, :], 2.0, float(NB - 1), ALU.add, ALU.min)\
                    .then_inc(s_tab[s], 1)
                dve.tensor_scalar(pio_w[:, :], pio_w[:, :], 128.0, None, ALU.add).then_inc(s_tab[s], 1)
                dve.tensor_scalar(iota_w[:, :], iota_w[:, :], 128.0, None, ALU.add).then_inc(s_tab[s], 1)
                dve.wait_ge(s_tab[s], w * 4 + 4)
                dve.tensor_copy(tab_i[:, :], tab_f[:, :]).then_inc(s_tab[s], 1)

            def onehot(s, w, i, k):
                dve.wait_ge(s_seg[s], (w * NI + i) * ITER + k + 1)
                dve.tensor_tensor(oh[:, k, :, :],
                                  iota_w[:, :].rearrange("p (a n) -> p a n", a=1).to_broadcast([128, 4, 128]),
                                  dstT[:, bass.ds(i * ITER + k, 1), :].rearrange("p a (c b) -> p (a c) b", b=1)
                                  .to_broadcast([128, 4, 128]), ALU.is_equal).then_inc(s_oh[s], 1)

            def row_rest(u, k):
                dve.wait_ge(s_rhi, u + 1)
                dve.tensor_tensor(R_left[:, k % 2, :, :], R[:, k % 2, :, :], RP[:, k % 2, 0, :, :], ALU.subtract)\
                    .then_inc(s_rre, 1)

            def row_lo(u, k):
                dve.wait_ge(s_rmi, u + 1)
                dve.tensor_tensor(RP[:, k % 2, 2, :, :], R_left[:, k % 2, :, :], RP[:, k % 2, 1, :, :],
                                  ALU.subtract).then_inc(s_rlo, 1)

            start_tables(L0)
            with dve.Fori(0, P) as w:
                move_tables(L0, w)
                with dve.Fori(0, NI) as i:
                    steps = w * NI + i

                    def build(k):
                        onehot(L0, w, i, k)
                        dve.wait_ge(s_rl[k], (steps + 1) * 32)
                        dve.tensor_scalar(sT[:, k, :], row_bc[:, k, :], pio_w[:, 0:1], None, ALU.is_equal)\
                            .then_inc(s_sT, 1)

                    def count_operands(k, r):
                        n = (steps * ITER + k) * 2 + r
                        dve.wait_ge(s_cmm, n + 1)
                        b = i * (2 * ITER) + 2 * k + r
                        for j in range(CT):
                            dve.tensor_scalar(mov[:, r, j, :], iota_m[:, :],
                                              K4[:, bass.ds(b, 1), j:j + 1].rearrange("p a j -> p (a j)"), None,
                                              ALU.is_equal)
                        dve.tensor_tensor(sta[:, r, :, :],
                                          iota[:, :].rearrange("p (a n) -> p a n", a=1).to_broadcast([128, CT, 128]),
                                          lo4[:, bass.ds(b, 1), :].rearrange("p a (c b) -> p (a c) b", b=1)
                                          .to_broadcast([128, CT, 128]), ALU.is_equal).then_inc(s_cop, 1)

                    build(0)
                    build(1)
                    row_rest(steps * ITER, 0)
                    row_lo(steps * ITER, 0)
                    for k in range(ITER):
                        count_operands(k, 0)
                        if k + 1 < ITER:
                            row_rest(steps * ITER + k + 1, k + 1)
                        count_operands(k, 1)
                        if k + 1 < ITER:
                            row_lo(steps * ITER + k + 1, k + 1)
                        if k + 2 < ITER:
                            build(k + 2)

            dve.wait_ge(s_seg[L0], P * NQ + ITER)
            link(dve.tensor_copy(degs[:, 1:1 + NB, :],
                                 ps[:, DEG:DEG + 4 * NB].rearrange("p (b f) -> p b f", f=4)))
            dve.tensor_copy(deg2[:, 0, 0:NB + 1], degs[:, :, 0])
            link(dve.tensor_tensor(deg2[:, 1, 0:NB + 1], degs[:, :, 2], degs[:, :, 3], ALU.add))
            link(dve.tensor_tensor(deg2[:, 1, 0:NB + 1], deg2[:, 1, 0:NB + 1], degs[:, :, 1], ALU.add))
            dve.memset(deg2[:, :, NB + 1:2 * NT + 1], 0.0).then_inc(ev["DG"], 1)
            dve.wait_ge(mm["DG"], 1)
            link(dve.tensor_copy(cnt[:, :, :], ps[:, PRE:PRE + 2 * NT].rearrange("p (f t) -> p f t", f=2)))
            link(dve.tensor_scalar(many[:, :], cnt[:, 0, :], 256.0, None, ALU.is_gt))
            dve.tensor_reduce(whole[:, 1:2], many[:, :], AX.X, ALU.add).then_inc(ev["DG"], 1)
            link(dve.tensor_scalar(dv[:, INV_CNT, :], cnt[:, 0, :], 1.0, None, ALU.max))
            dve.reciprocal(dv[:, INV_CNT, :], dv[:, INV_CNT, :])
            dve.tensor_scalar(dv[:, HAS, :], cnt[:, 0, :], 1.0, None, ALU.min).then_inc(ev["DG"], 1)
            dve.tensor_scalar(dv[:, T1_, :], cnt[:, 0, :], 1.0, None, ALU.add)
            link(dve.tensor_scalar(dv[:, SELF3, :], cnt[:, 1, :], 1.0, None, ALU.add))
            dve.tensor_scalar(dv[:, DINV2, :], dv[:, SELF3, :], 0.0, None, ALU.is_gt)
            dve.tensor_scalar(dv[:, T0_, :], dv[:, SELF3, :], TINY, None, ALU.max).then_inc(s_degs, 1)
            dve.wait_ge(s_degs, 3)
            dve.reciprocal(dv[:, T0_, :], dv[:, T0_, :])
            link(dve.reciprocal(dv[:, DINV3, :], dv[:, T1_, :]))
            dve.tensor_tensor(dv[:, DINV2, :], dv[:, DINV2, :], dv[:, T0_, :], ALU.mult)
            link(dve.tensor_scalar(dv[:, D09, :], dv[:, DINV3, :], 0.9, None, ALU.mult))
            link(dve.tensor_tensor(dv[:, SELF3, :], dv[:, D09, :], dv[:, DINV3, :], ALU.mult))
            link(dve.tensor_scalar(dv[:, SELF3, :], dv[:, SELF3, :], 0.1, None, ALU.add))
            dve.wait_ge(mm["DG"], 2)
            link(dve.tensor_copy(whole1[:, 0:2], ps[0:1, PRE + 128:PRE + 130]))
            dve.tensor_scalar(whole1[:, 0:1], whole1[:, 0:1], float(NQ * QE), None, ALU.is_equal)
            link(dve.tensor_scalar(whole1[:, 1:2], whole1[:, 1:2], 0.0, None, ALU.is_equal))
            link(dve.tensor_tensor(whole1[:, 2:3], whole1[:, 0:1], whole1[:, 1:2], ALU.mult))
            link(dve.tensor_scalar(whole1[:, 3:4], far1[:, :], 2.0, None, ALU.is_lt))
            dve.tensor_tensor(flag_i[:, :], whole1[:, 2:3], whole1[:, 3:4], ALU.mult).then_inc(s_flag, 1)
            for j in range(NC):
                dve.wait_ge(s_acc, j + 1)
                dve.wait_ge(mm["B"], j + 1)
                c = 128 * len(TILES[j])
                dve.tensor_tensor(ST[:, 512 * j:512 * j + c], ST[:, 512 * j:512 * j + c], bank(j, c), ALU.mult)\
                    .then_inc(ev["B"], 1)
            for j in range(NC):
                dve.wait_ge(mm["A"], j + 1)
                c = 128 * len(TILES[j])
                dve.scalar_tensor_tensor(aggT[:, 512 * j:512 * j + c], r_bc[:, 512 * j:512 * j + c], cols[:, 0:1],
                                         bank(j, c), ALU.mult, ALU.add).then_inc(ev["A"], 1)

            def tiles_of(a, j):
                return a[:, TILES[j][0]:TILES[j][-1] + 1, :]

            def bias_of(slot, n):
                return bc[:, slot:slot + 1, :].to_broadcast([128, n, D])

            def bank_of(j):
                return bank(j, 128 * len(TILES[j])).rearrange("p (t d) -> p t d", d=D)

            def update(j):
                dve.wait_ge(mm["V"], j + 1)
                dve.tensor_tensor(tiles_of(h, j), bank_of(j), tiles_of(h, j), ALU.add).then_inc(ev["V"], 1)
                dve.wait_ge(ev["V"], j + 1)
                link(dve.tensor_tensor(tiles_of(h, j), tiles_of(h, j), bias_of(B_U2, len(TILES[j])), ALU.add))

            def residual(j):
                n = len(TILES[j])
                dve.wait_ge(s_rows[1], j + 1)
                link(dve.tensor_tensor(tiles_of(h, j), tiles_of(h, j), bias_of(B_GA, n), ALU.mult))
                link(dve.tensor_tensor(tiles_of(x, j), tiles_of(x, j), bias_of(B_BE, n), ALU.add))
                link(dve.tensor_tensor(tiles_of(x, j), tiles_of(x, j), tiles_of(h, j), ALU.add))

            def both(*stages):
                def stage(j):
                    for s in stages:
                        s(j)
                return stage

            pipeline(both(update, variance(1, h)), norm(1), both(residual, variance(2, x)), norm(2))
            for j in range(NC):
                dve.wait_ge(mm["T1"], j + 1)
                c = 128 * len(TILES[j])
                dve.tensor_copy(hT[:, 512 * j:512 * j + c], bank(j, c)).then_inc(ev["T1"], 1)

            def plain_sweep(s):
                start_tables(s)
                with dve.Fori(0, P) as w:
                    move_tables(s, w)
                    with dve.Fori(0, NI) as i:
                        for k in range(ITER):
                            onehot(s, w, i, k)

            def add_bias(*slots):
                for slot in slots:
                    link(dve.tensor_tensor(x[:, :, :], x[:, :, :], bias_of(slot, NT), ALU.add))

            add_bias(B_L1, B_L1B)
            flag = dve.value_load(flag_i[0:1, 0:1], min_val=0, max_val=1)
            with dve.If(flag > 0):
                dve.wait_ge(s_den[L1], 1)
            with dve.Else():
                plain_sweep(L1)

            def out1(j):
                dve.wait_ge(mm["O1"], j + 1)
                dve.tensor_tensor(tiles_of(x, j), tiles_of(x, j), bank_of(j), ALU.add).then_inc(ev["O1"], 1)
                dve.wait_ge(ev["O1"], j + 1)

            pipeline(both(out1, variance(3, x)), norm(3, by=DINV2))
            for j in range(NC):
                dve.wait_ge(mm["T2"], j + 1)
                c = 128 * len(TILES[j])
                dve.tensor_copy(hT[:, 512 * j:512 * j + c], bank(j, c)).then_inc(ev["T2"], 1)
            add_bias(B_L2)

            start_tables(L2)
            with dve.Fori(0, P) as w:
                move_tables(L2, w)
                with dve.Fori(0, NI) as i:
                    steps = w * NI + i
                    split0 = split_count(L2, w, i, P)

                    def weigh(k):
                        dve.wait_ge(s_gat[L2][k], (steps + 1) * 64)
                        dve.wait_ge(s_rre, split0 + k + 1)
                        dve.tensor_tensor(R[:, k % 2, :, :], G[:, k, :, 0:2 * D].bitcast(fp32),
                                          wT[:, bass.ds(i * ITER + k, 1), :].rearrange("p a (c b) -> p (a c) b", b=1)
                                          .to_broadcast([128, 4, D]), ALU.mult).then_inc(s_R, 1)

                    onehot(L2, w, i, 0)
                    weigh(0)
                    for k in range(ITER):
                        row_rest(split0 + k, k)
                        if k + 1 < ITER:
                            onehot(L2, w, i, k + 1)
                            weigh(k + 1)
                        row_lo(split0 + k, k)

            def out2(j):
                dve.wait_ge(mm["O2"], j + 1)
                for n, t in enumerate(TILES[j]):
                    last = dve.scalar_tensor_tensor(x[:, t, :], bank(j)[:, 128 * n:128 * n + 128],
                                                    dv[:, DINV2, t:t + 1], x[:, t, :], ALU.mult, ALU.add)
                last.then_inc(ev["O2"], 1)
                dve.wait_ge(ev["O2"], j + 1)

            pipeline(both(out2, variance(4, x)), norm(4, by2=DINV3))
            dve.wait_ge(s_rows[4], NC)
            link(dve.tensor_tensor(x[:, :, :], x[:, :, :], h[:, :, :], ALU.add))
            with dve.If(flag > 0):
                dve.wait_ge(s_den[L3], 1)
            with dve.Else():
                plain_sweep(L3)
            own = hT[:, :].rearrange("p (t d) -> p t d", d=D)
            dve.wait_ge(s_bias, 1)
            for j in range(NC):
                dve.wait_ge(mm["O3"], j + 1)
                for n, t in enumerate(TILES[j]):
                    last = dve.scalar_tensor_tensor(own[:, t, :], bank(j)[:, 128 * n:128 * n + 128],
                                                    dv[:, D09, t:t + 1], own[:, t, :], ALU.mult, ALU.add)
                link(last)
                dve.scalar_tensor_tensor(tiles_of(h, j), tiles_of(own, j), 0.0, tiles_of(x, j), ALU.max, ALU.add)\
                    .then_inc(s_fin, 1)

        @block.tensor
        def _(pe):
            pe.wait_ge(s_con, 14)
            for n, (array, j, ready, value) in enumerate(((dst_r, 1, s_prep, 2), (src_f, 0, s_prep, 3),
                                                          (w_l, 2, s_src, 96))):
                pe.wait_ge(ready, value)
                for c in range(4):
                    last = pe.transpose(ps[:, 512 * j + NQ * c:512 * j + NQ * (c + 1)],
                                        array[:, 128 * c:128 * c + 128], ident[0:NQ, 0:NQ])
                last.then_inc(s_prepT, 1)
            pe.wait_ge(s_prep, 6)
            for c in range(4):
                last = pe.matmul(bank(3, NCB), onesb[0:NQ, :], later[0:NQ, c, :], start=c == 0, stop=c == 3)
            last.then_inc(s_c0, 1)

            def transposes(stage, source, ready, chunks=range(NC)):
                for j in chunks:
                    ready(j)
                    for n, t in enumerate(TILES[j]):
                        last = pe.transpose(ps[:, 512 * j + 128 * n:512 * j + 128 * n + 128], source[:, t, :],
                                            ident[:, :])
                    last.then_inc(mm[stage], 1)

            def h0_ready(j):
                pe.wait_ge(s_rows[0], j + 1)
                if j == 0:
                    pe.wait_ge(s_prepE, 3)
                    pe.wait_ge(s_slot, 1)
            transposes("T0", h, h0_ready)

            pe.wait_ge(s_wt, 16 * 19)
            pe.wait_ge(ev["T0"], NC)
            for m, tiles in enumerate(HALVES):
                if m >= 8:
                    pe.wait_ge(ev["PQ"], m - 7)
                for n, t in enumerate(tiles):
                    b = 512 * (m % 8) + 256 * n
                    last = pe.matmul(ps[:, b:b + 256], hT[:, 128 * t:128 * t + 128],
                                     wab[:, :, :].rearrange("p w d -> p (w d)"), start=True, stop=True)
                last.then_inc(mm["PQ"], 1)

            pe.wait_ge(s_pass, 1)
            P = pe.value_load(passes_i[0:1, 0:1], min_val=1, max_val=MAXP)

            def zero_acc():
                for b in range(ACC_BANKS):
                    last = pe.matmul(bank(b), zerob[:, 0:128], zerob[:, :], start=True, stop=True)
                last.then_inc(s_zero, 1)

            def add_to(col, width, lhsT, rhs):
                return pe.matmul(ps[:, bass.ds(col, width)], lhsT, rhs, start=False, stop=True,
                                 skip_group_check=True)

            def sum_chunk(b, rows, k, c):
                for half in range(2):
                    for a in range(PARTS):
                        last = add_to(b * WB + WB * half, WB, rows(a), oh[:, k, c, WB * half:WB * half + WB])
                return last

            pe.wait_ge(ev["PQ"], NH)
            for n, array in enumerate((key_f, lo_f)):
                for half in range(2):
                    w = NCB * CT // 2
                    for c in range(4):
                        last = pe.matmul(bank(2 * n + half, w), array[:, 128 * c:128 * c + 128],
                                         sel[0:NQ, c, w * half:w * half + w], start=c == 0, stop=c == 3)
            last.then_inc(s_K4, 1)
            pe.wait_ge(s_key, 1)
            zero_acc()
            for s in range(4):
                pe.sem_inc(s_seg[s], ITER)
            pe.sem_inc(s_cmm, 2)
            pe.sem_inc(s_cev, 1)
            pe.sem_inc(s_pre, ITER)
            pe.sem_inc(s_R, 1)
            pe.sem_inc(s_rre, 2)
            pe.wait_ge(s_qw, 32)
            pe.wait_ge(s_wc18, 16 * 2 * PARTS)

            with pe.Fori(0, P) as w:
                with pe.Fori(0, NI) as i:
                    pe.wait_ge(s_tab[L0], w * 4 + 5)
                    steps = w * NI + i
                    quads = steps * ITER
                    base = {}

                    def pre(k):
                        base[k] = pe.value_load(tab_i[0:1, bass.ds(i * ITER + k, 1)], min_val=0, max_val=NB - 1)
                        pe.wait_ge(s_sT, quads + k + 1)
                        pe.wait_ge(s_rl[k], (steps + 1) * 32)
                        pe.wait_ge(s_gat[L0][k], (steps + 1) * 64)
                        if k != 1:
                            pe.wait_ge(s_cev, 2 * (quads + max(k - 1, 0)) + 1)
                        pe.wait_ge(s_R, quads + k + 1)
                        for c in range(4):
                            to = ps[:, PRE + 128 * c:PRE + 128 * c + 128]
                            edges = slice(128 * c, 128 * c + 128)
                            pe.matmul(to, ea18[:, k, edges], wc18[:, :], start=True, stop=False)
                            for a in range(PARTS):
                                pe.matmul(to, identb[:, :], G[:, k, c, D * a:D * a + D], start=False, stop=False)
                            for a in range(PARTS):
                                last = pe.matmul(to, sT[:, k, edges],
                                                 Qw[:, bass.ds(base[k], 1), D * a:D * a + D]
                                                 .rearrange("p a d -> p (a d)"),
                                                 start=False, stop=a == PARTS - 1)
                        last.then_inc(s_pre, 1)

                    def seg(k, chunks):
                        if chunks[0] == 0:
                            pe.wait_ge(s_oh[L0], quads + k + 1)
                            pe.wait_ge(s_rlo, quads + k + 1)
                        for c in chunks:
                            add_to(base[k] * 4 + DEG, 4, oh[:, k, c, :],
                                   wq[:, bass.ds(i * ITER + k, 1), c, :].rearrange("p a f -> p (a f)"))
                            last = sum_chunk(base[k], lambda a: RP[:, k % 2, a, c, :], k, c)
                        if chunks[-1] == 3:
                            last.then_inc(s_seg[L0], 1)

                    def count(k, r):
                        n = (quads + k) * 2 + r
                        pe.wait_ge(s_cop, n + 1)
                        pe.wait_ge(s_R, quads + min(k + 1, ITER - 1) + 2)
                        pe.wait_ge(s_cev, n + 1)
                        for j in range(CT):
                            last = pe.matmul(bank(7, CW), sta[:, r, j, :], mov[:, r, j, :],
                                             start=j == 0, stop=j == CT - 1)
                        last.then_inc(s_cmm, 1)

                    pre(0)
                    for k in range(ITER):
                        if k + 1 < ITER:
                            pre(k + 1)
                        seg(k, (0, 1))
                        count(k, 0)
                        seg(k, (2,))
                        count(k, 1)
                        seg(k, (3,))

            pe.wait_ge(ev["DG"], 1)
            pe.wait_ge(s_cev, P * (2 * NQ) + 1)
            for f in range(2):
                to = ps[:, PRE + NT * f:PRE + NT * f + NT]
                pe.matmul(to, shift[:, WB:WB + 128], deg2[:, f, 1:2 * NT:2], start=True, stop=False)
                pe.matmul(to, shift[:, 128:256], deg2[:, f, 0:2 * NT - 1:2], start=False, stop=False)
                last = pe.matmul(to, shift[:, 0:128], deg2[:, f, 2:2 * NT + 1:2], start=False, stop=True)
            last.then_inc(mm["DG"], 1)
            pe.wait_ge(ev["DG"], 2)
            pe.matmul(ps[0:1, PRE + 128:PRE + 130], ones[:, :], whole[:, :], start=True, stop=True)\
                .then_inc(mm["DG"], 1)
            pe.wait_ge(ev["DG"], 3)
            for stage, slot in (("B", INV_CNT), ("R", HAS)):
                for j, tiles in enumerate(TILES):
                    if stage == "B":
                        pe.wait_ge(s_acc, j + 1)
                    else:
                        pe.wait_ge(ev["B"], j + 1)
                    for n, t in enumerate(tiles):
                        last = pe.matmul(ps[:, 512 * j + 128 * n:512 * j + 128 * n + 128],
                                         dv[:, slot, t:t + 1].to_broadcast([128, 128]), ident[:, :],
                                         start=True, stop=True)
                    last.then_inc(mm[stage], 1)
            for j, tiles in enumerate(TILES):
                pe.wait_ge(ev["R"], j + 1)
                c = 128 * len(tiles)
                pe.matmul(bank(j, c), w_m2[:, :], ST[:, 512 * j:512 * j + c], start=True, stop=True)\
                    .then_inc(mm["A"], 1)
            for j, tiles in enumerate(TILES):
                pe.wait_ge(ev["A"], j + 1)
                c = 128 * len(tiles)
                pe.matmul(bank(j, c), w_u1[:, 0, :], hT[:, 512 * j:512 * j + c], start=True, stop=False)
                pe.matmul(bank(j, c), w_u1[:, 1, :], aggT[:, 512 * j:512 * j + c], start=False, stop=True)\
                    .then_inc(mm["U"], 1)

            def by_node(stage, ready, *products, chunks=range(NC)):
                for j in chunks:
                    ready(j)
                    for n, t in enumerate(TILES[j]):
                        for k, (lhsT, weights) in enumerate(products):
                            last = pe.matmul(ps[:, 512 * j + 128 * n:512 * j + 128 * n + 128],
                                             lhsT[:, 128 * t:128 * t + 128], weights[:, :],
                                             start=k == 0, stop=k == len(products) - 1)
                    last.then_inc(mm[stage], 1)

            by_node("V", lambda j: pe.wait_ge(ev["U"], j + 1), (ST, w_u2))
            def h1_ready(j):
                pe.wait_ge(s_rows[2], j + 1)
            transposes("T1", h, h1_ready)
            pe.wait_ge(ev["T1"], NC)

            def plain_sweep(s):
                zero_acc()
                with pe.Fori(0, P) as w:
                    with pe.Fori(0, NI) as i:
                        pe.wait_ge(s_tab[s], w * 4 + 5)
                        steps = w * NI + i
                        for k in range(ITER):
                            b = pe.value_load(tab_i[0:1, bass.ds(i * ITER + k, 1)], min_val=0, max_val=NB - 1)
                            pe.wait_ge(s_oh[s], steps * ITER + k + 1)
                            pe.wait_ge(s_gat[s][k], (steps + 1) * 64)
                            for c in range(4):
                                last = sum_chunk(b, lambda a: G[:, k, c, D * a:D * a + D], k, c)
                            last.then_inc(s_seg[s], 1)

            def dense(s, j):
                c = j + NC * (s // 2)
                n = 4 * len(TILES[j]) * 2
                pe.wait_ge(s_cld[c % 2], 16 * (c // 2 + 1))
                block_counts = counts[:, c % 2, 0:n * CW].rearrange("p (b h w) -> p h b w", h=NT, w=CB)
                for a in range(PARTS):
                    for t in range(NT):
                        last = pe.matmul(bank(j, n * CB), Hp[:, t, a, :], block_counts[:, t, :, :],
                                         start=a == 0 and t == 0, stop=a == PARTS - 1 and t == NT - 1)
                last.then_inc(s_den[s], 1)

            def acc_ready(s):
                return lambda j: pe.wait_ge(s_acc, s * NC + j + 1)

            pe.wait_ge(s_flag, 1)
            flag = pe.value_load(flag_i[0:1, 0:1], min_val=0, max_val=1)
            with pe.If(flag > 0):
                pe.wait_ge(s_lo, SPLIT0["H1"] + NC)
                for j in range(NC):
                    dense(L1, j)
                    if j:
                        by_node("O1", acc_ready(L1), (hT, w_11), (ST, w_12), chunks=[j - 1])
                by_node("O1", acc_ready(L1), (hT, w_11), (ST, w_12), chunks=[NC - 1])
            with pe.Else():
                plain_sweep(L1)
                by_node("O1", acc_ready(L1), (hT, w_11), (ST, w_12))

            def g2_ready(j):
                pe.wait_ge(s_rows[3], j + 1)
                pe.wait_ge(ev["O1"], j + 1)
            transposes("T2", h, g2_ready)
            pe.wait_ge(ev["T2"], NC)

            zero_acc()
            with pe.Fori(0, P) as w:
                with pe.Fori(0, NI) as i:
                    pe.wait_ge(s_tab[L2], w * 4 + 5)
                    steps = w * NI + i
                    split0 = split_count(L2, w, i, P)
                    for k in range(ITER):
                        b = pe.value_load(tab_i[0:1, bass.ds(i * ITER + k, 1)], min_val=0, max_val=NB - 1)
                        pe.wait_ge(s_oh[L2], steps * ITER + k + 1)
                        pe.wait_ge(s_rlo, split0 + k + 1)
                        for c in range(4):
                            last = sum_chunk(b, lambda a: RP[:, k % 2, a, c, :], k, c)
                        last.then_inc(s_seg[L2], 1)
            by_node("O2", acc_ready(L2), (ST, w_3), (hT, w_3))
            pe.wait_ge(ev["O2"], NC)
            sums = ST[:, :].rearrange("p (t d) -> p t d", d=D)
            with pe.If(flag > 0):
                pe.wait_ge(s_lo, SPLIT0["G3"] + NC)
                for j in range(NC):
                    dense(L3, j)
                    if j:
                        transposes("O3", sums, acc_ready(L3), chunks=[j - 1])
                transposes("O3", sums, acc_ready(L3), chunks=[NC - 1])
            with pe.Else():
                plain_sweep(L3)
                transposes("O3", sums, acc_ready(L3))


_INS = ['x', 'src', 'dst', 'edge_attr_2', 'edge_weight', 'L0_gnn_mW1', 'L0_gnn_mb1', 'L0_gnn_mW2', 'L0_gnn_mb2',
        'L0_gnn_uW1', 'L0_gnn_ub1', 'L0_gnn_uW2', 'L0_gnn_ub2', 'L0_gnn_gamma', 'L0_gnn_beta', 'L1_gnn_W1',
        'L1_gnn_b1', 'L1_gnn_W2', 'L1_gnn_b2', 'L2_gnn_W', 'L2_gnn_bias']
_OUT = (3125, 128)


def kernel(**inputs):
    import numpy as _np
    import concourse.bacc as _bacc
    from concourse import mybir as _mybir
    from concourse.bass_utils import run_bass_kernel_spmd as _run

    nc = _bacc.Bacc("TRN2", target_bir_lowering=False, num_devices=1)
    arrays, args = {}, []
    for name in _INS:
        a = _np.ascontiguousarray(inputs[name])
        arrays[f"in_{name}"] = a
        args.append(nc.dram_tensor(f"in_{name}", a.shape, _mybir.dt.from_np(a.dtype), kind="ExternalInput").ap())
    args.append(nc.dram_tensor("out_0", _OUT, _mybir.dt.float32, kind="ExternalOutput").ap())
    gnn_kernel(nc, *args)
    r = _run(nc, [arrays], core_ids=[0])
    return r.results[0]["out_0"]
```

```python
import concourse.bass as bass
from concourse import mybir
from contextlib import ExitStack



def gnn_kernel(nc, x_in, src_in, dst_in, ea_in, ew_in, mW1, mb1, mW2, mb2, uW1, ub1, uW2, ub2,
               gamma, beta, W1, b1, W2, b2, W3, b3, out):
    fp32, bf16 = mybir.dt.float32, mybir.dt.bfloat16
    i32, u32 = mybir.dt.int32, mybir.dt.uint32
    ALU = mybir.AluOpType
    ACT = mybir.ActivationFunctionType
    AX = mybir.AxisListType

    N, D = x_in.shape
    E = src_in.shape[0]
    EPS = 1e-5
    TINY = 2.0 ** -116
    NT = -(-N // 128)
    NP = NT * 128
    NR = N - (NT - 1) * 128
    QE = 512
    NQ = -(-E // QE)
    ITER = 4
    NI = NQ // ITER
    assert NI * ITER == NQ
    QR = E - (NQ - 1) * QE
    QA = NQ // 32 * 32
    WB = 64
    NB = -(-N // WB)
    PAD_DST = NB * WB - 1
    assert N <= PAD_DST < NP
    MAXP = (NB - 1) // 2 + 1
    PARTS = 3
    NC = -(-NT // 4)
    TILES = [list(range(4 * j, min(4 * j + 4, NT))) for j in range(NC)]
    HALVES = [list(range(2 * m, min(2 * m + 2, NT))) for m in range(-(-NT // 2))]
    ACC_BANKS = -(-NB * WB // 512)
    DEG = 512 * (ACC_BANKS - 1) + 128
    assert NB * WB <= DEG and DEG + 4 * NB <= 512 * ACC_BANKS and ACC_BANKS < 8
    PRE = 7 * 512
    CB = 16
    CT = 4
    NCB = 2 * NQ
    assert NCB * CB >= NP and NT * CB <= 512 and NCB * CT % 2 == 0 and NT < 32
    CW = NT * CB
    CQ = 512 // (2 * CB)

    P_tab = nc.dram_tensor("p_parts", [NP, PARTS * D], bf16).ap()
    Q_tab = nc.dram_tensor("q_parts", [NP, PARTS * D], bf16).ap()
    H1_tab = nc.dram_tensor("h1_parts", [NP, PARTS * D], bf16).ap()
    G2_tab = nc.dram_tensor("g2_rows", [NP, D], fp32).ap()
    G3_tab = nc.dram_tensor("g3_parts", [NP, PARTS * D], bf16).ap()
    dst_row = nc.dram_tensor("dst_row", [NQ, QE], fp32).ap()
    ea_rows = nc.dram_tensor("ea_rows", [18, NQ * QE], bf16).ap()
    blk_tab = nc.dram_tensor("blk_tab", [NQ, 2], i32).ap()
    cnt_tab = nc.dram_tensor("count_blocks", [NQ, 128, 2 * CW], bf16).ap()
    first_tab = nc.dram_tensor("first_store", [2, 128], bf16).ap()
    wc_tab = nc.dram_tensor("wc_parts", [2, PARTS, D], bf16).ap()

    ctx = ExitStack()
    with ctx:
        def sb(name, shape, dt=fp32):
            return ctx.enter_context(nc.sbuf_tensor(name, shape, dt))

        def sem(name):
            return ctx.enter_context(nc.semaphore(name))

        x = sb("x", [128, NT, D])
        h = sb("h", [128, NT, D])
        hT = sb("hT", [128, NP])
        ST = sb("ST", [128, NP])
        aggT = sb("aggT", [128, NP])
        g3 = aggT[:, :].rearrange("p (t d) -> p t d", d=D)
        r_bc = sb("r_bc", [128, NP], bf16)
        bn = sb("bn", [128, NT, 6])
        mv = sb("mv", [128, NT, 2])
        sd = sb("sd", [128, NT])
        rs = sb("rs", [128, NT])
        nb = sb("nb", [128, NT])
        rs2 = sb("rs2", [128, NT])
        nb2 = sb("nb2", [128, NT])
        pq = sb("pq", [128, 2, 2, 2, D])
        Hp = sb("Hp", [128, NT, PARTS, D], bf16)
        parts = Hp[:, 0:16, :, :].rearrange("p (b t w) a d -> p b t w a d", b=4, t=2)
        rest = sb("rest", [128, 2, 4 * D])
        degs = sb("degs", [128, 1 + NB, 4])
        deg2 = sb("deg2", [128, 2, 2 * NT + 1])
        cnt = sb("cnt", [128, 2, NT])
        dv = sb("dv", [128, 8, NT])
        INV_CNT, LEFT, DINV2, DINV3, D09, SELF3, T0_, T1_ = range(8)
        dvb = sb("dvb", [128, PARTS + 1, NT], bf16)
        ident = sb("ident", [128, 128])
        shift = sb("shift", [128, 256])
        identb = sb("identb", [128, 128], bf16)
        iota = sb("iota", [128, 128])
        iota_w = sb("iota_w", [128, 128])
        pio = sb("pio", [128, 1])
        pio_w = sb("pio_w", [128, 1])
        eps = sb("eps", [128, 1])
        zerob = sb("zerob", [128, 512], bf16)
        wab = sb("wab", [128, 2, D])
        w_m2 = sb("w_m2", [128, D])
        w_u1 = sb("w_u1", [128, 2, D])
        w_u2 = sb("w_u2", [128, D])
        w_11 = sb("w_11", [128, D])
        w_12 = sb("w_12", [128, D])
        w_3 = sb("w_3", [128, D])
        wcf = sb("wcf", [2, D])
        wcp = sb("wcp", [2, PARTS, D], bf16)
        wcr = sb("wcr", [2, D])
        wc18 = sb("wc18", [18, D], bf16)
        cols = sb("cols", [128, 2])
        bc = sb("bc", [128, 8, D])
        B_P, B_Q, B_U2, B_GA, B_BE, B_L1, B_L1B, B_L2 = range(8)
        onesb = sb("onesb", [128, 128], bf16)
        ones = sb("ones", [128, 1])
        iota_i = sb("iota_i", [128, NT, CB])
        iota_m = sb("iota_m", [128, CW], mybir.dt.float16)
        iota_b = sb("iota_b", [128, NCB])
        iota_c = sb("iota_c", [128, CT])
        idx = sb("idx", [128, NQ + 1, 4], u32)
        idx_q = sb("idx_q", [128, ITER, 4], u32)
        dstT = sb("dstT", [128, NQ, 4])
        wT = sb("wT", [128, NQ, 4])
        wq = sb("wq", [128, NQ, 4, 4], bf16)
        blk = sb("blk", [128, 2])
        blk_i = sb("blk_i", [128, 2], i32)
        blk_s = sb("blk_s", [128, 2], i32)
        base64 = sb("base64", [128, 1])
        row_i = sb("row_i", [1, NQ, 2], i32)
        row_f = sb("row_f", [1, NQ, 2])
        far = sb("far", [1, NQ])
        far1 = sb("far1", [1, 1])
        far_i = sb("far_i", [1, 1], i32)
        far_s = sb("far_s", [1, 1], i32)
        passes_i = sb("passes_i", [1, 1], i32)
        tab_f = sb("tab_f", [1, NQ])
        tab_i = sb("tab_i", [1, NQ], i32)
        room = sb("room", [128, 2 * CQ * 2 * CW], bf16)
        sel = room[:, 0:8 * NCB * CT].bitcast(fp32).rearrange("p (j c) -> p j c", j=4)
        Qw = room[:, 0:NB * PARTS * D].rearrange("p (b c) -> p b c", b=NB)
        AT = NB * PARTS * D
        mov = room[:, AT:AT + 2 * CT * CW].rearrange("p (s j c) -> p s j c", s=2, j=CT)
        AT += 2 * CT * CW
        sta = room[:, AT:AT + 2 * CT * 128].rearrange("p (s j c) -> p s j c", s=2, j=CT)
        assert AT + 2 * CT * 128 <= 2 * CQ * 2 * CW
        counts = room[:, :].rearrange("p (s c) -> p s c", s=2)
        cmax = sb("cmax", [128, 4])
        later = sb("later", [128, 4, NCB], bf16)
        slots = sb("slots", [128, NCB, CT])
        K4 = sb("K4", [128, NCB, CT])
        lo4 = sb("lo4", [128, NCB, CT])
        whole = sb("whole", [128, 2])
        whole1 = sb("whole1", [1, 4])
        many = sb("many", [128, NT])
        flag_i = sb("flag_i", [1, 1], i32)
        cnt_out = sb("cnt_out", [128, 2, 2, CW], bf16)
        ea18 = sb("ea18", [18, ITER, QE], bf16)
        sT = sb("sT", [128, ITER, QE], bf16)
        aggT_b = aggT[:, :].bitcast(bf16)
        G = aggT_b[:, 0:ITER * 4 * PARTS * D].rearrange("p (k c d) -> p k c d", k=ITER, c=4)
        ST_b = ST[:, :].bitcast(bf16)
        oh = ST_b[:, 0:ITER * QE].rearrange("p (k c n) -> p k c n", k=ITER, c=4)
        RP = ST_b[:, ITER * QE:ITER * QE + 2 * PARTS * 4 * D].rearrange("p (k a c d) -> p k a c d", k=2, a=PARTS, c=4)
        Hp_f = Hp[:, :, :, :].rearrange("p t a d -> p (t a d)").bitcast(fp32)
        R = Hp_f[:, 0:8 * D].rearrange("p (k c d) -> p k c d", k=2, c=4)
        R_left = Hp_f[:, 8 * D:16 * D].rearrange("p (k c d) -> p k c d", k=2, c=4)
        row_bc = Hp_f[:, 16 * D:16 * D + ITER * QE].rearrange("p (k e) -> p k e", k=ITER)
        wr = r_bc[:, 2 * QE:2 * QE + 4 * NQ * 4].bitcast(fp32).rearrange("p (s q c) -> p s q c", s=2, q=NQ)
        inb = r_bc[:, 0:2 * NCB * CT].bitcast(fp32).rearrange("p (b j) -> p b j", b=NCB)
        dst_l = hT[0:NQ, 0:QE].bitcast(i32)
        src_l = hT[0:NQ, QE:2 * QE].bitcast(i32)
        w_l = hT[0:NQ, 2 * QE:3 * QE]
        hi_i = hT[0:NQ, 3 * QE:4 * QE].bitcast(i32)
        hi_f = hT[0:NQ, 4 * QE:5 * QE]
        key_f = ST[0:NQ, 5 * QE:6 * QE]
        lo_f = r_bc[0:NQ, 0:2 * QE].bitcast(fp32)
        dst_f = ST[0:NQ, 0:QE]
        src_f = ST[0:NQ, QE:2 * QE]
        ea_l = ST[0:NQ, 2 * QE:4 * QE]
        dst_r = ST[0:NQ, 4 * QE:5 * QE]
        ea_r = aggT[0:NQ, 0:2 * QE].rearrange("p (i e) -> p i e", i=2)
        ea_m = aggT[0:NQ, 2 * QE:5 * QE].bitcast(bf16).rearrange("p (i a e) -> p i a e", i=2, a=PARTS)

        ps = ctx.enter_context(nc.psum_tensor("ps", [128, 8 * 512], fp32))

        def bank(j, n=512):
            return ps[:, 512 * j:512 * j + n]

        def dense_bank(j):
            return j if j else 7

        s_con = sem("constants_made")
        s_pad = sem("padding_made")
        s_dst = sem("dst_loaded")
        s_src = sem("src_loaded")
        s_ea = sem("ea_loaded")
        s_x = sem("x_loaded")
        s_wt = sem("weights_loaded")
        s_wc = sem("wc_stored")
        s_wc18 = sem("wc18_loaded")
        s_blk = sem("blocks_stored")
        s_row = sem("blocks_loaded")
        s_dr = sem("dst_row_stored")
        s_eas = sem("ea_rows_stored")
        s_pass = sem("passes_known")
        s_prep = sem("edge_prep")
        s_prepT = sem("edge_transposes")
        s_prepE = sem("edge_transposes_read")
        s_wcp = sem("wc_parts")
        s_eap = sem("ea_parts")
        s_dve = sem("dve_chain")
        s_act = sem("act_chain")
        s_pool = sem("pool_chain")
        LN = range(5)
        s_var = [sem(f"ln{n}_variance") for n in LN]
        s_root = [sem(f"ln{n}_root") for n in LN]
        s_norm = [sem(f"ln{n}_scale") for n in LN]
        s_rows = [sem(f"ln{n}_rows") for n in LN]
        STAGES = ["T0", "PQ", "DG", "B", "R", "A", "U", "V", "T1", "O1", "T2", "O2", "O3"]
        mm = {n: sem(f"{n}_done") for n in STAGES}
        ev = {n: sem(f"{n}_read") for n in STAGES}
        s_hi = sem("parts_hi")
        s_re = sem("parts_rest")
        s_mi = sem("parts_mid")
        s_lo = sem("parts_lo")
        s_st = [sem(f"parts_stored_{k}") for k in range(4)]
        s_g2 = sem("g2_stored")
        s_qw = sem("q_windows_loaded")
        s_zero = sem("acc_zeroed")
        s_acc = sem("acc_read")
        s_fin = sem("out_rows")
        s_out = sem("out_stored")
        s_degs = sem("degrees_known")
        s_bias = sem("x_with_bias")
        SW = range(4)
        s_tab = [sem(f"pass_tables_{s}") for s in SW]
        s_oh = [sem(f"onehot_ready_{s}") for s in SW]
        s_seg = [sem(f"quad_summed_{s}") for s in SW]
        s_ix = [sem(f"indices_ready_{s}") for s in SW]
        s_turn = sem("quads_to_gather")
        s_seen = sem("pass_tables_seen")
        s_gat = [[sem(f"gathered_{s}_{k}") for k in range(ITER)] for s in SW]
        s_c0 = sem("first_chunks")
        s_slot = sem("slots_ready")
        s_K4 = sem("block_keys_in_psum")
        s_key = sem("block_keys")
        s_cop = sem("count_operands")
        s_cmm = sem("counts_in_psum")
        s_cev = sem("counts_read")
        s_cst = [sem(f"counts_stored_{k}") for k in range(2)]
        s_flag = sem("flag_known")
        s_cld = [sem(f"counts_loaded_{k}") for k in range(2)]
        s_den = {1: sem("dense_1"), 3: sem("dense_3")}
        s_fb = {1: sem("h1_stored"), 3: sem("g3_stored")}
        s_rl = [sem(f"edge_rows_loaded_{k}") for k in range(ITER)]
        s_sT = sem("window_rows_ready")
        s_pre = sem("messages_in_psum")
        s_R = sem("rows_to_split")
        s_rhi = sem("row_hi")
        s_rre = sem("row_rest")
        s_rmi = sem("row_mid")
        s_rlo = sem("row_lo")
        block = ctx.enter_context(nc.Block())

        L0, L1, L2, L3 = range(4)

        def split_count(s, w, i, P):
            return (P * (s // 2) + w) * (NI * ITER) + i * ITER

        def pipeline(*stages):
            for step in range(NC + len(stages) - 1):
                for lag, stage in enumerate(stages):
                    if 0 <= step - lag < NC:
                        stage(step - lag)

        NH = len(HALVES)
        SPLIT0 = {"PQ": 0, "H1": NH, "G3": NH + NC}

        def part(m, a):
            if m < NH:
                return parts[:, m % 4, 0:len(HALVES[m]), :, a, :]
            tiles = TILES[(m - NH) % NC]
            return Hp[:, tiles[0]:tiles[-1] + 1, a, :]

        def stored(m):
            return s_st[m % 4], 32 * (m // 4 + 1)

        def left(m, width):
            if m < NH:
                return rest[:, m % 2, 0:width].rearrange("p (t w d) -> p t w d", w=2, d=D)
            return rest[:, m % 2, 0:width].rearrange("p (t d) -> p t d", d=D)

        @block.sync
        def _(sp):
            sp.dma_start(dst_l[0:QA, :], dst_in[0:QA * QE].rearrange("(p e) -> p e", e=QE)).then_inc(s_dst, 16)
            sp.dma_start(x[:, 0:NT - 1, :], x_in[0:128 * (NT - 1), :].rearrange("(t p) d -> p t d", p=128))\
                .then_inc(s_x, 16)
            sp.wait_ge(s_pad, 5)
            sp.dma_start(x[0:NR, NT - 1, :], x_in[128 * (NT - 1):N, :]).then_inc(s_x, 16)
            for tile, array, width, arrived in ((dst_l, dst_in, QE, s_dst), (src_l, src_in, QE, s_src),
                                                (w_l, ew_in, QE, s_src),
                                                (ea_l, ea_in.rearrange("e i -> (e i)"), 2 * QE, s_ea)):
                if array is not dst_in:
                    sp.dma_start(tile[0:QA, :], array[0:QA * width].rearrange("(p e) -> p e", e=width))\
                        .then_inc(arrived, 16)
                sp.dma_start(tile[QA:NQ - 1, :],
                             array[QA * width:(NQ - 1) * width].rearrange("(p e) -> p e", e=width))\
                    .then_inc(arrived, 16)
                rest_of = QR * (width // QE)
                sp.dma_start(tile[NQ - 1:NQ, 0:rest_of],
                             array[(NQ - 1) * width:(NQ - 1) * width + rest_of].rearrange("(a e) -> a e", a=1))\
                    .then_inc(arrived, 16)
            sp.wait_ge(s_prep, 1)
            sp.dma_start(blk_tab, blk_s[0:NQ, :]).then_inc(s_blk, 16)
            sp.wait_ge(s_blk, 16)
            sp.dma_start(row_i[:, :, :], blk_tab.rearrange("q (a b) -> a q b", a=1)).then_inc(s_row, 16)
            sp.wait_ge(s_prep, 2)
            sp.dma_start(dst_row, dst_r).then_inc(s_dr, 16)
            sp.wait_ge(s_eap, 5)
            for b in range(PARTS):
                sp.dma_start(ea_rows[6 * b:6 * b + 6, :].rearrange("r (p e) -> p r e", e=QE),
                             ea_m.rearrange("p i a e -> p (i a) e")).then_inc(s_eas, 16)
            sp.wait_ge(s_wcp, 5)
            sp.dma_start(wc_tab, wcp[:, :, :]).then_inc(s_wc, 16)
            sp.wait_ge(s_wc, 16)
            for b in range(PARTS):
                for i in range(2):
                    sp.dma_start(wc18[6 * b + 3 * i:6 * b + 3 * i + 3, :],
                                 wc_tab[i, b:b + 1, :].to_broadcast([3, D])).then_inc(s_wc18, 16)
            for m, tiles in enumerate(HALVES):
                sp.wait_ge(s_lo, m + 1)
                t0, n = tiles[0], len(tiles)
                for which, table in enumerate((P_tab, Q_tab)):
                    sp.dma_start(table[128 * t0:128 * (t0 + n), :].rearrange("(t p) c -> p t c", p=128),
                                 parts[:, m % 4, 0:n, which, :, :].rearrange("p t a d -> p t (a d)"))\
                        .then_inc(s_st[m % 4], 16)
            for m in range(NH - 4, NH):
                which, value = stored(m)
                sp.wait_ge(which, value)
            sp.wait_ge(s_key, 1)
            for half in range(2):
                sp.dma_start(Qw[WB * half:WB * half + WB, :, :],
                             Q_tab[WB * half:WB * (half + NB), :].rearrange("(b p) c -> p b c", p=WB))\
                    .then_inc(s_qw, 16)
            sp.wait_ge(s_pass, 1)
            P = sp.value_load(passes_i[0:1, 0:1], min_val=1, max_val=MAXP)
            sp.wait_ge(s_dr, 16)
            sp.wait_ge(s_eas, 16 * PARTS)
            sp.wait_ge(s_con, 15)
            for k in range(2):
                sp.dma_start(first_tab[k:k + 1, :], zerob[0:1, 0:128]).then_inc(s_cst[k], 16)
            with sp.Fori(0, P) as w:
                with sp.Fori(0, NI) as i:
                    for k in range(ITER):
                        sp.wait_ge(s_pre, (w * NI + i) * ITER + k + 1)
                        q = i * ITER + k
                        sp.dma_start(row_bc[:, k, :], dst_row[bass.ds(q, 1), :].to_broadcast([128, QE]))\
                            .then_inc(s_rl[k], 16)
                        sp.dma_start(ea18[:, k, :], ea_rows[:, bass.ds(q * QE, QE)]).then_inc(s_rl[k], 16)
            sp.wait_ge(s_flag, 1)
            flag = sp.value_load(flag_i[0:1, 0:1], min_val=0, max_val=1)

            def load_counts(s):
                for j, tiles in enumerate(TILES):
                    n = 4 * len(tiles)
                    c = j + NC * (s // 2)
                    if j >= 2:
                        sp.wait_ge(s_den[s], j - 1)
                    elif s == L3:
                        sp.wait_ge(s_den[L1], NC)
                    sp.dma_start(counts[:, c % 2, 0:n * 2 * CW].rearrange("p (q c) -> p q c", q=n),
                                 cnt_tab[CQ * j:CQ * j + n, :, :].rearrange("q p c -> p q c"))\
                        .then_inc(s_cld[c % 2], 16)

            def store_rows(s, name, table):
                sp.wait_ge(s_lo, SPLIT0[name] + NC)
                sp.dma_start(table.rearrange("(t p) c -> p t c", p=128),
                             Hp[:, :, :, :].rearrange("p t a d -> p t (a d)")).then_inc(s_fb[s], 16)

            def counts_stored():
                for k in range(2):
                    sp.wait_ge(s_cst[k], P * (16 * NQ // 2) + 16)

            with sp.If(flag > 0):
                counts_stored()
                load_counts(L1)
            with sp.Else():
                counts_stored()
                store_rows(L1, "H1", H1_tab)
            for j, tiles in enumerate(TILES):
                t0, n = tiles[0], len(tiles)
                sp.wait_ge(s_rows[3], j + 1)
                sp.dma_start(G2_tab[128 * t0:128 * (t0 + n), :].rearrange("(t p) c -> p t c", p=128),
                             h[:, t0:t0 + n, :]).then_inc(s_g2, 16)
            with sp.If(flag > 0):
                load_counts(L3)
            with sp.Else():
                store_rows(L3, "G3", G3_tab)
            for j, tiles in enumerate(TILES):
                sp.wait_ge(s_fin, j + 1)
                t0, full = tiles[0], [t for t in tiles if 128 * (t + 1) <= N]
                if full:
                    sp.dma_start(out[128 * t0:128 * (t0 + len(full)), :].rearrange("(t p) d -> p t d", p=128),
                                 h[:, t0:t0 + len(full), :]).then_inc(s_out, 16)
                if len(full) < len(tiles):
                    sp.dma_start(out[128 * (NT - 1):N, :], h[0:NR, NT - 1, :]).then_inc(s_out, 16)
            sp.wait_ge(s_out, 16 * NC)

        @block.gpsimd
        def _(pool):
            links = [0]

            def link(ins):
                links[0] += 1
                ins.then_inc(s_pool, 1)
                pool.wait_ge(s_pool, links[0])

            pool.memset(zerob[:, :], 0.0).then_inc(s_con, 1)
            pool.memset(eps[:, :], EPS).then_inc(s_con, 1)
            pool.iota(iota[:, :], pattern=[[1, 128]], base=0, channel_multiplier=0,
                      allow_small_or_imprecise_dtypes=True).then_inc(s_con, 1)
            pool.iota(pio[:, :], pattern=[[0, 1]], base=0, channel_multiplier=1,
                      allow_small_or_imprecise_dtypes=True).then_inc(s_con, 1)
            link(pool.memset(shift[:, :], 0.0))
            link(pool.affine_select(out=shift[:, :], in_=shift[:, :], compare_op=ALU.not_equal, fill=1.0, base=WB,
                                    pattern=[[-1, 256]], channel_multiplier=1))
            pool.tensor_copy(ident[:, :], shift[:, WB:WB + 128]).then_inc(s_con, 1)
            pool.tensor_copy(identb[:, :], shift[:, WB:WB + 128]).then_inc(s_con, 1)
            pool.memset(bc[:, B_P, :], 0.0).then_inc(s_con, 1)
            pool.memset(degs[:, 0, :], 0.0).then_inc(s_con, 1)
            pool.memset(wq[:, :, :, 0], 1.0).then_inc(s_con, 1)
            pool.memset(onesb[:, :], 1.0).then_inc(s_con, 1)
            pool.memset(ones[:, :], 1.0).then_inc(s_con, 1)
            pool.memset(idx[:, NQ, :], 0).then_inc(s_con, 1)
            pool.iota(iota_i[:, :, :], pattern=[[1, NT], [32, CB]], base=0, channel_multiplier=0,
                      allow_small_or_imprecise_dtypes=True).then_inc(s_con, 1)
            pool.iota(iota_b[:, :], pattern=[[CB, NCB]], base=0, channel_multiplier=0,
                      allow_small_or_imprecise_dtypes=True).then_inc(s_con, 1)
            pool.iota(iota_c[:, :], pattern=[[1, CT]], base=0, channel_multiplier=0,
                      allow_small_or_imprecise_dtypes=True).then_inc(s_con, 1)

            pool.wait_ge(s_ea, 48)
            ea_v = ea_l.rearrange("p (e i) -> p i e", i=2)
            pool.tensor_copy(ea_m[:, :, 0, :], ea_v).then_inc(s_eap, 1)
            pool.wait_ge(s_eap, 1)
            pool.tensor_tensor(ea_r, ea_v, ea_m[:, :, 0, :], ALU.subtract).then_inc(s_eap, 1)
            pool.wait_ge(s_eap, 2)
            pool.tensor_copy(ea_m[:, :, 1, :], ea_r).then_inc(s_eap, 1)
            pool.wait_ge(s_eap, 3)
            pool.tensor_tensor(ea_r, ea_r, ea_m[:, :, 1, :], ALU.subtract).then_inc(s_eap, 1)
            pool.wait_ge(s_eap, 4)
            pool.tensor_copy(ea_m[:, :, 2, :], ea_r).then_inc(s_eap, 1)

            def split_rest(m, source, width):
                pool.wait_ge(s_hi, m + 1)
                pool.tensor_tensor(left(m, width), source, part(m, 0), ALU.subtract).then_inc(s_re, 1)

            def split_lo(m, width):
                pool.wait_ge(s_mi, m + 1)
                pool.tensor_tensor(part(m, 2), left(m, width), part(m, 1), ALU.subtract).then_inc(s_lo, 1)

            for m, tiles in enumerate(HALVES):
                split_lo(m, 2 * D * len(tiles))

            pool.wait_ge(s_pass, 1)
            P = pool.value_load(passes_i[0:1, 0:1], min_val=1, max_val=MAXP)
            pool.wait_ge(s_prepE, 3)

            def sweep(s, table, rows, free):
                with pool.Fori(0, P) as w:

                    def indices(i, k):
                        free((w * NI + i) * ITER + k)
                        pool.sem_inc(s_turn, 1)
                        pool.tensor_copy(idx_q[:, k % ITER, :],
                                         idx[:, bass.ds(i * ITER + k, 1), :].rearrange("p a c -> p (a c)"))\
                            .then_inc(s_ix[s], 1)

                    indices(0, 0)
                    with pool.Fori(0, NI) as i:
                        for k in range(ITER):
                            indices(i, k + 1)
                            pool.wait_ge(s_ix[s], w * (NQ + 1) + i * ITER + k + 1)
                            free((w * NI + i) * ITER + k)
                            pool.sem_inc(s_turn, 1)
                            for c in range(4):
                                pool.indirect_dma_start(
                                    rows(k, c), None, table,
                                    bass.IndirectOffsetOnAxis(ap=idx_q[:, k, c:c + 1], axis=0))\
                                    .then_inc(s_gat[s][k], 16)
                    pool.wait_ge(s_ix[s], w * (NQ + 1) + NQ + 1)
                    pool.sem_inc(s_turn, 1)

            def rows3(k, c):
                return G[:, k, c, :]

            def rows_f(k, c):
                return G[:, k, c, 0:2 * D].bitcast(fp32)

            for m in range(NH - 4, NH):
                which, value = stored(m)
                pool.wait_ge(which, value)
            sweep(L0, P_tab, rows3, free=lambda n: pool.wait_ge(s_pre, n + 1))
            pool.wait_ge(s_flag, 1)
            flag = pool.value_load(flag_i[0:1, 0:1], min_val=0, max_val=1)

            def split(name, source):
                for j, tiles in enumerate(TILES):
                    t0, n = tiles[0], len(tiles)
                    split_rest(SPLIT0[name] + j, source[:, t0:t0 + n, :], D * n)
                    split_lo(SPLIT0[name] + j, D * n)

            split("H1", h)
            with pool.If(flag > 0):
                pool.sem_inc(s_turn, 1)
            with pool.Else():
                pool.wait_ge(s_fb[L1], 16)
                sweep(L1, H1_tab, rows3, free=lambda n: pool.wait_ge(s_seg[L1], n + 1))
            pool.wait_ge(s_g2, 16 * NC)
            sweep(L2, G2_tab, rows_f, free=lambda n: pool.wait_ge(s_R, P * NQ + n + 1))
            split("G3", g3)
            with pool.If(flag > 0):
                pool.sem_inc(s_turn, 1)
            with pool.Else():
                pool.wait_ge(s_fb[L3], 16)
                sweep(L3, G3_tab, rows3, free=lambda n: pool.wait_ge(s_seg[L3], n + 1))

        @block.scalar
        def _(act):
            links = [0]

            def link(ins):
                links[0] += 1
                ins.then_inc(s_act, 1)
                act.wait_ge(s_act, links[0])

            loads = [(wab[:, 0, :], mW1[0:D, :]), (wab[:, 1, :], mW1[D:2 * D, :]), (wcf[:, :], mW1[2 * D:2 * D + 2, :]),
                     (w_m2[:, :], mW2), (w_u1[:, 0, :], uW1[0:D, :]), (w_u1[:, 1, :], uW1[D:2 * D, :]),
                     (w_u2[:, :], uW2), (w_11[:, :], W1), (w_12[:, :], W2), (w_3[:, :], W3),
                     (cols[:, 0:1], mb2.rearrange("(p a) -> p a", a=1)),
                     (cols[:, 1:2], ub1.rearrange("(p a) -> p a", a=1))]
            for slot, v in ((B_Q, mb1), (B_U2, ub2), (B_GA, gamma), (B_BE, beta), (B_L1, b1), (B_L1B, b2), (B_L2, b3)):
                loads.append((bc[:, slot, :], v.rearrange("(a d) -> a d", a=1).to_broadcast([128, D])))
            assert len(loads) == 19
            for to, of in loads:
                act.dma_start(to, of).then_inc(s_wt, 16)

            act.wait_ge(s_con, 15)

            def root(n):
                def stage(j):
                    act.wait_ge(s_var[n], j + 1)
                    ts = slice(TILES[j][0], TILES[j][-1] + 1)
                    act.activation(sd[:, ts], mv[:, ts, 1], ACT.Sqrt, bias=eps[:, 0:1]).then_inc(s_root[n], 1)
                return stage

            def rows(n, to, func, source, scaled=None):
                def stage(j):
                    act.wait_ge(s_norm[n], j + 1)
                    for t in TILES[j]:
                        last = act.activation(to[:, t, :], source[:, t, :], func, scale=rs[:, t:t + 1],
                                              bias=nb[:, t:t + 1])
                        if scaled is not None:
                            last = act.activation(scaled[:, t, :], source[:, t, :], func, scale=rs2[:, t:t + 1],
                                                  bias=nb2[:, t:t + 1])
                    last.then_inc(s_rows[n], 1)
                return stage

            def split_hi(m, source):
                if 4 <= m < NH:
                    which, value = stored(m - 4)
                    act.wait_ge(which, value)
                act.activation(part(m, 0), source, ACT.Copy).then_inc(s_hi, 1)

            def split_mid(m, width):
                act.wait_ge(s_re, m + 1)
                act.activation(part(m, 1), left(m, width), ACT.Copy).then_inc(s_mi, 1)

            def split_rows(name, source, n):
                def stage(j):
                    t0, c = TILES[j][0], len(TILES[j])
                    act.wait_ge(s_rows[n], j + 1)
                    split_hi(SPLIT0[name] + j, source[:, t0:t0 + c, :])
                    split_mid(SPLIT0[name] + j, D * c)
                return stage

            act.wait_ge(s_x, 32)
            pipeline(root(0), rows(0, h, ACT.Relu, x))
            act.wait_ge(s_wt, 16 * 19)
            act.activation(wcp[:, 0, :], wcf[:, :], ACT.Copy).then_inc(s_wcp, 1)
            act.wait_ge(s_wcp, 2)
            act.activation(wcp[:, 1, :], wcr[:, :], ACT.Copy).then_inc(s_wcp, 1)
            act.wait_ge(s_wcp, 4)
            act.activation(wcp[:, 2, :], wcr[:, :], ACT.Copy).then_inc(s_wcp, 1)
            act.wait_ge(s_prepT, 3)
            for j in range(NC):
                act.wait_ge(mm["T0"], j + 1)
                c = 128 * len(TILES[j])
                act.activation(hT[:, 512 * j:512 * j + c], bank(j, c), ACT.Copy).then_inc(ev["T0"], 1)
            for m, tiles in enumerate(HALVES):
                act.wait_ge(ev["PQ"], m + 1)
                split_hi(m, pq[:, m % 2, 0:len(tiles), :, :])
                if m:
                    split_mid(m - 1, 2 * D * len(HALVES[m - 1]))
            split_mid(NH - 1, 2 * D * len(HALVES[-1]))

            act.wait_ge(s_pass, 1)
            P = act.value_load(passes_i[0:1, 0:1], min_val=1, max_val=MAXP)

            def splitter(s, w):

                def hi(i, k):
                    n, u = (w * NI + i) * ITER + k, split_count(s, w, i, P) + k
                    act.wait_ge(s_R, u + 1 + ITER)
                    act.wait_ge(s_seg[s], n + ITER - 1)
                    act.activation(RP[:, k % 2, 0, :, :], R[:, k % 2, :, :], ACT.Copy).then_inc(s_rhi, 1)

                def mid(i, k):
                    act.wait_ge(s_rre, split_count(s, w, i, P) + k + 3)
                    act.activation(RP[:, k % 2, 1, :, :], R_left[:, k % 2, :, :], ACT.Copy).then_inc(s_rmi, 1)

                return hi, mid

            with act.Fori(0, P) as w:
                hi, mid = splitter(L0, w)

                def relu(i, k):
                    n = (w * NI + i) * ITER + k
                    act.wait_ge(s_pre, n + 1 + ITER)
                    act.wait_ge(s_rre, n + 1)
                    act.activation(R[:, k % 2, :, :], bank(7).rearrange("p (c d) -> p c d", d=D), ACT.Relu)\
                        .then_inc(s_R, 1)

                def read_counts(i, k, r):
                    act.wait_ge(s_cmm, (w * NI + i) * (2 * ITER) + 2 * k + r + 3)
                    if r == 0:
                        act.wait_ge(s_cst[k % 2], (w * NI + i) * 32 + 16 * (k // 2) + 16)
                    act.activation(cnt_out[:, k % 2, r, :], bank(7, CW), ACT.Copy).then_inc(s_cev, 1)

                def store_counts(i, k):
                    act.wait_ge(s_cev, (w * NI + i) * (2 * ITER) + 2 * k + 3)
                    act.dma_start(cnt_tab[bass.ds(i * ITER + k, 1), :, :].rearrange("q p c -> p (q c)"),
                                  cnt_out[:, k % 2, :, :].rearrange("p r c -> p (r c)"))\
                        .then_inc(s_cst[k % 2], 16)

                def step(i, peeled):
                    for k in range(ITER):
                        ahead = not (peeled and k == ITER - 1)
                        if ahead:
                            relu(i, k + 1)
                            hi(i, k + 1)
                        read_counts(i, k, 0)
                        if ahead:
                            mid(i, k + 1)
                        read_counts(i, k, 1)
                        store_counts(i, k)

                relu(0, 0)
                hi(0, 0)
                mid(0, 0)
                with act.Fori(0, NI - 1) as i:
                    step(i, False)
                step(NI - 1, True)

            def read_acc(s, dense=False):
                def stage(j):
                    if dense:
                        act.wait_ge(s_den[s], j + 1)
                    elif j == 0:
                        act.wait_ge(s_seg[s], P * NQ + ITER)
                    c = 128 * len(TILES[j])
                    if s == L0 and j == NC - 1:
                        act.wait_ge(ev["DG"], 1)
                    of = bank(dense_bank(j) if dense else j, c)
                    act.activation(ST[:, 512 * j:512 * j + c], of, ACT.Copy).then_inc(s_acc, 1)
                return stage

            pipeline(read_acc(L0))
            act.wait_ge(s_degs, 1)
            act.activation(dv[:, T0_, :], dv[:, T0_, :], ACT.Sqrt).then_inc(s_degs, 1)
            act.activation(dv[:, T1_, :], dv[:, T1_, :], ACT.Sqrt).then_inc(s_degs, 1)
            for j in range(NC):
                act.wait_ge(mm["R"], j + 1)
                c = 128 * len(TILES[j])
                act.activation(r_bc[:, 512 * j:512 * j + c], bank(j, c), ACT.Copy).then_inc(ev["R"], 1)
            for j in range(NC):
                act.wait_ge(mm["U"], j + 1)
                c = 128 * len(TILES[j])
                act.activation(ST[:, 512 * j:512 * j + c], bank(j, c), ACT.Relu, bias=cols[:, 1:2])\
                    .then_inc(ev["U"], 1)
            pipeline(root(1), rows(1, h, ACT.Identity, h), lambda j: None, root(2), rows(2, h, ACT.Relu, x),
                     split_rows("H1", h, 2))
            act.wait_ge(s_flag, 1)
            flag = act.value_load(flag_i[0:1, 0:1], min_val=0, max_val=1)

            def idle(j):
                pass

            with act.If(flag > 0):
                pipeline(read_acc(L1, dense=True), idle, root(3), rows(3, h, ACT.Relu, x))
            with act.Else():
                pipeline(read_acc(L1))
                pipeline(root(3), rows(3, h, ACT.Relu, x))

            with act.Fori(0, P) as w:
                hi, mid = splitter(L2, w)
                with act.Fori(0, NI) as i:
                    for k in range(ITER):
                        hi(i, k)
                        mid(i, k)
            pipeline(read_acc(L2))
            pipeline(root(4), rows(4, h, ACT.Relu, x, scaled=g3), split_rows("G3", g3, 4))
            own = hT[:, :].rearrange("p (t d) -> p t d", d=D)
            for t in range(NT):
                last = act.activation(own[:, t, :], h[:, t, :], ACT.Copy, scale=dv[:, SELF3, t:t + 1])
            last.then_inc(s_bias, 1)
            with act.If(flag > 0):
                pipeline(read_acc(L3, dense=True))
            with act.Else():
                pipeline(read_acc(L3))

        @block.vector
        def _(dve):
            links = [0]

            def link(ins):
                links[0] += 1
                ins.then_inc(s_dve, 1)
                dve.wait_ge(s_dve, links[0])

            dve.memset(dst_l[QA:NQ, :], PAD_DST).then_inc(s_pad, 1)
            dve.memset(src_l[QA:NQ, :], 0).then_inc(s_pad, 1)
            dve.memset(w_l[QA:NQ, :], 0.0).then_inc(s_pad, 1)
            dve.memset(ea_l[QA:NQ, :], 0.0).then_inc(s_pad, 1)
            dve.memset(x[:, NT - 1, :], 0.0).then_inc(s_pad, 1)
            dve.wait_ge(s_dst, 48)
            link(dve.tensor_copy(dst_f, dst_l))
            dve.tensor_reduce(blk[0:NQ, 0:1], dst_f, AX.X, ALU.min)
            link(dve.tensor_reduce(blk[0:NQ, 1:2], dst_f, AX.X, ALU.max))
            link(dve.tensor_copy(blk_i[0:NQ, :], blk[0:NQ, :]))
            link(dve.tensor_single_scalar(blk_s[0:NQ, :], blk_i[0:NQ, :], 6, ALU.arith_shift_right))
            dve.tensor_scalar(base64[0:NQ, :], blk_s[0:NQ, 0:1], float(WB), None, ALU.mult).then_inc(s_prep, 1)
            dve.wait_ge(s_prep, 1)
            dve.tensor_scalar(dst_r, dst_f, base64[0:NQ, 0:1], None, ALU.subtract).then_inc(s_prep, 1)
            dve.wait_ge(s_src, 96)
            dve.tensor_copy(src_f, src_l).then_inc(s_prep, 1)
            link(dve.tensor_single_scalar(hi_i, src_l, 7, ALU.arith_shift_right))
            dve.tensor_reduce(cmax[0:NQ, :], dst_f.rearrange("p (c e) -> p c e", c=4), AX.X, ALU.max)
            link(dve.tensor_copy(hi_f, hi_i))
            dve.scalar_tensor_tensor(key_f, dst_f, 32.0, hi_f, ALU.mult, ALU.add)
            dve.wait_ge(s_prep, 3)
            dve.scalar_tensor_tensor(lo_f, hi_f, -128.0, src_f, ALU.mult, ALU.add).then_inc(s_prep, 1)
            dve.wait_ge(s_con, 15)
            for c in range(4):
                last = dve.tensor_scalar(later[0:NQ, c, :], iota_b[0:NQ, :], cmax[0:NQ, c:c + 1], None, ALU.is_gt)
            last.then_inc(s_prep, 1)
            dve.tensor_copy(iota_m[:, :], iota_i[:, :, :].rearrange("p h w -> p (h w)")).then_inc(s_prep, 1)

            def variance(n, source):
                def stage(j):
                    for t in TILES[j]:
                        last = dve.bn_stats(bn[:, t, :], source[:, t, :])
                    link(last)
                    for t in TILES[j]:
                        last = dve.bn_aggr(mv[:, t, :], bn[:, t, :])
                    last.then_inc(s_var[n], 1)
                return stage

            def norm(n, by=None, by2=None):
                def stage(j):
                    ts = slice(TILES[j][0], TILES[j][-1] + 1)
                    dve.wait_ge(s_root[n], j + 1)
                    link(dve.reciprocal(rs[:, ts], sd[:, ts]))
                    if by is not None:
                        link(dve.tensor_tensor(rs[:, ts], rs[:, ts], dv[:, by, ts], ALU.mult))
                    last = dve.scalar_tensor_tensor(nb[:, ts], mv[:, ts, 0], -1.0, rs[:, ts], ALU.mult, ALU.mult)
                    if by2 is not None:
                        link(last)
                        dve.tensor_tensor(rs2[:, ts], rs[:, ts], dv[:, by2, ts], ALU.mult)
                        last = dve.tensor_tensor(nb2[:, ts], nb[:, ts], dv[:, by2, ts], ALU.mult)
                    last.then_inc(s_norm[n], 1)
                return stage

            dve.wait_ge(s_x, 32)
            pipeline(variance(0, x), norm(0))

            dve.wait_ge(s_row, 16)
            link(dve.tensor_copy(row_f[:, :, :], row_i[:, :, :]))
            link(dve.tensor_tensor(far[:, :], row_f[:, :, 1], row_f[:, :, 0], ALU.subtract))
            link(dve.tensor_reduce(far1[:, :], far[:, :], AX.X, ALU.max))
            link(dve.tensor_copy(far_i[:, :], far1[:, :]))
            link(dve.tensor_single_scalar(far_s[:, :], far_i[:, :], 1, ALU.arith_shift_right))
            dve.tensor_scalar(passes_i[:, :], far_s[:, :], 1.0, None, ALU.add).then_inc(s_pass, 1)

            dve.wait_ge(s_c0, 1)
            link(dve.tensor_tensor(slots[:, :, :],
                                   bank(3, NCB).rearrange("p (b j) -> p b j", j=1).to_broadcast([128, NCB, CT]),
                                   iota_c[:, :].rearrange("p (a j) -> p a j", a=1).to_broadcast([128, NCB, CT]),
                                   ALU.add))
            link(dve.tensor_scalar(base64[:, :], pio[:, :], 4.0, None, ALU.mult))
            for c in range(4):
                last = dve.tensor_scalar(sel[0:NQ, c, :], slots[0:NQ, :, :].rearrange("p b j -> p (b j)"),
                                         -float(c), base64[0:NQ, 0:1], ALU.add, ALU.is_equal)
            last.then_inc(s_slot, 1)

            dve.wait_ge(s_wcp, 1)
            dve.tensor_tensor(wcr[:, :], wcf[:, :], wcp[:, 0, :], ALU.subtract).then_inc(s_wcp, 1)
            dve.wait_ge(s_wcp, 3)
            dve.tensor_tensor(wcr[:, :], wcr[:, :], wcp[:, 1, :], ALU.subtract).then_inc(s_wcp, 1)

            for n, (to, j) in enumerate(((dstT, 1), (idx, 0), (wT, 2))):
                dve.wait_ge(s_prepT, n + 1)
                dve.tensor_copy(to[:, 0:NQ, :].rearrange("p q c -> p c q"),
                                bank(j, 4 * NQ).rearrange("p (c q) -> p c q", c=4)).then_inc(s_prepE, 1)
            dve.wait_ge(s_prepE, 3)
            dve.wait_ge(s_con, 15)
            link(dve.tensor_copy(wq[:, :, :, 1], wT[:, :, :]))
            link(dve.tensor_tensor(wr[:, 0, :, :], wT[:, :, :], wq[:, :, :, 1], ALU.subtract))
            link(dve.tensor_copy(wq[:, :, :, 2], wr[:, 0, :, :]))
            link(dve.tensor_tensor(wr[:, 1, :, :], wr[:, 0, :, :], wq[:, :, :, 2], ALU.subtract))
            link(dve.tensor_copy(wq[:, :, :, 3], wr[:, 1, :, :]))

            dve.wait_ge(s_wt, 16 * 19)
            def pq_rest(m):
                n = len(HALVES[m])
                dve.wait_ge(s_hi, m + 1)
                if m >= 2:
                    dve.wait_ge(s_lo, m - 1)
                dve.tensor_tensor(left(m, 2 * D * n), pq[:, m % 2, 0:n, :, :], part(m, 0), ALU.subtract)\
                    .then_inc(s_re, 1)

            for m, tiles in enumerate(HALVES):
                n = len(tiles)
                dve.wait_ge(mm["PQ"], m + 1)
                if m >= 2:
                    dve.wait_ge(s_re, m - 1)
                dve.tensor_tensor(pq[:, m % 2, 0:n, :, :],
                                  bank(m % 8, 256 * n).rearrange("p (t w d) -> p t w d", w=2, d=D),
                                  bc[:, B_P:B_Q + 1, :].rearrange("p (a w) d -> p a w d", a=1)
                                  .to_broadcast([128, n, 2, D]), ALU.add).then_inc(ev["PQ"], 1)
                if m:
                    pq_rest(m - 1)
            pq_rest(NH - 1)

            dve.wait_ge(s_K4, 1)
            link(dve.tensor_scalar(slots[:, :, 0], iota_b[:, :], 32.0, None, ALU.mult))
            for n in range(2):
                half = slice(n * (NCB // 2), (n + 1) * (NCB // 2))
                dve.tensor_tensor(K4[:, half, :],
                                  bank(n, NCB * CT // 2).rearrange("p (b j) -> p b j", j=CT),
                                  slots[:, half, 0:1].to_broadcast([128, NCB // 2, CT]), ALU.subtract)
                last = dve.tensor_copy(lo4[:, half, :],
                                       bank(2 + n, NCB * CT // 2).rearrange("p (b j) -> p b j", j=CT))
            last.then_inc(s_key, 1)
            dve.wait_ge(s_key, 1)
            link(dve.tensor_scalar(inb[:, :, :], K4[:, :, :], 32.0 * CB, None, ALU.is_lt))
            link(dve.scalar_tensor_tensor(inb[:, :, :], K4[:, :, :], 0.0, inb[:, :, :], ALU.is_ge, ALU.mult))
            link(dve.tensor_reduce(whole[:, 0:1], inb[:, :, :], AX.XY, ALU.add))

            P = dve.value_load(passes_i[0:1, 0:1], min_val=1, max_val=MAXP)

            def start_tables(s):
                dve.tensor_scalar(tab_f[:, :], row_f[:, :, 0], -2.0, None, ALU.add)
                dve.tensor_scalar(pio_w[:, :], pio[:, :], -128.0, None, ALU.add)
                dve.tensor_scalar(iota_w[:, :], iota[:, :], -128.0, None, ALU.add).then_inc(s_tab[s], 1)
                dve.wait_ge(s_tab[s], 1)

            def move_tables(s, w):
                dve.wait_ge(s_seg[s], w * NQ + ITER)
                dve.tensor_scalar(tab_f[:, :], tab_f[:, :], 2.0, float(NB - 1), ALU.add, ALU.min)\
                    .then_inc(s_tab[s], 1)
                dve.tensor_scalar(pio_w[:, :], pio_w[:, :], 128.0, None, ALU.add).then_inc(s_tab[s], 1)
                dve.tensor_scalar(iota_w[:, :], iota_w[:, :], 128.0, None, ALU.add).then_inc(s_tab[s], 1)
                dve.wait_ge(s_tab[s], w * 4 + 4)
                dve.tensor_copy(tab_i[:, :], tab_f[:, :]).then_inc(s_tab[s], 1)

            def onehot(s, w, i, k):
                dve.wait_ge(s_seg[s], (w * NI + i) * ITER + k + 1)
                dve.tensor_tensor(oh[:, k % ITER, :, :],
                                  iota_w[:, :].rearrange("p (a n) -> p a n", a=1).to_broadcast([128, 4, 128]),
                                  dstT[:, bass.ds(i * ITER + k, 1), :].rearrange("p a (c b) -> p (a c) b", b=1)
                                  .to_broadcast([128, 4, 128]), ALU.is_equal).then_inc(s_oh[s], 1)

            def row_rest(u, k):
                dve.wait_ge(s_rhi, u + 1)
                dve.tensor_tensor(R_left[:, k % 2, :, :], R[:, k % 2, :, :], RP[:, k % 2, 0, :, :], ALU.subtract)\
                    .then_inc(s_rre, 1)

            def row_lo(u, k):
                dve.wait_ge(s_rmi, u + 1)
                dve.tensor_tensor(RP[:, k % 2, 2, :, :], R_left[:, k % 2, :, :], RP[:, k % 2, 1, :, :],
                                  ALU.subtract).then_inc(s_rlo, 1)

            start_tables(L0)
            with dve.Fori(0, P) as w:

                def build(i, k):
                    onehot(L0, w, i, k)
                    dve.wait_ge(s_rl[k % ITER], (w * NI + i + k // ITER + 1) * 32)
                    dve.tensor_scalar(sT[:, k % ITER, :], row_bc[:, k % ITER, :], pio_w[:, 0:1], None, ALU.is_equal)\
                        .then_inc(s_sT, 1)

                def count_operands(i, k, r):
                    n = (w * NI + i) * (2 * ITER) + 2 * k + r
                    dve.wait_ge(s_cmm, n + 1)
                    b = i * (2 * ITER) + 2 * k + r
                    for j in range(CT):
                        dve.tensor_scalar(mov[:, r, j, :], iota_m[:, :],
                                          K4[:, bass.ds(b, 1), j:j + 1].rearrange("p a j -> p (a j)"), None,
                                          ALU.is_equal)
                    dve.tensor_tensor(sta[:, r, :, :],
                                      iota[:, :].rearrange("p (a n) -> p a n", a=1).to_broadcast([128, CT, 128]),
                                      lo4[:, bass.ds(b, 1), :].rearrange("p a (c b) -> p (a c) b", b=1)
                                      .to_broadcast([128, CT, 128]), ALU.is_equal).then_inc(s_cop, 1)

                def step(i, peeled):
                    before = (w * NI + i) * ITER
                    for k in range(ITER):
                        ahead = not (peeled and k == ITER - 1)
                        count_operands(i, k, 1)
                        if ahead:
                            row_rest(before + k + 1, k + 1)
                        if not peeled or k + 3 < ITER:
                            build(i, k + 3)
                        if ahead:
                            row_lo(before + k + 1, k + 1)
                            count_operands(i, k + 1, 0)

                move_tables(L0, w)
                build(0, 0)
                build(0, 1)
                row_rest(w * NQ, 0)
                build(0, 2)
                row_lo(w * NQ, 0)
                count_operands(0, 0, 0)
                with dve.Fori(0, NI - 1) as i:
                    step(i, False)
                step(NI - 1, True)

            dve.wait_ge(s_seg[L0], P * NQ + ITER)
            link(dve.tensor_copy(degs[:, 1:1 + NB, :],
                                 ps[:, DEG:DEG + 4 * NB].rearrange("p (b f) -> p b f", f=4)))
            dve.tensor_copy(deg2[:, 0, 0:NB + 1], degs[:, :, 0])
            link(dve.tensor_tensor(deg2[:, 1, 0:NB + 1], degs[:, :, 2], degs[:, :, 3], ALU.add))
            link(dve.tensor_tensor(deg2[:, 1, 0:NB + 1], deg2[:, 1, 0:NB + 1], degs[:, :, 1], ALU.add))
            dve.memset(deg2[:, :, NB + 1:2 * NT + 1], 0.0).then_inc(ev["DG"], 1)
            dve.wait_ge(mm["DG"], 1)
            link(dve.tensor_copy(cnt[:, :, :], ps[:, PRE:PRE + 2 * NT].rearrange("p (f t) -> p f t", f=2)))
            link(dve.tensor_scalar(many[:, :], cnt[:, 0, :], 256.0, None, ALU.is_gt))
            dve.tensor_reduce(whole[:, 1:2], many[:, :], AX.X, ALU.add).then_inc(ev["DG"], 1)
            link(dve.tensor_scalar(dv[:, INV_CNT, :], cnt[:, 0, :], 1.0, None, ALU.max))
            link(dve.reciprocal(dv[:, INV_CNT, :], dv[:, INV_CNT, :]))
            link(dve.tensor_copy(dvb[:, 0, :], dv[:, INV_CNT, :]))
            link(dve.tensor_tensor(dv[:, LEFT, :], dv[:, INV_CNT, :], dvb[:, 0, :], ALU.subtract))
            link(dve.tensor_copy(dvb[:, 1, :], dv[:, LEFT, :]))
            link(dve.tensor_tensor(dv[:, T0_, :], dv[:, LEFT, :], dvb[:, 1, :], ALU.subtract))
            link(dve.tensor_copy(dvb[:, 2, :], dv[:, T0_, :]))
            dve.tensor_scalar(dvb[:, PARTS, :], cnt[:, 0, :], 1.0, None, ALU.min).then_inc(ev["DG"], 1)
            dve.tensor_scalar(dv[:, T1_, :], cnt[:, 0, :], 1.0, None, ALU.add)
            link(dve.tensor_scalar(dv[:, SELF3, :], cnt[:, 1, :], 1.0, None, ALU.add))
            dve.tensor_scalar(dv[:, DINV2, :], dv[:, SELF3, :], 0.0, None, ALU.is_gt)
            dve.tensor_scalar(dv[:, T0_, :], dv[:, SELF3, :], TINY, None, ALU.max).then_inc(s_degs, 1)
            dve.wait_ge(s_degs, 3)
            dve.reciprocal(dv[:, T0_, :], dv[:, T0_, :])
            link(dve.reciprocal(dv[:, DINV3, :], dv[:, T1_, :]))
            dve.tensor_tensor(dv[:, DINV2, :], dv[:, DINV2, :], dv[:, T0_, :], ALU.mult)
            link(dve.tensor_scalar(dv[:, D09, :], dv[:, DINV3, :], 0.9, None, ALU.mult))
            link(dve.tensor_tensor(dv[:, SELF3, :], dv[:, D09, :], dv[:, DINV3, :], ALU.mult))
            link(dve.tensor_scalar(dv[:, SELF3, :], dv[:, SELF3, :], 0.1, None, ALU.add))
            dve.wait_ge(mm["DG"], 2)
            link(dve.tensor_copy(whole1[:, 0:2], ps[0:1, PRE + 128:PRE + 130]))
            dve.tensor_scalar(whole1[:, 0:1], whole1[:, 0:1], float(NQ * QE), None, ALU.is_equal)
            link(dve.tensor_scalar(whole1[:, 1:2], whole1[:, 1:2], 0.0, None, ALU.is_equal))
            link(dve.tensor_tensor(whole1[:, 2:3], whole1[:, 0:1], whole1[:, 1:2], ALU.mult))
            link(dve.tensor_scalar(whole1[:, 3:4], far1[:, :], 2.0, None, ALU.is_lt))
            dve.tensor_tensor(flag_i[:, :], whole1[:, 2:3], whole1[:, 3:4], ALU.mult).then_inc(s_flag, 1)
            for j in range(NC):
                dve.wait_ge(s_acc, j + 1)
                dve.wait_ge(mm["B"], j + 1)
                c = 128 * len(TILES[j])
                dve.tensor_tensor(ST[:, 512 * j:512 * j + c], ST[:, 512 * j:512 * j + c], bank(j, c), ALU.mult)\
                    .then_inc(ev["B"], 1)
            for j in range(NC):
                dve.wait_ge(mm["A"], j + 1)
                c = 128 * len(TILES[j])
                dve.scalar_tensor_tensor(aggT[:, 512 * j:512 * j + c], r_bc[:, 512 * j:512 * j + c], cols[:, 0:1],
                                         bank(j, c), ALU.mult, ALU.add).then_inc(ev["A"], 1)

            def tiles_of(a, j):
                return a[:, TILES[j][0]:TILES[j][-1] + 1, :]

            def bias_of(slot, n):
                return bc[:, slot:slot + 1, :].to_broadcast([128, n, D])

            def bank_of(j):
                return bank(j, 128 * len(TILES[j])).rearrange("p (t d) -> p t d", d=D)

            def update(j):
                dve.wait_ge(mm["V"], j + 1)
                dve.tensor_tensor(tiles_of(h, j), bank_of(j), tiles_of(h, j), ALU.add).then_inc(ev["V"], 1)
                dve.wait_ge(ev["V"], j + 1)
                link(dve.tensor_tensor(tiles_of(h, j), tiles_of(h, j), bias_of(B_U2, len(TILES[j])), ALU.add))

            def residual(j):
                n = len(TILES[j])
                dve.wait_ge(s_rows[1], j + 1)
                link(dve.tensor_tensor(tiles_of(h, j), tiles_of(h, j), bias_of(B_GA, n), ALU.mult))
                link(dve.tensor_tensor(tiles_of(x, j), tiles_of(x, j), bias_of(B_BE, n), ALU.add))
                link(dve.tensor_tensor(tiles_of(x, j), tiles_of(x, j), tiles_of(h, j), ALU.add))

            def both(*stages):
                def stage(j):
                    for s in stages:
                        s(j)
                return stage

            pipeline(both(update, variance(1, h)), norm(1), both(residual, variance(2, x)), norm(2))
            for j in range(NC):
                dve.wait_ge(mm["T1"], j + 1)
                c = 128 * len(TILES[j])
                dve.tensor_copy(hT[:, 512 * j:512 * j + c], bank(j, c)).then_inc(ev["T1"], 1)

            def plain_sweep(s):
                start_tables(s)
                with dve.Fori(0, P) as w:
                    move_tables(s, w)
                    with dve.Fori(0, NI) as i:
                        for k in range(ITER):
                            onehot(s, w, i, k)

            def add_bias(*slots):
                for slot in slots:
                    link(dve.tensor_tensor(x[:, :, :], x[:, :, :], bias_of(slot, NT), ALU.add))

            add_bias(B_L1, B_L1B)
            flag = dve.value_load(flag_i[0:1, 0:1], min_val=0, max_val=1)
            with dve.If(flag > 0):
                dve.wait_ge(s_den[L1], 1)
            with dve.Else():
                plain_sweep(L1)

            def out1(j):
                dve.wait_ge(mm["O1"], j + 1)
                dve.tensor_tensor(tiles_of(x, j), tiles_of(x, j), bank_of(j), ALU.add).then_inc(ev["O1"], 1)
                dve.wait_ge(ev["O1"], j + 1)

            pipeline(both(out1, variance(3, x)), norm(3, by=DINV2))
            for j in range(NC):
                dve.wait_ge(mm["T2"], j + 1)
                c = 128 * len(TILES[j])
                dve.tensor_copy(hT[:, 512 * j:512 * j + c], bank(j, c)).then_inc(ev["T2"], 1)
            add_bias(B_L2)

            start_tables(L2)
            with dve.Fori(0, P) as w:
                move_tables(L2, w)
                with dve.Fori(0, NI) as i:
                    steps = w * NI + i
                    split0 = split_count(L2, w, i, P)

                    def weigh(k):
                        dve.wait_ge(s_gat[L2][k], (steps + 1) * 64)
                        dve.wait_ge(s_rre, split0 + k + 1)
                        dve.tensor_tensor(R[:, k % 2, :, :], G[:, k, :, 0:2 * D].bitcast(fp32),
                                          wT[:, bass.ds(i * ITER + k, 1), :].rearrange("p a (c b) -> p (a c) b", b=1)
                                          .to_broadcast([128, 4, D]), ALU.mult).then_inc(s_R, 1)

                    onehot(L2, w, i, 0)
                    weigh(0)
                    for k in range(ITER):
                        row_rest(split0 + k, k)
                        if k + 1 < ITER:
                            onehot(L2, w, i, k + 1)
                            weigh(k + 1)
                        row_lo(split0 + k, k)

            def out2(j):
                dve.wait_ge(mm["O2"], j + 1)
                for n, t in enumerate(TILES[j]):
                    last = dve.scalar_tensor_tensor(x[:, t, :], bank(j)[:, 128 * n:128 * n + 128],
                                                    dv[:, DINV2, t:t + 1], x[:, t, :], ALU.mult, ALU.add)
                last.then_inc(ev["O2"], 1)
                dve.wait_ge(ev["O2"], j + 1)

            pipeline(both(out2, variance(4, x)), norm(4, by2=DINV3))
            dve.wait_ge(s_rows[4], NC)
            link(dve.tensor_tensor(x[:, :, :], x[:, :, :], h[:, :, :], ALU.add))
            with dve.If(flag > 0):
                dve.wait_ge(s_den[L3], 1)
            with dve.Else():
                plain_sweep(L3)
            own = hT[:, :].rearrange("p (t d) -> p t d", d=D)
            dve.wait_ge(s_bias, 1)
            for j in range(NC):
                dve.wait_ge(mm["O3"], j + 1)
                for n, t in enumerate(TILES[j]):
                    last = dve.scalar_tensor_tensor(own[:, t, :], bank(j)[:, 128 * n:128 * n + 128],
                                                    dv[:, D09, t:t + 1], own[:, t, :], ALU.mult, ALU.add)
                link(last)
                dve.scalar_tensor_tensor(tiles_of(h, j), tiles_of(own, j), 0.0, tiles_of(x, j), ALU.max, ALU.add)\
                    .then_inc(s_fin, 1)

        @block.tensor
        def _(pe):
            pe.wait_ge(s_con, 15)
            for n, (array, j, ready, value) in enumerate(((dst_r, 1, s_prep, 2), (src_f, 0, s_prep, 3),
                                                          (w_l, 2, s_src, 96))):
                pe.wait_ge(ready, value)
                for c in range(4):
                    last = pe.transpose(ps[:, 512 * j + NQ * c:512 * j + NQ * (c + 1)],
                                        array[:, 128 * c:128 * c + 128], ident[0:NQ, 0:NQ])
                last.then_inc(s_prepT, 1)
            pe.wait_ge(s_prep, 6)
            for c in range(4):
                last = pe.matmul(bank(3, NCB), onesb[0:NQ, :], later[0:NQ, c, :], start=c == 0, stop=c == 3)
            last.then_inc(s_c0, 1)

            def transposes(stage, source, ready, chunks=range(NC)):
                for j in chunks:
                    ready(j)
                    for n, t in enumerate(TILES[j]):
                        last = pe.transpose(ps[:, 512 * j + 128 * n:512 * j + 128 * n + 128], source[:, t, :],
                                            ident[:, :])
                    last.then_inc(mm[stage], 1)

            def h0_ready(j):
                pe.wait_ge(s_rows[0], j + 1)
                if j == 0:
                    pe.wait_ge(s_prepE, 3)
                    pe.wait_ge(s_slot, 1)
            transposes("T0", h, h0_ready)

            pe.wait_ge(s_wt, 16 * 19)
            pe.wait_ge(ev["T0"], NC)
            for m, tiles in enumerate(HALVES):
                if m >= 8:
                    pe.wait_ge(ev["PQ"], m - 7)
                for n, t in enumerate(tiles):
                    b = 512 * (m % 8) + 256 * n
                    last = pe.matmul(ps[:, b:b + 256], hT[:, 128 * t:128 * t + 128],
                                     wab[:, :, :].rearrange("p w d -> p (w d)"), start=True, stop=True)
                last.then_inc(mm["PQ"], 1)

            pe.wait_ge(s_pass, 1)
            P = pe.value_load(passes_i[0:1, 0:1], min_val=1, max_val=MAXP)

            def zero_acc():
                for b in range(ACC_BANKS):
                    last = pe.matmul(bank(b), zerob[:, 0:128], zerob[:, :], start=True, stop=True)
                last.then_inc(s_zero, 1)

            def add_to(col, width, lhsT, rhs):
                return pe.matmul(ps[:, bass.ds(col, width)], lhsT, rhs, start=False, stop=True,
                                 skip_group_check=True)

            def window(i, k):
                return pe.value_load(tab_i[0:1, bass.ds(i * ITER + k, 1)], min_val=0, max_val=NB - 1)

            def sum_chunk(b, rows, k, c):
                for half in range(2):
                    for a in range(PARTS):
                        last = add_to(b * WB + WB * half, WB, rows(a), oh[:, k, c, WB * half:WB * half + WB])
                return last

            pe.wait_ge(ev["PQ"], NH)
            for s in range(4):
                pe.sem_inc(s_seg[s], ITER)
            pe.sem_inc(s_cmm, 2)
            pe.sem_inc(s_cev, 1)
            pe.sem_inc(s_pre, ITER)
            pe.sem_inc(s_R, ITER)
            pe.sem_inc(s_rre, 2)
            for n, array in enumerate((key_f, lo_f)):
                for half in range(2):
                    w = NCB * CT // 2
                    for c in range(4):
                        last = pe.matmul(bank(2 * n + half, w), array[:, 128 * c:128 * c + 128],
                                         sel[0:NQ, c, w * half:w * half + w], start=c == 0, stop=c == 3)
            last.then_inc(s_K4, 1)
            pe.wait_ge(s_key, 1)
            zero_acc()
            pe.wait_ge(s_qw, 32)
            pe.wait_ge(s_wc18, 16 * 2 * PARTS)

            registers = [pe.alloc_register(f"window_{k}") for k in range(ITER)]
            with pe.Fori(0, P) as w:

                def load_window(i, k):
                    pe.reg_load(registers[k % ITER], tab_i[0:1, bass.ds(i * ITER + k, 1)])

                def window_of(k):
                    return pe.snap(registers[k % ITER], min_val=0, max_val=NB - 1)

                def pre(i, k):
                    base = window_of(k)
                    n, step, slot = (w * NI + i) * ITER + k, w * NI + i + k // ITER, k % ITER
                    pe.wait_ge(s_sT, n + 1)
                    pe.wait_ge(s_rl[slot], (step + 1) * 32)
                    pe.wait_ge(s_gat[L0][slot], (step + 1) * 64)
                    pe.wait_ge(s_cev, n * 2 - 1 if k else n * 2 + 1)
                    pe.wait_ge(s_R, n + ITER)
                    for c in range(4):
                        to = ps[:, PRE + 128 * c:PRE + 128 * c + 128]
                        edges = slice(128 * c, 128 * c + 128)
                        pe.matmul(to, ea18[:, slot, edges], wc18[:, :], start=True, stop=False)
                        for a in range(PARTS):
                            pe.matmul(to, identb[:, :], G[:, slot, c, D * a:D * a + D], start=False, stop=False)
                        for a in range(PARTS):
                            last = pe.matmul(to, sT[:, slot, edges],
                                             Qw[:, bass.ds(base, 1), D * a:D * a + D]
                                             .rearrange("p a d -> p (a d)"),
                                             start=False, stop=a == PARTS - 1)
                    last.then_inc(s_pre, 1)

                def seg(i, k, chunks):
                    base = window_of(k)
                    n = (w * NI + i) * ITER + k
                    if chunks[0] == 0:
                        pe.wait_ge(s_oh[L0], n + 1)
                        pe.wait_ge(s_rlo, n + 1)
                    for c in chunks:
                        add_to(base * 4 + DEG, 4, oh[:, k, c, :],
                               wq[:, bass.ds(i * ITER + k, 1), c, :].rearrange("p a f -> p (a f)"))
                        last = sum_chunk(base, lambda a: RP[:, k % 2, a, c, :], k, c)
                    if chunks[-1] == 3:
                        last.then_inc(s_seg[L0], 1)

                def count(i, k, r, ahead):
                    n = (w * NI + i) * ITER + k
                    pe.wait_ge(s_cop, n * 2 + r + 1)
                    pe.wait_ge(s_R, n + ahead + 1 + ITER)
                    pe.wait_ge(s_cev, n * 2 + r + 1)
                    for j in range(CT):
                        last = pe.matmul(bank(7, CW), sta[:, r, j, :], mov[:, r, j, :],
                                         start=j == 0, stop=j == CT - 1)
                    last.then_inc(s_cmm, 1)

                def step(i, peeled):
                    for k in range(ITER):
                        ahead = 0 if peeled and k == ITER - 1 else 1
                        if ahead:
                            pre(i, k + 1)
                        seg(i, k, (0, 1))
                        count(i, k, 0, ahead)
                        if not peeled or k + 2 < ITER:
                            load_window(i, k + 2)
                        seg(i, k, (2,))
                        count(i, k, 1, ahead)
                        seg(i, k, (3,))

                pe.wait_ge(s_tab[L0], w * 4 + 5)
                pe.sem_inc(s_seen, 1)
                load_window(0, 0)
                load_window(0, 1)
                pre(0, 0)
                with pe.Fori(0, NI - 1) as i:
                    step(i, False)
                step(NI - 1, True)

            pe.wait_ge(ev["DG"], 1)
            pe.wait_ge(s_cev, P * (2 * NQ) + 1)
            for f in range(2):
                to = ps[:, PRE + NT * f:PRE + NT * f + NT]
                pe.matmul(to, shift[:, WB:WB + 128], deg2[:, f, 1:2 * NT:2], start=True, stop=False)
                pe.matmul(to, shift[:, 128:256], deg2[:, f, 0:2 * NT - 1:2], start=False, stop=False)
                last = pe.matmul(to, shift[:, 0:128], deg2[:, f, 2:2 * NT + 1:2], start=False, stop=True)
            last.then_inc(mm["DG"], 1)
            pe.wait_ge(ev["DG"], 2)
            pe.matmul(ps[0:1, PRE + 128:PRE + 130], ones[:, :], whole[:, :], start=True, stop=True)\
                .then_inc(mm["DG"], 1)
            pe.wait_ge(ev["DG"], 3)
            for stage, slots_of in (("B", range(PARTS)), ("R", [PARTS])):
                for j, tiles in enumerate(TILES):
                    if stage == "B":
                        pe.wait_ge(s_acc, j + 1)
                    else:
                        pe.wait_ge(ev["B"], j + 1)
                    for n, t in enumerate(tiles):
                        for a in slots_of:
                            last = pe.matmul(ps[:, 512 * j + 128 * n:512 * j + 128 * n + 128],
                                             dvb[:, a, t:t + 1].to_broadcast([128, 128]), identb[:, :],
                                             start=a == slots_of[0], stop=a == slots_of[-1])
                    last.then_inc(mm[stage], 1)
            for j, tiles in enumerate(TILES):
                pe.wait_ge(ev["R"], j + 1)
                c = 128 * len(tiles)
                pe.matmul(bank(j, c), w_m2[:, :], ST[:, 512 * j:512 * j + c], start=True, stop=True)\
                    .then_inc(mm["A"], 1)
            for j, tiles in enumerate(TILES):
                pe.wait_ge(ev["A"], j + 1)
                c = 128 * len(tiles)
                pe.matmul(bank(j, c), w_u1[:, 0, :], hT[:, 512 * j:512 * j + c], start=True, stop=False)
                pe.matmul(bank(j, c), w_u1[:, 1, :], aggT[:, 512 * j:512 * j + c], start=False, stop=True)\
                    .then_inc(mm["U"], 1)

            def by_node(stage, ready, *products, chunks=range(NC)):
                for j in chunks:
                    ready(j)
                    for n, t in enumerate(TILES[j]):
                        for k, (lhsT, weights) in enumerate(products):
                            last = pe.matmul(ps[:, 512 * j + 128 * n:512 * j + 128 * n + 128],
                                             lhsT[:, 128 * t:128 * t + 128], weights[:, :],
                                             start=k == 0, stop=k == len(products) - 1)
                    last.then_inc(mm[stage], 1)

            by_node("V", lambda j: pe.wait_ge(ev["U"], j + 1), (ST, w_u2))
            def h1_ready(j):
                pe.wait_ge(s_rows[2], j + 1)
            transposes("T1", h, h1_ready)

            def plain_sweep(s):
                zero_acc()
                with pe.Fori(0, P) as w:
                    with pe.Fori(0, NI) as i:
                        pe.wait_ge(s_tab[s], w * 4 + 5)
                        steps = w * NI + i
                        for k in range(ITER):
                            b = window(i, k)
                            pe.wait_ge(s_oh[s], steps * ITER + k + 1)
                            pe.wait_ge(s_gat[s][k], (steps + 1) * 64)
                            for c in range(4):
                                last = sum_chunk(b, lambda a: G[:, k, c, D * a:D * a + D], k, c)
                            last.then_inc(s_seg[s], 1)

            def dense(s, j, name=None):
                c = j + NC * (s // 2)
                n = 4 * len(TILES[j]) * 2
                pe.wait_ge(s_cld[c % 2], 16 * (c // 2 + 1))
                block_counts = counts[:, c % 2, 0:n * CW].rearrange("p (b h w) -> p h b w", h=NT, w=CB)
                for t in range(NT):
                    if j == 0 and t % 4 == 0:
                        pe.wait_ge(s_lo, SPLIT0[name] + t // 4 + 1)
                    for a in range(PARTS):
                        last = pe.matmul(bank(dense_bank(j), n * CB), Hp[:, t, a, :], block_counts[:, t, :, :],
                                         start=a == 0 and t == 0, stop=a == PARTS - 1 and t == NT - 1)
                last.then_inc(s_den[s], 1)

            def acc_ready(s):
                return lambda j: pe.wait_ge(s_acc, s * NC + j + 1)

            pe.wait_ge(s_flag, 1)
            flag = pe.value_load(flag_i[0:1, 0:1], min_val=0, max_val=1)
            with pe.If(flag > 0):
                dense(L1, 0, "H1")
                pe.wait_ge(ev["T1"], NC)
                for j in range(1, NC):
                    dense(L1, j)
                    by_node("O1", acc_ready(L1), (hT, w_11), (ST, w_12), chunks=[j - 1])
                by_node("O1", acc_ready(L1), (hT, w_11), (ST, w_12), chunks=[NC - 1])
            with pe.Else():
                pe.wait_ge(ev["T1"], NC)
                plain_sweep(L1)
                by_node("O1", acc_ready(L1), (hT, w_11), (ST, w_12))

            def g2_ready(j):
                pe.wait_ge(s_rows[3], j + 1)
                pe.wait_ge(ev["O1"], j + 1)
            transposes("T2", h, g2_ready)
            pe.wait_ge(ev["T2"], NC)

            zero_acc()
            with pe.Fori(0, P) as w:
                with pe.Fori(0, NI) as i:
                    pe.wait_ge(s_tab[L2], w * 4 + 5)
                    steps = w * NI + i
                    split0 = split_count(L2, w, i, P)
                    for k in range(ITER):
                        b = window(i, k)
                        pe.wait_ge(s_oh[L2], steps * ITER + k + 1)
                        pe.wait_ge(s_rlo, split0 + k + 1)
                        for c in range(4):
                            last = sum_chunk(b, lambda a: RP[:, k % 2, a, c, :], k, c)
                        last.then_inc(s_seg[L2], 1)
            by_node("O2", acc_ready(L2), (ST, w_3), (hT, w_3))
            sums = ST[:, :].rearrange("p (t d) -> p t d", d=D)
            with pe.If(flag > 0):
                dense(L3, 0, "G3")
                pe.wait_ge(ev["O2"], NC)
                for j in range(1, NC):
                    dense(L3, j)
                    transposes("O3", sums, acc_ready(L3), chunks=[j - 1])
                transposes("O3", sums, acc_ready(L3), chunks=[NC - 1])
            with pe.Else():
                pe.wait_ge(ev["O2"], NC)
                plain_sweep(L3)
                transposes("O3", sums, acc_ready(L3))


_INS = ['x', 'src', 'dst', 'edge_attr_2', 'edge_weight', 'L0_gnn_mW1', 'L0_gnn_mb1', 'L0_gnn_mW2', 'L0_gnn_mb2',
        'L0_gnn_uW1', 'L0_gnn_ub1', 'L0_gnn_uW2', 'L0_gnn_ub2', 'L0_gnn_gamma', 'L0_gnn_beta', 'L1_gnn_W1',
        'L1_gnn_b1', 'L1_gnn_W2', 'L1_gnn_b2', 'L2_gnn_W', 'L2_gnn_bias']
_OUT = (3125, 128)


def kernel(**inputs):
    import numpy as _np
    import concourse.bacc as _bacc
    from concourse import mybir as _mybir
    from concourse.bass_utils import run_bass_kernel_spmd as _run

    nc = _bacc.Bacc("TRN2", target_bir_lowering=False, num_devices=1)
    arrays, args = {}, []
    for name in _INS:
        a = _np.ascontiguousarray(inputs[name])
        arrays[f"in_{name}"] = a
        args.append(nc.dram_tensor(f"in_{name}", a.shape, _mybir.dt.from_np(a.dtype), kind="ExternalInput").ap())
    args.append(nc.dram_tensor("out_0", _OUT, _mybir.dt.float32, kind="ExternalOutput").ap())
    gnn_kernel(nc, *args)
    r = _run(nc, [arrays], core_ids=[0])
    return r.results[0]["out_0"]
```
